# Optimizing a Trainium2 kernel written in Bass

```python
import numpy as np
import jax
import jax.numpy as jnp

def _softmax(x, axis=-1):
    return jax.nn.softmax(x, axis=axis)
def _gelu(x):
    return jax.nn.gelu(x, approximate=True)
def _silu(x):
    return jax.nn.silu(x)
def _sigmoid(x):
    return jax.nn.sigmoid(x)
def _layernorm(x, axis=-1, eps=1e-5):
    m = jnp.mean(x, axis=axis, keepdims=True)
    v = jnp.var(x, axis=axis, keepdims=True)
    return (x - m) / jnp.sqrt(v + eps)
def _scatter_add(tgt, idx, src, axis=0):
    return tgt.at[idx].add(src)
def _segment_sum(src, seg, n):
    return jax.ops.segment_sum(src, seg, n)

kernel_name = 'mk_conv_preact_d4_conv_nhwc64_cfb0a7'

def setup_inputs(seed: int = 0):
    np.random.seed(seed)
    _w = jnp.asarray
    def _rec_inputs():
        import jax
        import jax.numpy as jnp
        _gk = jax.random.key(seed)
        x = -7.109e-05 + 0.9999 * jax.random.normal(jax.random.fold_in(_gk, 1), (8, 256, 256, 64), jnp.float32)
        return x
    x = _rec_inputs()
    def _L0_conv_setup():
        import jax, jax.numpy as jnp
        import numpy as np

        def _complex_matmul_2d(a, w):
            wr, wi = (w[..., 0], w[..., 1])
            ar, ai = (jnp.real(a), jnp.imag(a))
            out_r = jnp.einsum('bixy,ioxy->boxy', ar, wr) - jnp.einsum('bixy,ioxy->boxy', ai, wi)
            out_i = jnp.einsum('bixy,ioxy->boxy', ai, wr) + jnp.einsum('bixy,ioxy->boxy', ar, wi)
            return out_r + 1j * out_i
        key = jax.random.key(seed)
        ks = jax.random.split(key, 5)
        B, M, N, C, NM = (16, 256, 256, 64, 32)
        x = jax.random.normal(ks[0], (B, M, N, C), dtype=jnp.float32)
        fw_scale = 1.0 / (C * C) ** 0.5 * 0.5
        fw1 = jax.random.normal(ks[1], (C, C, NM, NM, 2), dtype=jnp.float32) * fw_scale
        fw2 = jax.random.normal(ks[2], (C, C, NM, NM, 2), dtype=jnp.float32) * fw_scale
        W = jax.random.normal(ks[3], (C, C), dtype=jnp.float32) * (1.0 / C ** 0.5)
        b = jnp.zeros((C,), dtype=jnp.float32)
        return {'x': x, 'fw1': fw1, 'fw2': fw2, 'W': W, 'b': b}
    _L0_conv_all = _L0_conv_setup()
    _L0_conv_in = {k: v for k, v in _L0_conv_all.items() if k in ('fw1', 'fw2', 'W', 'b', )}
    del _L0_conv_all

    def _L1_conv_setup():
        import jax, jax.numpy as jnp
        import numpy as np
        WIN = 8
        HEADS = 4

        def _local_mixer(x1, w_qkv, b_qkv, pos_emb):
            b, h, w, half = x1.shape
            hb, wb = (h // WIN, w // WIN)
            hc = half // HEADS
            xw = x1.reshape(b, hb, WIN, wb, WIN, half).transpose(0, 1, 3, 2, 4, 5)
            xw = xw.reshape(b * hb * wb, WIN * WIN, half)
            qkv = jnp.einsum('bnc,dc->bnd', xw, w_qkv) + b_qkv
            q, k, v = jnp.split(qkv, 3, axis=-1)

            def heads(t):
                B, n, _ = t.shape
                return t.reshape(B, n, HEADS, hc).transpose(0, 2, 1, 3)
            q, k, v = (heads(q), heads(k), heads(v))
            q = q * hc ** (-0.5)
            sim = jnp.einsum('bhic,bhjc->bhij', q, k) + pos_emb
            attn = jax.nn.softmax(sim, axis=-1)
            out = jnp.einsum('bhij,bhjc->bhic', attn, v)
            out = out.transpose(0, 2, 1, 3).reshape(b * hb * wb, WIN * WIN, half)
            out = out.reshape(b, hb, wb, WIN, WIN, half).transpose(0, 1, 3, 2, 4, 5)
            return out.reshape(b, h, w, half)

        def _global_mixer(x2, amp_w, amp_b, pha_w, pha_b):
            b, h, w, half = x2.shape
            xc = x2.transpose(0, 3, 1, 2)
            fre = jnp.fft.rfft2(xc, axes=(-2, -1), norm='backward')
            amp = jnp.abs(fre)
            pha = jnp.angle(fre)
            cw = lambda p: p[None, :, None, None]
            amp_fea = amp * cw(amp_w) + cw(amp_b)
            pha_fea = pha * cw(pha_w) + cw(pha_b)
            real = amp_fea * jnp.cos(pha_fea) + 1e-08
            imag = amp_fea * jnp.sin(pha_fea) + 1e-08
            out = jax.lax.complex(real, imag) + 1e-08
            out = jnp.abs(jnp.fft.irfft2(out, s=(h, w), axes=(-2, -1), norm='backward'))
            return out.transpose(0, 2, 3, 1)
        key = jax.random.key(seed)
        ks = jax.random.split(key, 10)
        b, h, w, c = (8, 256, 256, 64)
        half = c // 2
        seq = WIN * WIN
        return {'x': jax.random.normal(ks[0], (b, h, w, c), jnp.float32), 'w_qkv': jax.random.normal(ks[1], (3 * half, half), jnp.float32) * 0.05, 'b_qkv': jax.random.normal(ks[2], (3 * half,), jnp.float32) * 0.02, 'pos_emb': jax.random.truncated_normal(ks[3], -2.0, 2.0, (1, HEADS, seq, seq), jnp.float32), 'amp_w': jax.random.normal(ks[4], (half,), jnp.float32) * 0.05 + 1.0, 'amp_b': jax.random.normal(ks[5], (half,), jnp.float32) * 0.02, 'pha_w': jax.random.normal(ks[6], (half,), jnp.float32) * 0.05 + 1.0, 'pha_b': jax.random.normal(ks[7], (half,), jnp.float32) * 0.02, 'proj_w': jax.random.normal(ks[8], (c, c), jnp.float32) * 0.05, 'proj_b': jax.random.normal(ks[9], (c,), jnp.float32) * 0.02}
    _L1_conv_all = _L1_conv_setup()
    _L1_conv_in = {k: v for k, v in _L1_conv_all.items() if k in ('w_qkv', 'b_qkv', 'pos_emb', 'amp_w', 'amp_b', 'pha_w', 'pha_b', 'proj_w', 'proj_b', )}
    del _L1_conv_all

    def _L2_conv_setup():
        import jax, jax.numpy as jnp
        import numpy as np
        B, H, W, C = (4, 128, 128, 64)
        MODES, SCHMIDT = (16, 4)
        key = jax.random.key(seed)
        k1, k2, k3 = jax.random.split(key, 3)
        w_scale = float(np.sqrt(2.0 / (MODES * MODES * C + MODES * MODES * C)))
        return {'x': jax.random.normal(k1, (B, H, W, C), dtype=jnp.float32), 'weights_real': jax.random.normal(k2, (MODES, MODES, C, C, SCHMIDT), dtype=jnp.float32) * w_scale, 'weights_imag': jax.random.normal(k3, (MODES, MODES, C, C, SCHMIDT), dtype=jnp.float32) * w_scale, 'modes': MODES, 'schmidt_rank': SCHMIDT}
    _L2_conv_all = _L2_conv_setup()
    _L2_conv_in = {k: v for k, v in _L2_conv_all.items() if k in ('weights_real', 'weights_imag', )}
    del _L2_conv_all

    def _L3_conv_setup():
        import jax, jax.numpy as jnp
        import numpy as np
        B, C, H, W = (8, 512, 64, 64)
        HOLE = 32
        EPS = 1e-08

        def _mask_and_indices():
            m = np.zeros((H, W), np.float32)
            r0, c0 = ((H - HOLE) // 2, (W - HOLE) // 2)
            m[r0:r0 + HOLE, c0:c0 + HOLE] = 1.0
            flat = m.reshape(-1)
            mask_idx = np.nonzero(flat > 0.5)[0].astype(np.int32)
            nonmask_idx = np.nonzero(flat <= 0.5)[0].astype(np.int32)
            return (m, nonmask_idx, mask_idx)

        def _csa(x, nonmask_point_idx, mask_point_idx):
            b, c, h, w = x.shape
            feats = x.reshape(b, c, h * w)
            ctx = feats[:, :, nonmask_point_idx]
            msk = feats[:, :, mask_point_idx]
            ctx_n = ctx / (jnp.linalg.norm(ctx, axis=1, keepdims=True) + EPS)
            msk_n = msk / (jnp.linalg.norm(msk, axis=1, keepdims=True) + EPS)
            cos = jnp.einsum('bcm,bcn->bmn', msk_n, ctx_n)
            maxc = cos.max(axis=-1)
            amax = cos.argmax(axis=-1)
            best = jnp.take_along_axis(ctx.transpose(0, 2, 1), amax[..., None], axis=1)
            xs = (msk_n.transpose(2, 0, 1), best.transpose(1, 0, 2), maxc.T)

            def step(prev, inp):
                mn, bst, mx = inp
                prev_n = prev / (jnp.linalg.norm(prev, axis=-1, keepdims=True) + EPS)
                d_ad = jnp.maximum(jnp.sum(mn * prev_n, axis=-1), 0.0)
                cur = (d_ad[:, None] * prev + mx[:, None] * bst) / (d_ad + mx + EPS)[:, None]
                return (cur, cur)
            _, gen = jax.lax.scan(step, jnp.zeros((b, c), x.dtype), xs)
            out = feats.at[:, :, mask_point_idx].set(gen.transpose(1, 2, 0))
            return out.reshape(b, c, h, w)
        key = jax.random.key(seed)
        x = jax.random.normal(key, (B, C, H, W), dtype=jnp.float32)
        m, nm, mi = _mask_and_indices()
        return {'input': x, 'mask': jnp.asarray(m), 'nonmask_point_idx': jnp.asarray(nm), 'mask_point_idx': jnp.asarray(mi)}
    _L3_conv_all = _L3_conv_setup()
    _L3_conv_in = {k: v for k, v in _L3_conv_all.items() if k in ('mask', 'nonmask_point_idx', 'mask_point_idx', )}
    del _L3_conv_all

    return {
        "x": x,
        "L0_conv_fw1": _L0_conv_in["fw1"],
        "L0_conv_fw2": _L0_conv_in["fw2"],
        "L0_conv_W": _L0_conv_in["W"],
        "L0_conv_b": _L0_conv_in["b"],
        "L1_conv_w_qkv": _L1_conv_in["w_qkv"],
        "L1_conv_b_qkv": _L1_conv_in["b_qkv"],
        "L1_conv_pos_emb": _L1_conv_in["pos_emb"],
        "L1_conv_amp_w": _L1_conv_in["amp_w"],
        "L1_conv_amp_b": _L1_conv_in["amp_b"],
        "L1_conv_pha_w": _L1_conv_in["pha_w"],
        "L1_conv_pha_b": _L1_conv_in["pha_b"],
        "L1_conv_proj_w": _L1_conv_in["proj_w"],
        "L1_conv_proj_b": _L1_conv_in["proj_b"],
        "L2_conv_weights_real": _L2_conv_in["weights_real"],
        "L2_conv_weights_imag": _L2_conv_in["weights_imag"],
        "L3_conv_mask": _L3_conv_in["mask"],
        "L3_conv_nonmask_point_idx": _L3_conv_in["nonmask_point_idx"],
        "L3_conv_mask_point_idx": _L3_conv_in["mask_point_idx"],
    }

def reference(x, L0_conv_fw1, L0_conv_fw2, L0_conv_W, L0_conv_b, L1_conv_w_qkv, L1_conv_b_qkv, L1_conv_pos_emb, L1_conv_amp_w, L1_conv_amp_b, L1_conv_pha_w, L1_conv_pha_b, L1_conv_proj_w, L1_conv_proj_b, L2_conv_weights_real, L2_conv_weights_imag, L3_conv_mask, L3_conv_nonmask_point_idx, L3_conv_mask_point_idx):
    import jax
    import jax.numpy as jnp
    def _L0_conv_ref(x, fw1, fw2, W, b):
        import jax, jax.numpy as jnp
        import numpy as np

        def _complex_matmul_2d(a, w):
            wr, wi = (w[..., 0], w[..., 1])
            ar, ai = (jnp.real(a), jnp.imag(a))
            out_r = jnp.einsum('bixy,ioxy->boxy', ar, wr) - jnp.einsum('bixy,ioxy->boxy', ai, wi)
            out_i = jnp.einsum('bixy,ioxy->boxy', ai, wr) + jnp.einsum('bixy,ioxy->boxy', ar, wi)
            return out_r + 1j * out_i
        B, M, N, C = x.shape
        nm = fw1.shape[2]
        O = fw1.shape[1]
        xt = jnp.transpose(x, (0, 3, 1, 2))
        scale_fwd = jnp.sqrt(jnp.asarray(M * N, dtype=jnp.float32))
        x_ft = jnp.fft.rfft2(xt, s=(M, N)) / scale_fwd
        a = x_ft[:, :, :nm, :nm]
        blk1 = _complex_matmul_2d(a, fw1)
        blk2 = _complex_matmul_2d(a, fw2)
        out_ft = jnp.zeros((B, O, N, M // 2 + 1), dtype=x_ft.dtype)
        out_ft = out_ft.at[:, :, :nm, :nm].set(blk1)
        out_ft = out_ft.at[:, :, N - nm:, :nm].set(blk2)
        out = jnp.fft.irfft2(out_ft, s=(N, M))
        scale_bwd = jnp.sqrt(jnp.asarray(N * (M // 2 + 1), dtype=jnp.float32))
        out = out / scale_bwd
        out = jnp.transpose(out, (0, 2, 3, 1))
        res = out @ W + b
        return jax.nn.relu(res + out)

    def _L1_conv_ref(x, w_qkv, b_qkv, pos_emb, amp_w, amp_b, pha_w, pha_b, proj_w, proj_b):
        import jax, jax.numpy as jnp
        import numpy as np
        WIN = 8
        HEADS = 4

        def _local_mixer(x1, w_qkv, b_qkv, pos_emb):
            b, h, w, half = x1.shape
            hb, wb = (h // WIN, w // WIN)
            hc = half // HEADS
            xw = x1.reshape(b, hb, WIN, wb, WIN, half).transpose(0, 1, 3, 2, 4, 5)
            xw = xw.reshape(b * hb * wb, WIN * WIN, half)
            qkv = jnp.einsum('bnc,dc->bnd', xw, w_qkv) + b_qkv
            q, k, v = jnp.split(qkv, 3, axis=-1)

            def heads(t):
                B, n, _ = t.shape
                return t.reshape(B, n, HEADS, hc).transpose(0, 2, 1, 3)
            q, k, v = (heads(q), heads(k), heads(v))
            q = q * hc ** (-0.5)
            sim = jnp.einsum('bhic,bhjc->bhij', q, k) + pos_emb
            attn = jax.nn.softmax(sim, axis=-1)
            out = jnp.einsum('bhij,bhjc->bhic', attn, v)
            out = out.transpose(0, 2, 1, 3).reshape(b * hb * wb, WIN * WIN, half)
            out = out.reshape(b, hb, wb, WIN, WIN, half).transpose(0, 1, 3, 2, 4, 5)
            return out.reshape(b, h, w, half)

        def _global_mixer(x2, amp_w, amp_b, pha_w, pha_b):
            b, h, w, half = x2.shape
            xc = x2.transpose(0, 3, 1, 2)
            fre = jnp.fft.rfft2(xc, axes=(-2, -1), norm='backward')
            amp = jnp.abs(fre)
            pha = jnp.angle(fre)
            cw = lambda p: p[None, :, None, None]
            amp_fea = amp * cw(amp_w) + cw(amp_b)
            pha_fea = pha * cw(pha_w) + cw(pha_b)
            real = amp_fea * jnp.cos(pha_fea) + 1e-08
            imag = amp_fea * jnp.sin(pha_fea) + 1e-08
            out = jax.lax.complex(real, imag) + 1e-08
            out = jnp.abs(jnp.fft.irfft2(out, s=(h, w), axes=(-2, -1), norm='backward'))
            return out.transpose(0, 2, 3, 1)
        b, h, w, c = x.shape
        half = c // 2
        x1 = _local_mixer(x[..., :half], w_qkv, b_qkv, pos_emb)
        x2 = _global_mixer(x[..., half:], amp_w, amp_b, pha_w, pha_b)
        cat = jnp.concatenate([x1, x2], axis=-1)
        out = jnp.einsum('bhwc,dc->bhwd', cat, proj_w) + proj_b
        return out

    def _L2_conv_ref(x, weights_real, weights_imag, modes, schmidt_rank):
        import jax, jax.numpy as jnp
        import numpy as np
        B, H, W, C = (4, 128, 128, 64)
        MODES, SCHMIDT = (16, 4)
        b, h, w, c = x.shape
        x_ft = jnp.fft.fftn(x, axes=(1, 2))[:, :modes, :modes, :]
        weights = weights_real + 1j * weights_imag
        out_ft = jnp.einsum('bknc,mncos->bkmos', x_ft, weights)
        out_modes = out_ft.sum(axis=-1) / float(np.sqrt(schmidt_rank))
        o = out_modes.shape[-1]
        full = jnp.zeros((b, h, w, o), dtype=out_modes.dtype)
        full = full.at[:, :modes, :modes, :].set(out_modes)
        out = jnp.fft.ifftn(full, axes=(1, 2))
        return out.real

    def _L3_conv_ref(input, mask, nonmask_point_idx, mask_point_idx):
        import jax, jax.numpy as jnp
        import numpy as np
        B, C, H, W = (8, 512, 64, 64)
        HOLE = 32
        EPS = 1e-08

        def _mask_and_indices():
            m = np.zeros((H, W), np.float32)
            r0, c0 = ((H - HOLE) // 2, (W - HOLE) // 2)
            m[r0:r0 + HOLE, c0:c0 + HOLE] = 1.0
            flat = m.reshape(-1)
            mask_idx = np.nonzero(flat > 0.5)[0].astype(np.int32)
            nonmask_idx = np.nonzero(flat <= 0.5)[0].astype(np.int32)
            return (m, nonmask_idx, mask_idx)

        def _csa(x, nonmask_point_idx, mask_point_idx):
            b, c, h, w = x.shape
            feats = x.reshape(b, c, h * w)
            ctx = feats[:, :, nonmask_point_idx]
            msk = feats[:, :, mask_point_idx]
            ctx_n = ctx / (jnp.linalg.norm(ctx, axis=1, keepdims=True) + EPS)
            msk_n = msk / (jnp.linalg.norm(msk, axis=1, keepdims=True) + EPS)
            cos = jnp.einsum('bcm,bcn->bmn', msk_n, ctx_n)
            maxc = cos.max(axis=-1)
            amax = cos.argmax(axis=-1)
            best = jnp.take_along_axis(ctx.transpose(0, 2, 1), amax[..., None], axis=1)
            xs = (msk_n.transpose(2, 0, 1), best.transpose(1, 0, 2), maxc.T)

            def step(prev, inp):
                mn, bst, mx = inp
                prev_n = prev / (jnp.linalg.norm(prev, axis=-1, keepdims=True) + EPS)
                d_ad = jnp.maximum(jnp.sum(mn * prev_n, axis=-1), 0.0)
                cur = (d_ad[:, None] * prev + mx[:, None] * bst) / (d_ad + mx + EPS)[:, None]
                return (cur, cur)
            _, gen = jax.lax.scan(step, jnp.zeros((b, c), x.dtype), xs)
            out = feats.at[:, :, mask_point_idx].set(gen.transpose(1, 2, 0))
            return out.reshape(b, c, h, w)
        return _csa(input, nonmask_point_idx, mask_point_idx)

    def _gn(v, G=32, eps=1e-5):
        B_, H_, W_, C_ = v.shape
        g = v.reshape(B_, H_, W_, G, C_ // G)
        m = jnp.mean(g, axis=(1, 2, 4), keepdims=True)
        s = jnp.var(g, axis=(1, 2, 4), keepdims=True)
        return ((g - m) / jnp.sqrt(s + eps)).reshape(v.shape)

    def _ln_c(v, eps=1e-6):
        m = jnp.mean(v, axis=-1, keepdims=True)
        s = jnp.var(v, axis=-1, keepdims=True)
        return (v - m) / jnp.sqrt(s + eps)

    def _ln_t(v, eps=1e-5):
        m = jnp.mean(v, axis=-1, keepdims=True)
        s = jnp.var(v, axis=-1, keepdims=True)
        return (v - m) / jnp.sqrt(s + eps)

    def _to_tokens(v):
        B_, H_, W_, C_ = v.shape
        return v.reshape(B_, H_ * W_, C_)
    def _from_tokens(t, like):
        return t.reshape(like.shape)

    x = x + _L0_conv_ref(_gn(x), L0_conv_fw1, L0_conv_fw2, L0_conv_W, L0_conv_b)
    x = x + _L1_conv_ref(_gn(x), L1_conv_w_qkv, L1_conv_b_qkv, L1_conv_pos_emb, L1_conv_amp_w, L1_conv_amp_b, L1_conv_pha_w, L1_conv_pha_b, L1_conv_proj_w, L1_conv_proj_b)
    x = x + _L2_conv_ref(_gn(x), L2_conv_weights_real, L2_conv_weights_imag, 16, 4)
    x = x + _L3_conv_ref(_gn(x), L3_conv_mask, L3_conv_nonmask_point_idx, L3_conv_mask_point_idx)
    return x


_drawn_inputs = setup_inputs


def setup_inputs(seed=0):
    import zlib

    import numpy as np

    out = dict(_drawn_inputs(seed))
    spreads = {'L0_conv_b': (0.0, 0.1)}
    factors = {'L0_conv_fw1': 200.0,
     'L0_conv_fw2': 200.0,
     'L0_conv_W': 200.0,
     'L1_conv_b_qkv': 3.038,
     'L1_conv_amp_b': 200.0,
     'L1_conv_pha_b': 3.36}
    for name, (base, spread) in spreads.items():
        noise = np.random.default_rng([zlib.crc32(name.encode()), seed]).standard_normal(out[name].shape)
        drawn = base * np.exp(spread * noise) if base else spread * noise
        out[name] = jnp.asarray(drawn.astype(out[name].dtype))
    for name, factor in factors.items():
        out[name] = (out[name] * factor).astype(out[name].dtype)
    return out
```

```python
from contextlib import ExitStack

import numpy as np

import concourse.bass as bass
from concourse import mybir

F32 = mybir.dt.float32
I32 = mybir.dt.int32
U32 = mybir.dt.uint32
ALU = mybir.AluOpType
ACT = mybir.ActivationFunctionType
AX = mybir.AxisListType

P = 128
H = W = 256
C = 64
HALF = C // 2
PIX = H * W
GROUP_N = 2 * PIX
EPS = 1e-5
NM0, NM2 = 32, 16
WIN, HEADS, HC = 8, 4, 8
NWIN = W // WIN
NF = W // 2 + 1
NPTS = 64 * 64
NMASK, NCTX = 1024, 3072
CSA_EPS = 1e-8


class Chain:

    def __init__(self, eng, sem, base=0):
        self.eng, self.sem, self.base, self.n = eng, sem, base, 0

    def step(self, ins):
        self.n += 1
        ins.then_inc(self.sem, 1)
        self.eng.wait_ge(self.sem, self.base + self.n)


class Mem:

    def __init__(self, nc, ctx, tag):
        self.nc, self.ctx, self.tag, self.sems = nc, ctx, tag, []
        ctx.callback(self.clear)

    def sb(self, name, shape, dt=F32):
        return self.ctx.enter_context(self.nc.sbuf_tensor(f"{self.tag}_{name}", shape, dt))

    def ps(self, name, shape, dt=F32):
        return self.ctx.enter_context(self.nc.psum_tensor(f"{self.tag}_{name}", shape, dt))

    def sem(self, name):
        self.sems.append(self.nc.alloc_semaphore(f"{self.tag}_{name}"))
        return self.sems[-1]

    def clear(self):
        self.nc.clear_and_free_semaphores(self.sems)
        self.nc.all_engine_barrier()


def forward_modes(nc, tag, B, x, fa, fb, pair, modes, nm, out_scale, split_rows):
    n2 = 2 * nm
    per_bank = 512 // n2
    nbank = C // per_bank
    kbank = (nm + per_bank - 1) // per_bank
    nsq, sqw = 16, 2048
    with ExitStack() as ctx:
        m = Mem(nc, ctx, tag)
        xt = m.sb("xt", [P, 2, 2, P * C])
        y = m.sb("y", [P, 2, C, n2])
        sq = m.sb("sq", [P, 2, sqw])
        part = m.sb("part", [P, nsq, C])
        tot_c = m.sb("tot_c", [P, C])
        ao = m.sb("ao", [C, 3, nm * nm])
        fas, fbs = m.sb("fas", [P, 2, n2]), m.sb("fbs", [P, 2, n2])
        pairs = m.sb("pairs", [C, C])
        ones = m.sb("ones", [P, 1])
        vs, st = m.sb("vs", [C, 2]), m.sb("st", [C, 8])
        yp = m.ps("yp", [P, 2, 512])
        ap = m.ps("ap", [C, kbank, 512])
        sp_ = m.ps("sp", [C, 512])
        s_const, s_ones = m.sem("const"), m.sem("ones")
        s_x = [m.sem(f"x{j}") for j in range(2)]
        s_xfree = [m.sem(f"xfree{j}") for j in range(2)]
        s_y, s_yfree = m.sem("y"), m.sem("yfree")
        s_yread = m.sem("yread")
        s_sq, s_sqfree = m.sem("sq"), m.sem("sqfree")
        s_red, s_tot, s_vs, s_grp = m.sem("red"), m.sem("tot"), m.sem("vs"), m.sem("grp")
        s_a, s_var, s_std, s_ao = m.sem("a"), m.sem("var"), m.sem("std"), m.sem("ao")
        s_store, s_aofree, s_pe = m.sem("store"), m.sem("aofree"), m.sem("pe")
        s_ch, s_ach = m.sem("ch"), m.sem("ach")
        with nc.Block() as block:

            @block.sync
            def _(sp):
                for dst, src in ((fas, fa), (fbs, fb)):
                    sp.dma_start(dst[:, :, :], src.rearrange("(a p) n -> p a n", p=P)).then_inc(s_const, 16)
                sp.dma_start(pairs[:, :], pair).then_inc(s_const, 16)
                with sp.Fori(0, B) as b:
                    for wh in range(2):
                        sp.wait_ge(s_xfree[wh], b + 1)
                        src = x[bass.ds(b, 1), :, wh * P:(wh + 1) * P, :]
                        sp.dma_start(xt[:, wh, :, :],
                                     src.rearrange("a (q p) w c -> p (a q) (w c)", p=P)).then_inc(s_x[wh], 16)

            @block.tensor
            def _(pe):
                pe.wait_ge(s_const, 48)
                pe.wait_ge(s_ones, 1)
                with pe.Fori(0, B) as b:
                    for wh in range(2):
                        pe.wait_ge(s_x[wh], b * 16 + 16)
                        xv = xt[:, wh, :, :].rearrange("p q (w c) -> p q w c", c=C)
                        for g in range(nbank):
                            n = wh * nbank + g
                            pe.wait_ge(s_yfree, b * (2 * nbank) + n + 1)
                            for j in range(per_bank):
                                c = g * per_bank + j
                                for hh in range(2):
                                    last = nc.tensor.matmul(yp[:, n % 2, j * n2:(j + 1) * n2], xv[:, hh, :, c],
                                                            fas[:, hh, :], start=(hh == 0), stop=(hh == 1))
                            last.then_inc(s_y, 1)
                    pe.wait_ge(s_yfree, b * (2 * nbank) + 2 * nbank + 2)
                    pe.wait_ge(s_ao, b + 1)
                    for k in range(nm):
                        for n in range(4):
                            wh, p = n // 2, n % 2
                            o = (k % per_bank) * n2
                            last = nc.tensor.matmul(ap[:, k // per_bank, o:o + n2], y[:, wh, :, p * nm + k],
                                                    (fas, fbs)[p][:, wh, :], start=(n == 0), stop=(n == 3))
                    last.then_inc(s_a, 1)
                    pe.wait_ge(s_red, b + 1)
                    nc.tensor.matmul(sp_[:, 0:1], tot_c[:, :], ones[:, :], start=True, stop=True).then_inc(s_tot, 1)
                    pe.wait_ge(s_vs, b * 2 + 1)
                    pe.sem_inc(s_pe, 1)
                    nc.tensor.matmul(sp_[:, 4:6], pairs[:, :], vs[:, :], start=True, stop=True).then_inc(s_grp, 1)

            @block.scalar
            def _(act):
                act.sem_inc(s_yfree, 2)
                act.sem_inc(s_xfree[0], 1)
                act.sem_inc(s_xfree[1], 1)
                with act.Fori(0, B) as b:
                    for wh in range(2):
                        act.wait_ge(s_x[wh], b * 16 + 16)
                        xf = xt[:, wh, :, :].rearrange("p q (s n) -> p (q s) n", n=sqw)
                        for s in range(nsq // 2):
                            n = wh * (nsq // 2) + s
                            act.wait_ge(s_sqfree, b * nsq + n + 1)
                            last = nc.scalar.activation(sq[:, n % 2, :], xf[:, s, :], ACT.Square)
                            last.then_inc(s_sq, 1)
                            for g in range(s * nbank // (nsq // 2), (s + 1) * nbank // (nsq // 2)):
                                k = wh * nbank + g
                                act.wait_ge(s_y, b * (2 * nbank) + k + 1)
                                if k == 0:
                                    act.wait_ge(s_a, b + 1)
                                nc.scalar.activation(y[:, wh, g * per_bank:(g + 1) * per_bank, :],
                                                     yp[:, k % 2, :].rearrange("p (c n) -> p c n", n=n2),
                                                     ACT.Copy).then_inc(s_yfree, 1)
                        act.wait_ge(s_sq, b * nsq + (wh + 1) * (nsq // 2))
                        act.sem_inc(s_xfree[wh], 1)
                    act.wait_ge(s_var, b + 1)
                    nc.scalar.activation(st[:, 4:5], st[:, 3:4], ACT.Sqrt).then_inc(s_std, 1)

            @block.vector
            def _(dve):
                dve.sem_inc(s_sqfree, 2)
                dve.sem_inc(s_a, 1)
                dve.sem_inc(s_ao, 1)
                nc.vector.memset(ones[:, :], 1.0).then_inc(s_ones, 1)
                with dve.Fori(0, B) as b:
                    ch = Chain(dve, s_ch, b * 8)
                    for n in range(nsq):
                        dve.wait_ge(s_sq, b * nsq + n + 1)
                        nc.vector.reduce_sum(part[:, n, :], sq[:, n % 2, :].rearrange("p (w c) -> p c w", c=C),
                                             axis=AX.X).then_inc(s_sqfree, 1)
                    dve.wait_ge(s_sqfree, b * nsq + nsq + 2)
                    nc.vector.reduce_sum(tot_c[:, :], part[:, :, :].rearrange("p n c -> p c n"),
                                         axis=AX.X).then_inc(s_red, 1)
                    dve.wait_ge(s_tot, b + 1)
                    dve.wait_ge(s_a, b + 2)
                    nc.vector.tensor_copy(vs[:, 0:1], ap[:, 0, 0:1])
                    nc.vector.tensor_copy(vs[:, 1:2], sp_[:, 0:1]).then_inc(s_vs, 1)
                    dve.wait_ge(s_grp, b + 1)
                    ch.step(nc.vector.tensor_scalar(st[:, 0:2], sp_[:, 4:6], 1.0 / GROUP_N, None, ALU.mult))
                    ch.step(nc.vector.tensor_tensor(st[:, 2:3], st[:, 0:1], st[:, 0:1], ALU.mult))
                    ch.step(nc.vector.tensor_tensor(st[:, 2:3], st[:, 1:2], st[:, 2:3], ALU.subtract))
                    nc.vector.tensor_scalar(st[:, 3:4], st[:, 2:3], 0.0, EPS, ALU.max, ALU.add).then_inc(s_var, 1)
                    dve.wait_ge(s_std, b + 1)
                    ch.step(nc.vector.reciprocal(st[:, 5:6], st[:, 4:5]))
                    ch.step(nc.vector.tensor_scalar(st[:, 6:7], st[:, 5:6], out_scale, None, ALU.mult))
                    ch.step(nc.vector.tensor_scalar(st[:, 7:8], st[:, 5:6], -out_scale, None, ALU.mult))
                    ch.step(nc.vector.tensor_scalar(st[:, 0:1], st[:, 0:1], float(-PIX), None, ALU.mult))
                    nc.vector.tensor_tensor(vs[:, 0:1], ap[:, 0, 0:1], st[:, 0:1], ALU.add).then_inc(s_ch, 1)
                    dve.wait_ge(s_ch, b * 8 + 8)
                    dve.wait_ge(s_aofree, b + 1)
                    av = ap[:, :, :].rearrange("p a n -> p (a n)")[:, 0:nm * n2].rearrange("p (k q r) -> p k q r", q=2, r=nm)
                    for q, src, s in ((0, 1, 7), (1, 0, 6), (2, 1, 6)):
                        if split_rows:
                            for d in range(2):
                                dst = ao[:, q, d * nm * nm // 2:(d + 1) * nm * nm // 2]
                                last = nc.vector.tensor_scalar(
                                    dst.rearrange("p (r k) -> p k r", k=nm), av[:, :, src, d::2],
                                    st[:, s:s + 1], None, ALU.mult)
                        else:
                            last = nc.vector.tensor_scalar(ao[:, q, :].rearrange("p (k r) -> p k r", r=nm), av[:, :, src, :],
                                                           st[:, s:s + 1], None, ALU.mult)
                    last.then_inc(s_ao, 1)
                    dve.wait_ge(s_ao, b + 2)
                    nc.vector.tensor_tensor(ao[:, 1, 0:1], vs[:, 0:1], st[:, 6:7], ALU.mult).then_inc(s_vs, 1)

            @block.gpsimd
            def _(pool):
                pool.sem_inc(s_aofree, 1)
                with pool.Fori(0, B) as b:
                    pool.wait_ge(s_vs, b * 2 + 2)
                    pool.dma_start(modes[bass.ds(b, 1)].rearrange("a q p n -> p (a q) n"), ao[:, :, :]).then_inc(s_store, 16)
                    pool.wait_ge(s_store, b * 16 + 16)
                    pool.sem_inc(s_aofree, 1)


def mix_modes0(nc, B, modes, fw1, fw2, wmat, eye, zd):
    NK = 2
    with ExitStack() as ctx:
        m = Mem(nc, ctx, "mx")
        a = m.sb("a", [P, B, 3, NM0, NM0])
        fw = m.sb("fw", [P, 2, C, NK * NM0 * 2])
        z = m.sb("z", [P, B, 3, NM0])
        zo = m.sb("zo", [P, 2, B, 2, C])
        wi, eyes = m.sb("wi", [P, C]), m.sb("eyes", [P, C])
        mp = [m.ps(f"mp{f}", [P, 512]) for f in range(2)]
        qp = [m.ps(f"qp{f}", [P, B * 2 * C]) for f in range(2)]
        s_const = m.sem("const")
        s_fw = [m.sem(f"fw{j}") for j in range(2)]
        s_fwfree = m.sem("fwfree")
        s_wi, s_m, s_z, s_q, s_zo = m.sem("wi"), m.sem("m"), m.sem("z"), m.sem("q"), m.sem("zo")
        s_store = [m.sem(f"store{j}") for j in range(2)]
        nt = NM0 // NK
        with nc.Block() as block:

            def load_fw(sp, t, j):
                for f, src in enumerate((fw1, fw2)):
                    v = src.rearrange("i o (t x) y r -> i t o (x y r)", x=NK)
                    sp.dma_start(fw[f * C:(f + 1) * C, j, :, :],
                                 v[:, bass.ds(t, 1), :, :].rearrange("i a o n -> i (a o) n")).then_inc(s_fw[j], 16)

            @block.sync
            def _(sp):
                for f in range(2):
                    half = slice(f * C, (f + 1) * C)
                    sp.dma_start(wi[half, :], wmat).then_inc(s_const, 16)
                    sp.dma_start(eyes[half, :], eye).then_inc(s_const, 16)
                    for b in range(B):
                        sp.dma_start(a[half, b, :, :, :].rearrange("p q x y -> p q (x y)"),
                                     modes[b].rearrange("q i n -> i q n")).then_inc(s_const, 16)
                with sp.Fori(0, nt // 2) as t:
                    for j in range(2):
                        sp.wait_ge(s_fwfree, t * 2 + j + 1)
                        load_fw(sp, t * 2 + j, j)

            @block.tensor
            def _(pe):
                pe.sem_inc(s_fwfree, 2)
                pe.wait_ge(s_wi, 1)
                for t in range(nt):
                    j = t % 2
                    pe.wait_ge(s_fw[j], 32 * (t // 2 + 1))
                    fv = fw[:, j, :, :].rearrange("p o (x y r) -> p o x y r", y=NM0, r=2)
                    for x in range(NK):
                        n, kx = t * NK + x, t * NK + x
                        if n:
                            pe.wait_ge(s_z, n)
                        for ky in range(NM0):
                            for r in range(2):
                                for f in range(2):
                                    half = slice(f * C, (f + 1) * C)
                                    rhs = a[half, :, 1 - r:3 - r, kx, ky].rearrange("p b q -> p q b")
                                    last = nc.tensor.matmul(mp[f][half, ky * 2 * B:(ky + 1) * 2 * B],
                                                            fv[half, :, x, ky, r], rhs, start=(r == 0), stop=(r == 1))
                        last.then_inc(s_m, 1)
                        pe.wait_ge(s_z, n + 1)
                        if n:
                            pe.wait_ge(s_zo, n)
                        for b in range(B):
                            for p in range(2):
                                for f in range(2):
                                    half = slice(f * C, (f + 1) * C)
                                    o = (b * 2 + p) * C
                                    last = nc.tensor.matmul(qp[f][half, o:o + C],
                                                            z[half, b, 1 - p:3 - p, :].rearrange("p q y -> p (q y)"),
                                                            wi[half, :], start=True, stop=True)
                        last.then_inc(s_q, 1)
                    pe.sem_inc(s_fwfree, 1)

            @block.vector
            def _(dve):
                dve.wait_ge(s_const, 16 * (4 + 2 * B))
                nc.vector.tensor_tensor(wi[:, :], wi[:, :], eyes[:, :], ALU.add).then_inc(s_wi, 1)
                for n in range(NM0):
                    dve.wait_ge(s_m, n + 1)
                    for f in range(2):
                        half = slice(f * C, (f + 1) * C)
                        src = mp[f][half, 0:NM0 * 2 * B].rearrange("p (y q b) -> p q b y", q=2, b=B)
                        for q, p, sign in ((0, 1, 1.0), (1, 0, 1.0), (2, 1, -1.0)):
                            if n:
                                dve.wait_ge(s_q, n)
                            last = nc.vector.tensor_scalar(z[half, :, q, :], src[:, p], sign, None, ALU.mult)
                    last.then_inc(s_z, 1)

            @block.scalar
            def _(act):
                for n in range(NM0):
                    if n >= 2:
                        act.wait_ge(s_store[n % 2], 32 * (n // 2))
                    act.wait_ge(s_q, n + 1)
                    for f in range(2):
                        half = slice(f * C, (f + 1) * C)
                        last = nc.scalar.activation(zo[half, n % 2, :, :, :].rearrange("p b q o -> p (b q o)"),
                                                    qp[f][half, :], ACT.Copy)
                    last.then_inc(s_zo, 1)
                    act.wait_ge(s_zo, n + 1)
                    for f in range(2):
                        half = slice(f * C, (f + 1) * C)
                        act.dma_start(zd[:, :, f * NM0 + n, :, :].rearrange("b p q o -> p b (q o)"),
                                      zo[half, n % 2, :, :, :].rearrange("p b q o -> p b (q o)")).then_inc(s_store[n % 2], 16)
                for j in range(2):
                    act.wait_ge(s_store[j], 16 * NM0)


def inverse_modes(nc, tag, B, zd, ky_mat, kx_mat, res, out_nat, out_l, out_g, stats, bias, bias_scale):
    kr, nk2 = zd.shape[1], zd.shape[2]
    mc = nk2 * 2
    WC = 32
    NP = W // WC
    NW = WC // WIN
    CH = WC * C
    NB = CH // 512
    NV = C // 2
    NFQ = NP * 2 * NB
    HELD = 3 * NB
    split = out_nat is None
    stores = 4 if split else 1
    with ExitStack() as ctx:
        m = Mem(nc, ctx, tag)
        zx = m.sb("zx", [kr, nk2, 2, C])
        v = m.sb("v", [mc, W, C])
        km, kxm = m.sb("km", [kr, W]), m.sb("kxm", [mc, H])
        xr = m.sb("xr", [P, 2, 2, CH])
        xo = m.sb("xo", [P, 2, 2 * CH])
        sq = m.sb("sq", [P, 2 * CH])
        part = m.sb("part", [P, 2, C, NP])
        tot = m.sb("tot", [P, 2, C])
        ones = m.sb("ones", [P, P])
        stp = m.sb("stp", [P, 6, C // 2])
        so = m.sb("so", [P, 2, C // 2, 2])
        brow = m.sb("brow", [1, C])
        vp = [m.ps(f"vp{j}", [mc, 2, W]) for j in range(2)]
        fp = [m.ps(f"fp{j}", [P, 512]) for j in range(4)]
        tp = m.ps("tp", [P, 2 * C])
        s_const, s_ones = m.sem("const"), m.sem("ones")
        s_z, s_zb = m.sem("z"), m.sem("zb")
        s_vp, s_vused = m.sem("vp"), m.sem("vused")
        s_x = [m.sem(f"x{j}") for j in range(2)]
        s_f, s_fused = m.sem("f"), m.sem("fused")
        s_sq, s_sqfree = m.sem("sq"), m.sem("sqfree")
        s_store = [m.sem(f"store{j}") for j in range(2)]
        s_tot, s_tp, s_var, s_std = m.sem("tot"), m.sem("tp"), m.sem("var"), m.sem("std")
        s_st, s_sst, s_ch, s_pe = m.sem("st"), m.sem("sst"), m.sem("ch"), m.sem("pe")

        def local(t, j):
            return t[:, j, 0:CH].rearrange("p (r u n c) -> p r u n c", r=2, u=WIN, c=HALF)

        def glob(t, j):
            return t[:, j, CH:2 * CH].rearrange("p (r u n c) -> p r u n c", r=2, u=WIN, c=HALF)

        def channel_views(flat):
            if not split:
                return [(slice(0, C), flat.rearrange("p (n c) -> p c n", c=C))]
            return [(slice(h * HALF, (h + 1) * HALF),
                     flat[:, h * CH:(h + 1) * CH].rearrange("p (n c) -> p c n", c=HALF)) for h in range(2)]

        with nc.Block() as block:

            @block.sync
            def _(sp):
                sp.dma_start(km[:, :], ky_mat).then_inc(s_const, 16)
                sp.dma_start(kxm[:, :], kx_mat).then_inc(s_const, 16)
                if bias is not None:
                    sp.dma_start(brow[:, :], bias.rearrange("(a c) -> a c", a=1)).then_inc(s_const, 16)
                with sp.Fori(0, B) as b:
                    sp.wait_ge(s_vp, b * NV + 1)
                    sp.dma_start(zx[:, :, :, :].rearrange("p k q o -> p (k q o)"),
                                 zd[bass.ds(b, 1)].rearrange("a p k q o -> (a p) (k q o)")).then_inc(s_z, 16)
                    for wc in range(NP):
                        sp.wait_ge(s_fused, b * NFQ + wc * 2 * NB + HELD - 2 * NB)
                        sp.dma_start(xr[:, wc % 2, :, :],
                                     res[bass.ds(b, 1), :, wc * WC:(wc + 1) * WC, :]
                                     .rearrange("a (r p) w c -> p (a r) (w c)", p=P)).then_inc(s_x[wc % 2], 16)

            @block.tensor
            def _(pe):
                pe.sem_inc(s_vp, 1)
                pe.wait_ge(s_const, 48 if bias is not None else 32)
                pe.wait_ge(s_ones, 1)
                with pe.Fori(0, B) as b:
                    if bias is not None:
                        pe.wait_ge(s_zb, b + 1)
                    else:
                        pe.wait_ge(s_z, b * 16 + 16)
                    zv = zx[:, :, :, :].rearrange("p k q o -> p (k q) o")
                    for n in range(NV):
                        pe.wait_ge(s_vused, b * NV + n + 1)
                        pe.sem_inc(s_pe, 1)
                        for k in range(2):
                            last = nc.tensor.matmul(vp[n % 2][:, k, :], zv[:, :, 2 * n + k], km[:, :],
                                                    start=True, stop=True)
                        last.then_inc(s_vp, 1)
                    pe.wait_ge(s_vused, b * NV + NV + 2)
                    for wc in range(NP):
                        for r in range(2):
                            for i in range(NB):
                                n = (wc * 2 + r) * NB + i
                                pe.wait_ge(s_fused, b * NFQ + n + HELD - 3)
                                pe.sem_inc(s_pe, 1)
                                w0 = wc * WC + i * WIN
                                nc.tensor.matmul(fp[n % 4][:, :], kxm[:, r * P:(r + 1) * P],
                                                 v[:, w0:w0 + WIN, :].rearrange("p w c -> p (w c)"),
                                                 start=True, stop=True).then_inc(s_f, 1)
                    pe.wait_ge(s_tot, b + 1)
                    nc.tensor.matmul(tp[:, :], ones[:, :], tot[:, :, :].rearrange("p a c -> p (a c)"),
                                     start=True, stop=True).then_inc(s_tp, 1)

            @block.vector
            def _(dve):
                dve.sem_inc(s_fused, HELD)
                dve.sem_inc(s_sqfree, 1)
                nc.vector.memset(ones[:, :], 1.0).then_inc(s_ones, 1)
                if bias is not None:
                    dve.wait_ge(s_const, 48)
                    nc.vector.tensor_scalar(brow[:, :], brow[:, :], bias_scale, None, ALU.mult).then_inc(s_ones, 1)
                    dve.wait_ge(s_ones, 2)
                with dve.Fori(0, B) as b:
                    ch = Chain(dve, s_ch, b * 5)
                    if bias is not None:
                        dve.wait_ge(s_z, b * 16 + 16)
                        nc.vector.tensor_tensor(zx[0:1, 0, 0, :], zx[0:1, 0, 0, :], brow[:, :], ALU.add).then_inc(s_zb, 1)

                    def square_sums(wc):
                        dve.wait_ge(s_sq, b * NP + wc + 1)
                        for cs, vv in channel_views(sq[:, :]):
                            last = nc.vector.reduce_sum(part[:, 1, cs, wc], vv, axis=AX.X)
                        last.then_inc(s_sqfree, 1)

                    for wc in range(NP):
                        j = wc % 2
                        dve.wait_ge(s_x[j], b * (8 * NP) + 16 * (wc // 2) + 16)
                        dve.wait_ge(s_store[j], (b * (NP // 2) + wc // 2 + 1) * (16 * stores))
                        for r in range(2):
                            for i in range(NB):
                                n = (wc * 2 + r) * NB + i
                                dve.wait_ge(s_f, b * NFQ + n + 1)
                                f = fp[n % 4][:, :].rearrange("p (w c) -> p w c", c=C)
                                x = xr[:, j, r, i * 512:(i + 1) * 512].rearrange("p (w c) -> p w c", c=C)
                                if split:
                                    nc.vector.scalar_tensor_tensor(local(xo, j)[:, r, :, i, :], f[:, :, 0:HALF], 0.0,
                                                                   x[:, :, 0:HALF], ALU.max, ALU.add)
                                    last = nc.vector.scalar_tensor_tensor(
                                        glob(xo, j)[:, r, :, i, :], f[:, :, HALF:C], 0.0,
                                        x[:, :, HALF:C], ALU.max, ALU.add)
                                else:
                                    o = r * CH + i * 512
                                    last = nc.vector.tensor_tensor(xo[:, j, o:o + 512], fp[n % 4][:, :],
                                                                   xr[:, j, r, i * 512:(i + 1) * 512], ALU.add)
                                last.then_inc(s_fused, 1)
                        dve.wait_ge(s_fused, b * NFQ + (wc + 1) * 2 * NB + HELD)
                        for cs, vv in channel_views(xo[:, j, :]):
                            nc.vector.reduce_sum(part[:, 0, cs, wc], vv, axis=AX.X)
                        if wc:
                            square_sums(wc - 1)
                    square_sums(NP - 1)
                    dve.wait_ge(s_sqfree, b * NP + NP + 1)
                    nc.vector.reduce_sum(tot[:, :, :], part[:, :, :, :], axis=AX.X).then_inc(s_tot, 1)
                    dve.wait_ge(s_tp, b + 1)
                    mean, msq, var = stp[:, 0, :], stp[:, 1, :], stp[:, 2, :]
                    ch.step(nc.vector.reduce_sum(stp[:, 0:2, :], tp[:, :].rearrange("p (a g t) -> p a g t", a=2, t=2), axis=AX.X))
                    ch.step(nc.vector.tensor_scalar(stp[:, 0:2, :], stp[:, 0:2, :], 1.0 / GROUP_N, None, ALU.mult))
                    ch.step(nc.vector.tensor_tensor(var, mean, mean, ALU.mult))
                    ch.step(nc.vector.tensor_tensor(var, msq, var, ALU.subtract))
                    nc.vector.tensor_scalar(stp[:, 3, :], var, 0.0, EPS, ALU.max, ALU.add).then_inc(s_var, 1)
                    dve.wait_ge(s_std, b + 1)
                    ch.step(nc.vector.reciprocal(stp[:, 5, :], stp[:, 4, :]))
                    dve.wait_ge(s_sst, b * 16 + 16)
                    for t in range(2):
                        nc.vector.tensor_copy(so[:, 0, :, t], mean)
                        last = nc.vector.tensor_copy(so[:, 1, :, t], stp[:, 5, :])
                    last.then_inc(s_st, 1)

            @block.scalar
            def _(act):
                act.sem_inc(s_vused, 2)
                act.sem_inc(s_sst, 16)
                for j in range(2):
                    act.sem_inc(s_store[j], 16 * stores)
                with act.Fori(0, B) as b:
                    for n in range(NV):
                        act.wait_ge(s_vp, b * NV + n + 2)
                        nc.scalar.activation(v[:, :, 2 * n:2 * n + 2].rearrange("p w k -> p k w"), vp[n % 2][:, :, :],
                                             ACT.Copy).then_inc(s_vused, 1)
                    for wc in range(NP):
                        j = wc % 2
                        act.wait_ge(s_fused, b * NFQ + (wc + 1) * 2 * NB + HELD)
                        rows = slice(wc * WC, (wc + 1) * WC)
                        if split:
                            for half, out in ((local(xo, j), out_l), (glob(xo, j), out_g)):
                                for r in range(2):
                                    act.dma_start(out[bass.ds(b, 1), r * P:(r + 1) * P, :, wc * NW:(wc + 1) * NW, :]
                                                  .rearrange("a p u n c -> (a p) u (n c)"),
                                                  half[:, r].rearrange("p u n c -> p u (n c)")).then_inc(s_store[j], 16)
                        else:
                            act.dma_start(out_nat[bass.ds(b, 1), :, rows, :].rearrange("a (r p) w c -> p (a r) (w c)", p=P),
                                          xo[:, j, :].rearrange("p (r n) -> p r n", r=2)).then_inc(s_store[j], 16)
                        act.wait_ge(s_sqfree, b * NP + wc + 1)
                        nc.scalar.activation(sq[:, :], xo[:, j, :], ACT.Square).then_inc(s_sq, 1)
                    act.wait_ge(s_var, b + 1)
                    nc.scalar.activation(stp[:, 4, :], stp[:, 3, :], ACT.Sqrt).then_inc(s_std, 1)
                    act.wait_ge(s_st, b + 1)
                    act.dma_start(stats[bass.ds(b, 1)].rearrange("a q c -> a (q c)"),
                                  so[0:1, :, :, :].rearrange("p q g t -> p (q g t)")).then_inc(s_sst, 16)
                for j in range(2):
                    act.wait_ge(s_store[j], (B * (NP // 2) + 1) * (16 * stores))
                act.wait_ge(s_sst, B * 16 + 16)


def at_least(eng, sem, value):
    if not isinstance(value, int) or value > 0:
        eng.wait_ge(sem, value)


def local_attention(nc, B, x1l, stats, wqkv_t, b_qkv, pos, masks, eye, ol):
    NBLK = B * (H // (2 * WIN))
    NG, NU = 8, 16
    N2 = WIN * WIN
    LAG_M, LAG_E, LAG_T, LAG_V, LAG_N = 1, 2, 5, 6, 8
    RS, RT = 8, 2
    VC = HC + 1
    AT = {1: 0, 2: 1, 4: 2, 5: 3, 7: 4, 8: 5, 12: 6, 13: 7}
    ACT_AT = {2: (0, 0), 3: (1, 0), 4: (2, 0), 5: (2, 1), 6: (3, 0), 7: (3, 1), 8: (4, 0), 9: (4, 1), 10: (4, 2), 11: (4, 3)}
    DVE_AT = {8: (5, 0), 9: (5, 1), 10: (5, 2), 11: (5, 3), 12: (6, 0), 13: (6, 1), 14: (7, 0), 15: (7, 1)}
    T0, Q0, K0, V0 = 0, 2, 4, 6
    QS = HC ** -0.5
    with ExitStack() as ctx:
        m = Mem(nc, ctx, "la")
        x = m.sb("x", [P, 2, NG * P])
        tn = m.sb("tn", [P, NG, P])
        qx = m.sb("qx", [P, 2, NG * 2, 2, N2])
        kx = m.sb("kx", [P, 2, NG * 2, HEADS, N2])
        v2 = m.sb("v2", [P, 2, NG, 4, HEADS, 2, VC])
        s = m.sb("s", [P, RS, HEADS, 2, N2])
        et = m.sb("et", [P, RT, HEADS, P])
        mx = m.sb("mx", [P, RS, HEADS * 2])
        o = m.sb("o", [P, 2, 2, NU, HALF])
        rc = m.sb("rc", [P, 2, 2 * HEADS, 2])
        post = m.sb("post", [P, HEADS, 2, N2])
        idn = m.sb("idn", [P, P])
        wq, wk, wv = m.sb("wq", [P, P]), m.sb("wk", [P, P]), m.sb("wv", [P, P])
        bq, bk, bv = m.sb("bq", [P, 1]), m.sb("bk", [P, 1]), m.sb("bv", [P, 4, HALF])
        msk = m.sb("msk", [P, 6])
        sq_, bq_, bk_ = m.sb("sq_", [P, 2]), m.sb("bq_", [P, 2]), m.sb("bk_", [P, HEADS])
        mr = m.sb("mr", [P, B, 2])
        nb = m.sb("nb", [P, B])
        sc = m.sb("sc", [P, B, 16])
        sh = m.sb("sh", [P, B, 16])
        pa = [m.ps(f"pa{i}", [P, 512]) for i in range(2)]
        ps = [m.ps(f"ps{i}", [P, HEADS, 2, N2]) for i in range(2)]
        pt = [m.ps(f"pt{i}", [P, HEADS, P]) for i in range(2)]
        po = [m.ps(f"po{i}", [P, 2, HEADS, 2, 2, VC]) for i in range(2)]
        s_zero, s_const, s_prep, s_ready = m.sem("zero"), m.sem("const"), m.sem("prep"), m.sem("ready")
        s_x = [m.sem(f"x{j}") for j in range(2)]
        s_piece, s_apiece, s_dpiece = m.sem("piece"), m.sem("apiece"), m.sem("dpiece")
        s_s, s_add, s_max, s_sub, s_exp = m.sem("s"), m.sem("add"), m.sem("max"), m.sem("sub"), m.sem("exp")
        s_t, s_te, s_av, s_rc, s_norm = m.sem("t"), m.sem("te"), m.sem("av"), m.sem("rc"), m.sem("norm")
        s_act = m.sem("act")
        s_store = [m.sem(f"store{j}") for j in range(2)]
        xv = x1l.rearrange("b (j r) u n c -> (b j) (r u) (n c)", r=2 * WIN)
        ov = ol.rearrange("b (j d r) w (u t) c -> (b j) d (r w) u (t c)", d=2, r=WIN, u=2)

        def for_blocks(eng, body):
            body(0, 0, True, False)
            with eng.Fori(0, NBLK // 2 - 1) as t:
                body(t * 2 + 1, 1, False, False)
                body(t * 2 + 2, 0, False, False)
            body(NBLK - 1, 1, False, True)

        with nc.Block() as block:

            @block.sync
            def _(sp):
                for w in range(4):
                    rows = slice(w * HALF, (w + 1) * HALF)
                    for dst, i in ((bq, 0), (bk, 1)):
                        sp.dma_start(dst[rows, :], b_qkv[i * HALF:(i + 1) * HALF].rearrange("(c a) -> c a", a=1)).then_inc(s_const, 16)
                    for q in range(2):
                        sp.dma_start(mr[rows, :, q:q + 1], stats[:, q, 0:HALF].rearrange("b (c a) -> c b a", a=1),
                                     allow_slow_non_contiguous=True).then_inc(s_const, 16)
                sp.dma_start(msk[:, :], masks).then_inc(s_const, 16)
                sp.dma_start(idn[:, :], eye).then_inc(s_const, 16)
                bvv = b_qkv[2 * HALF:3 * HALF]
                sp.dma_start(bv[:, :, :], bass.AP(bvv.tensor, bvv.offset, [[0, P], [0, 4], [1, HALF]])).then_inc(s_const, 16)
                for u in range(2):
                    for d in range(2):
                        sp.dma_start(post[u * N2:(u + 1) * N2, :, d, :], pos[0].rearrange("h i j -> i h j")).then_inc(s_const, 16)
                sp.wait_ge(s_zero, 1)
                for w in range(4):
                    rows = slice(w * HALF, (w + 1) * HALF)
                    for i, dst in enumerate((wq, wk, wv)):
                        sp.dma_start(dst[rows, rows], wqkv_t[:, i * HALF:(i + 1) * HALF]).then_inc(s_const, 16)
                for j in range(2):
                    sp.dma_start(x[:, j, :], xv[j]).then_inc(s_x[j], 16)
                with sp.Fori(0, NBLK // 2 - 1) as t:
                    for j in range(2):
                        sp.wait_ge(s_piece, t * 16 + (j * 8 + 2))
                        sp.dma_start(x[:, j, :], xv[bass.ds(t * 2 + (2 + j), 1)].rearrange("a p n -> (a p) n")).then_inc(s_x[j], 16)

            @block.tensor
            def _(pe):
                pe.wait_ge(s_const, 16 * (4 * 4 + 3 + 4 + 12))

                def piece(p, n, j):
                    bank = pa[p % 2]
                    half = p % 2
                    if p < Q0:
                        if p == T0:
                            pe.wait_ge(s_x[j], (n // 2) * 16 + 16 if isinstance(n, int) else (n - j) * 8 + 16)
                        at_least(pe, s_dpiece, n * 3 - 1 + half)
                        for g in range(4):
                            gg = half * 4 + g
                            last = nc.tensor.transpose(bank[:, g * P:(g + 1) * P], x[:, j, gg * P:(gg + 1) * P], idn[:, :])
                    elif p < V0:
                        pe.wait_ge(s_apiece, n * 5 + (2 if p < K0 else p - 1))
                        last = nc.tensor.matmul(bank[:, :], (wq if p < K0 else wk)[:, :],
                                                tn[:, half * 4:half * 4 + 4, :].rearrange("p g n -> p (g n)"),
                                                start=True, stop=True)
                    else:
                        if half:
                            pe.wait_ge(s_dpiece, n * 3 + 1)
                        else:
                            pe.wait_ge(s_apiece, n * 5 + 5)
                        for g in range(4):
                            last = nc.tensor.matmul(bank[:, g * P:(g + 1) * P], tn[:, half * 4 + g, :], wv[:, :],
                                                    start=True, stop=True)
                    last.then_inc(s_piece, 1)

                def scores(n, k, j):
                    g, e = k // 2, k % 2
                    if k == 0:
                        pe.wait_ge(s_apiece, n * 5 + 5)
                        pe.wait_ge(s_dpiece, n * 3 + 1)
                    at_least(pe, s_add, n * NU + k - 1)
                    rows = slice(e * 64, e * 64 + 64)
                    for d in range(2):
                        last = nc.tensor.matmul(ps[k % 2][:, :, d, :],
                                                qx[rows, j, g * 2 + d, :, :].rearrange("p u i -> p (u i)"),
                                                kx[rows, j, g * 2 + d, :, :], start=True, stop=True)
                    last.then_inc(s_s, 1)

                def transposes(n, k):
                    at_least(pe, s_te, n * NU + k - 1)
                    pe.wait_ge(s_exp, n * NU + k + 1)
                    for h in range(HEADS):
                        last = nc.tensor.transpose(pt[k % 2][:, h, :], s[:, k % RS, h, :, :].rearrange("p d j -> p (d j)"), idn[:, :])
                    last.then_inc(s_t, 1)

                def values(n, k, j):
                    g, e = k // 2, k % 2
                    if k == 0:
                        pe.wait_ge(s_dpiece, n * 3 + 3)
                    pe.wait_ge(s_te, n * NU + k + 1)
                    if k % 2 == 0:
                        at_least(pe, s_norm, n * (NU // 2) + k // 2 - 1)
                    for h in range(HEADS):
                        last = nc.tensor.matmul(po[(k // 2) % 2][:, e, h, :, :, :].rearrange("p u d c -> p (u d c)"),
                                                et[:, k % RT, h, :],
                                                v2[:, j, g, 2 * e:2 * e + 2, h, :, :].rearrange("p w d c -> p w (d c)"),
                                                start=True, stop=True)
                    last.then_inc(s_av, 1)

                for p in range(8):
                    piece(p, 0, 0)

                def body(n, j, first, last):
                    for k in range(NU):
                        scores(n, k, j)
                        if k in AT and not last:
                            piece(AT[k], n + 1, 1 - j)
                        for lag, op in ((LAG_T, lambda n, k, j: transposes(n, k)), (LAG_V, values)):
                            if k >= lag:
                                op(n, k - lag, j)
                            elif not first:
                                op(n - 1, k - lag + NU, 1 - j)
                    if last:
                        for k in range(NU, NU + LAG_V):
                            if k < NU + LAG_T:
                                transposes(n, k - LAG_T)
                            values(n, k - LAG_V, j)

                for_blocks(pe, body)

            @block.vector
            def _(dve):
                for t in (wq, wk, wv):
                    last = nc.vector.memset(t[:, :], 0.0)
                last.then_inc(s_zero, 1)
                nc.vector.memset(v2[:, :, :, :, :, :, :].rearrange("p a g w h d c -> p (a g w h d c)"), 0.0).then_inc(s_prep, 1)
                dve.wait_ge(s_prep, 1)
                for d in range(2):
                    ones = v2[d * 64:(d + 1) * 64, :, :, :, :, d, HC:VC]
                    nc.vector.memset(ones.rearrange("p a g w h c -> p (a g w h) c"), 1.0).then_inc(s_prep, 1)
                dve.wait_ge(s_const, 16 * (4 * 4 + 3 + 4 + 12))
                nc.vector.tensor_scalar(sq_[:, :], msk[:, 0:2], QS, None, ALU.mult).then_inc(s_prep, 1)
                nc.vector.tensor_scalar(bk_[:, :], msk[:, 2:6], bk[:, 0:1], None, ALU.mult).then_inc(s_prep, 1)
                dve.wait_ge(s_prep, 5)
                nc.vector.tensor_scalar(bq_[:, :], sq_[:, :], bq[:, 0:1], None, ALU.mult).then_inc(s_prep, 1)
                nc.vector.scalar_tensor_tensor(nb[:, :], mr[:, :, 0], -1.0, mr[:, :, 1], ALU.mult, ALU.mult).then_inc(s_prep, 1)
                dve.wait_ge(s_prep, 7)
                for i in range(16):
                    nc.vector.tensor_copy(sc[:, :, i], mr[:, :, 1])
                    last = nc.vector.tensor_copy(sh[:, :, i], nb[:, :])
                last.then_inc(s_ready, 1)

                def add(n, k):
                    dve.wait_ge(s_s, n * NU + k + 1)
                    at_least(dve, s_t, n * NU + k - RS + 1)
                    nc.vector.tensor_tensor(s[:, k % RS], ps[k % 2][:, :, :, :], post[:, :, :, :], ALU.add).then_inc(s_add, 1)

                def maximum(n, k):
                    dve.wait_ge(s_add, n * NU + k + 1)
                    nc.vector.reduce_max(mx[:, k % RS, :], s[:, k % RS].rearrange("p h d j -> p (h d) j"), axis=AX.X).then_inc(s_max, 1)

                def divide(n, k, j):
                    i = (k // 2) % 2
                    dve.wait_ge(s_av, n * NU + k + 1)
                    if k == 1:
                        dve.wait_ge(s_store[j], (n - j) * 16 + 16)
                    for u in range(2):
                        rows = slice(u * 64, u * 64 + 64)
                        po_ = po[i][rows, :, :, u, :, :].rearrange("p e h d c -> p (e h) d c")
                        last = nc.vector.reciprocal(rc[rows, i, :, :], po_[:, :, :, HC])
                    last.then_inc(s_rc, 1)
                    dve.wait_ge(s_rc, n * (NU // 2) + k // 2 + 1)
                    for u in range(2):
                        rows = slice(u * 64, u * 64 + 64)
                        po_ = po[i][rows, :, :, u, :, :].rearrange("p e h d c -> p (e h) d c")
                        out = o[rows, j, :, k - 1:k + 1, :].rearrange("p d e (h c) -> p (e h) d c", h=HEADS)
                        r = rc[rows, i, :, :]
                        rb = bass.AP(r.tensor, r.offset, list(r.ap) + [[0, HC]])
                        last = nc.vector.tensor_tensor(out, po_[:, :, :, 0:HC], rb, ALU.mult)
                    last.then_inc(s_norm, 1)

                def piece(p, part, n, j):
                    if part == 0:
                        dve.wait_ge(s_piece, n * 8 + p + 1)
                    half, h, d = p % 2, part, part
                    if p < V0:
                        last = nc.vector.tensor_scalar(kx[:, j, half * 8:half * 8 + 8, h, :],
                                                       pa[p % 2][:, :].rearrange("p (a i) -> p a i", i=N2),
                                                       msk[:, 2 + h:3 + h], bk_[:, h:h + 1], ALU.mult, ALU.add)
                    else:
                        rows = slice(d * 64, d * 64 + 64)
                        for g in range(4):
                            last = nc.vector.tensor_tensor(
                                v2[rows, j, half * 4 + g, :, :, d, 0:HC],
                                pa[p % 2][rows, g * P:(g + 1) * P].rearrange("p (w h c) -> p w h c", w=4, h=HEADS),
                                bv[rows, :, :].rearrange("p w (h c) -> p w h c", h=HEADS), ALU.add)
                    if part == (HEADS if p < V0 else 2) - 1:
                        last.then_inc(s_dpiece, 1)

                for p, part in DVE_AT.values():
                    piece(p, part, 0, 0)

                def body(n, j, first, last):
                    for k in range(NU):
                        add(n, k)
                        if k >= LAG_M:
                            maximum(n, k - LAG_M)
                        elif not first:
                            maximum(n - 1, k - LAG_M + NU)
                        if k in DVE_AT and not last:
                            piece(*DVE_AT[k], n + 1, 1 - j)
                        q = k - LAG_N
                        if q % 2 and q >= 0:
                            divide(n, q, j)
                        elif q % 2 and not first:
                            divide(n - 1, q + NU, 1 - j)
                    if last:
                        for k in range(NU - LAG_M, NU):
                            maximum(n, k)
                        for q in range(NU - LAG_N, NU):
                            if q % 2:
                                divide(n, q, j)

                for_blocks(dve, body)

            @block.gpsimd
            def _(pool):
                def body(n, j, first, last):
                    for k in range(NU):
                        pool.wait_ge(s_max, n * NU + k + 1)
                        mk = mx[:, k % RS, :]
                        mb = bass.AP(mk.tensor, mk.offset, list(mk.ap) + [[0, N2]])
                        sv = s[:, k % RS].rearrange("p h d j -> p (h d) j")
                        nc.gpsimd.tensor_tensor(sv, sv, mb, ALU.subtract).then_inc(s_sub, 1)

                for_blocks(pool, body)

            @block.scalar
            def _(act):
                for j in range(2):
                    act.sem_inc(s_store[j], 16)
                act.wait_ge(s_ready, 1)

                def piece(p, part, n, j):
                    if part == 0:
                        act.wait_ge(s_piece, n * 8 + p + 1)
                    half, u, h = p % 2, part, part
                    if p < Q0:
                        act.sem_inc(s_act, 1)
                        scale = sc[:, :, :].rearrange("p b i -> p (b i)")[:, bass.ds(n, 1)]
                        shift = sh[:, :, :].rearrange("p b i -> p (b i)")[:, bass.ds(n, 1)]
                        last = nc.scalar.activation(tn[:, half * 4:half * 4 + 4, :].rearrange("p g n -> p (g n)"),
                                                    pa[p % 2][:, :], ACT.Identity, bias=shift, scale=scale)
                    elif p < K0:
                        last = nc.scalar.activation(qx[:, j, half * 8:half * 8 + 8, u, :],
                                                    pa[p % 2][:, :].rearrange("p (a i) -> p a i", i=N2),
                                                    ACT.Identity, bias=bq_[:, u:u + 1], scale=sq_[:, u:u + 1])
                    else:
                        last = nc.scalar.activation(kx[:, j, half * 8:half * 8 + 8, h, :],
                                                    pa[p % 2][:, :].rearrange("p (a i) -> p a i", i=N2),
                                                    ACT.Identity, bias=bk_[:, h:h + 1], scale=msk[:, 2 + h:3 + h])
                    if part == (1 if p < Q0 else 2 if p < K0 else HEADS) - 1:
                        last.then_inc(s_apiece, 1)

                def exponentials(n, k):
                    act.wait_ge(s_sub, n * NU + k + 1)
                    sk = s[:, k % RS].rearrange("p h d j -> p (h d j)")
                    nc.scalar.activation(sk, sk, ACT.Exp).then_inc(s_exp, 1)

                def copy_out(n, k, j):
                    act.wait_ge(s_t, n * NU + k + 1)
                    at_least(act, s_av, n * NU + k - 1)
                    nc.scalar.activation(et[:, k % RT].rearrange("p h n -> p (h n)"),
                                         pt[k % 2][:, :, :].rearrange("p h n -> p (h n)"), ACT.Copy).then_inc(s_te, 1)

                def store(n, j):
                    act.wait_ge(s_norm, n * (NU // 2) + NU // 2)
                    for u in range(2):
                        dst = ov[n, :, :, u, :] if isinstance(n, int) else ov[bass.ds(n, 1), :, :, u, :].rearrange("a d i n -> (a d) i n")
                        act.dma_start(dst.rearrange("d i n -> i d n"),
                                      o[u * 64:u * 64 + 64, j, :, :, :].rearrange("p d e c -> p d (e c)")).then_inc(s_store[j], 16)

                for p, part in ACT_AT.values():
                    piece(p, part, 0, 0)

                def body(n, j, first, last):
                    for k in range(NU):
                        if k >= LAG_E:
                            exponentials(n, k - LAG_E)
                        elif not first:
                            exponentials(n - 1, k - LAG_E + NU)
                        if k >= LAG_T:
                            copy_out(n, k - LAG_T, j)
                        elif not first:
                            copy_out(n - 1, k - LAG_T + NU, 1 - j)
                        if k in ACT_AT and not last:
                            piece(*ACT_AT[k], n + 1, 1 - j)
                        if k == LAG_N + 2 and not first:
                            store(n - 1, 1 - j)
                    if last:
                        for k in range(NU, NU + LAG_T):
                            if k < NU + LAG_E:
                                exponentials(n, k - LAG_E)
                            copy_out(n, k - LAG_T, j)
                        store(n, j)

                for_blocks(act, body)
                for j in range(2):
                    act.wait_ge(s_store[j], NBLK * 16 + 16)


def spread(ap, dims):
    return bass.AP(ap.tensor, ap.offset, [[0, P]] + dims)


def global_mixer(nc, B, x1g, stats, amp_w, amp_b, pha_w, pha_b, mats, og):
    fh, fw_, ec, ew = mats
    NG, GC = 8, 4
    SL = 2 * GC
    PI = float(np.pi)
    ROUND = 1.5 * 2.0 ** 23
    CLAMP = 3.1415925
    TINY = 1e-30
    NS = 17
    with ExitStack() as ctx:
        m = Mem(nc, ctx, "gm")
        x = m.sb("x", [P, 2, W, HALF])
        out = m.sb("out", [P, 2, W, HALF])
        y = m.sb("y", [P, 2, 2, 2 * NF])
        ri = m.sb("ri", [P, SL, 2, NF])
        t = [m.sb(f"t{i}", [P, SL, NF]) for i in range(5)]
        zr, zi = (m.sb(n, [P, 2, SL, NF]) for n in ("zr", "zi"))
        u = m.sb("u", [P, 2, 2, H])
        fhs = m.sb("fhs", [P, 2, 2 * NF])
        fws = m.sb("fws", [P, 3, 2, 2 * NF])
        ecs = m.sb("ecs", [P, 3, 2, H])
        ews = m.sb("ews", [P, 2, W])
        aw, ab, pw, pb_ = (m.sb(n, [P, HALF]) for n in ("aw", "ab", "pw", "pb"))
        mr = m.sb("mr", [P, B, 2, HALF])
        rc, dc = m.sb("rc", [P, HALF]), m.sb("dc", [1, HALF])
        one, hpi = m.sb("one", [P, 1]), m.sb("hpi", [P, 1])
        yp = [m.ps(f"yp{i}", [P, 2 * NF]) for i in range(2)]
        xp = [m.ps(f"xp{i}", [P, 2 * NF]) for i in range(2)]
        up = [m.ps(f"up{i}", [P, 2, H]) for i in range(2)]
        op = [m.ps(f"op{i}", [P, 2, W]) for i in range(2)]
        s_const, s_init, s_x = m.sem("const"), m.sem("init"), m.sem("x")
        s_y, s_ye, s_xp, s_xe = m.sem("y"), m.sem("ye"), m.sem("xp"), m.sem("xe")
        s_u, s_ue, s_o, s_oe = m.sem("u"), m.sem("ue"), m.sem("o"), m.sem("oe")
        s_rc, s_ch, s_ach = m.sem("rc"), m.sem("ch"), m.sem("ach")
        s_dc, s_abs, s_ratio, s_atan, s_phase, s_trig, s_ri, s_prod, s_z = (
            m.sem(n) for n in ("dc", "abs", "ratio", "atan", "phase", "trig", "ri", "prod", "z"))
        s_store, s_pool = m.sem("store"), m.sem("pool")
        with nc.Block() as block:

            @block.sync
            def _(sp):
                sp.dma_start(fhs[:, :, :], fh.rearrange("(a p) n -> p a n", p=P)).then_inc(s_const, 16)
                for i in range(3):
                    sp.dma_start(fws[:, i, :, :], fw_[i].rearrange("(a p) n -> p a n", p=P)).then_inc(s_const, 16)
                    sp.dma_start(ecs[:, i, :, :], ec[i].rearrange("a p n -> p a n")).then_inc(s_const, 16)
                sp.dma_start(ews[:, :, :], ew.rearrange("a p n -> p a n")).then_inc(s_const, 16)
                for dst, src in ((aw, amp_w), (ab, amp_b), (pw, pha_w), (pb_, pha_b)):
                    sp.dma_start(dst[:, :], spread(src, [[1, HALF]])).then_inc(s_const, 16)
                for b in range(B):
                    sp.dma_start(mr[:, b, :, :], spread(stats[b, :, HALF:C], [[C, 2], [1, HALF]])).then_inc(s_const, 16)
                with sp.Fori(0, B) as b:
                    sp.wait_ge(s_xp, b * 64 + 1)
                    sp.dma_start(x[:, :, :, :].rearrange("p r w c -> p r (w c)"),
                                 x1g[bass.ds(b, 1)].rearrange("a (r p) u n c -> p (a r) (u n c)", p=P)).then_inc(s_x, 16)

            @block.tensor
            def _(pe):
                pe.sem_inc(s_xp, 1)
                pe.wait_ge(s_const, 16 * (12 + B))
                with pe.Fori(0, B) as b:
                    pe.wait_ge(s_x, b * 16 + 16)

                    def rows(c):
                        for wh in range(2):
                            pe.wait_ge(s_ye, b * 64 + (2 * c + wh + 1))
                            for r in range(2):
                                last = nc.tensor.matmul(yp[wh][:, :], x[:, r, wh * P:(wh + 1) * P, c], fhs[:, r, :],
                                                        start=(r == 0), stop=(r == 1))
                            last.then_inc(s_y, 1)

                    def columns(c):
                        pe.wait_ge(s_ye, b * 64 + (2 * c + 4))
                        for s in range(2):
                            pe.wait_ge(s_xe, b * 64 + (2 * c + s + 1))
                            for k in range(4):
                                wh, q = k // 2, k % 2
                                last = nc.tensor.matmul(xp[s][:, :], y[:, c % 2, wh, q * NF + s:q * NF + s + P],
                                                        fws[:, q * (1 + s), wh, :], start=(k == 0), stop=(k == 3))
                            last.then_inc(s_xp, 1)

                    def inverse_rows(g, i):
                        n = g * GC + i
                        if i == 0:
                            pe.wait_ge(s_z, b * NG + (g + 2))
                        pe.wait_ge(s_ue, b * 32 + (n + 1))
                        for blk in range(2):
                            for k in range(4):
                                s, q = k // 2, k % 2
                                mat = ((0, 2), (1, 0))[blk][q]
                                last = nc.tensor.matmul(up[n % 2][:, blk, :],
                                                        (zr, zi)[q][:, g % 2, 2 * i + s, blk:blk + P], ecs[:, mat, s, :],
                                                        start=(k == 0), stop=(k == 3))
                        last.then_inc(s_u, 1)

                    def inverse_columns(g, i):
                        n = g * GC + i
                        pe.wait_ge(s_ue, b * 32 + (n + 3))
                        pe.wait_ge(s_oe, b * 32 + (n + 1))
                        for r in range(2):
                            for blk in range(2):
                                last = nc.tensor.matmul(op[n % 2][:, r, :], u[:, n % 2, blk, r * P:(r + 1) * P],
                                                        ews[:, blk, :], start=(blk == 0), stop=(blk == 1))
                        last.then_inc(s_o, 1)

                    for g in range(NG + 1):
                        if g < NG:
                            rows(g * GC)
                            for i in range(GC):
                                if i + 1 < GC:
                                    rows(g * GC + i + 1)
                                columns(g * GC + i)
                        if g:
                            inverse_rows(g - 1, 0)
                            for i in range(GC):
                                if i + 1 < GC:
                                    inverse_rows(g - 1, i + 1)
                                inverse_columns(g - 1, i)

            @block.scalar
            def _(act):
                act.sem_inc(s_ye, 2)
                act.sem_inc(s_xe, 2)
                act.sem_inc(s_ue, 2)
                act.sem_inc(s_oe, 2)
                act.sem_inc(s_store, 16)
                act.wait_ge(s_init, 3)
                with act.Fori(0, B) as b:
                    act.wait_ge(s_rc, b * 3 + 3)

                    def copy_rows(c):
                        for wh in range(2):
                            act.wait_ge(s_y, b * 64 + (2 * c + wh + 1))
                            nc.scalar.activation(y[:, c % 2, wh, :], yp[wh][:, :], ACT.Copy).then_inc(s_ye, 1)

                    def copy_columns(c):
                        if c % GC == 0:
                            act.wait_ge(s_ri, b * NG + (c // GC + 1))
                        for s in range(2):
                            act.wait_ge(s_xp, b * 64 + (2 * c + s + 2))
                            nc.scalar.activation(ri[:, 2 * (c % GC) + s, :, :].rearrange("p q k -> p (q k)"), xp[s][:, :],
                                                 ACT.Copy, scale=rc[:, c:c + 1]).then_inc(s_xe, 1)

                    def copy_u(g, i):
                        n = g * GC + i
                        act.wait_ge(s_u, b * 32 + (n + 1))
                        nc.scalar.activation(u[:, n % 2, :, :].rearrange("p k h -> p (k h)"),
                                             up[n % 2][:, :, :].rearrange("p k h -> p (k h)"), ACT.Copy).then_inc(s_ue, 1)

                    def copy_o(g, i):
                        n = g * GC + i
                        act.wait_ge(s_o, b * 32 + (n + 1))
                        if n == 0:
                            act.wait_ge(s_store, b * 16 + 16)
                        nc.scalar.activation(out[:, :, :, n], op[n % 2][:, :, :], ACT.Abs).then_inc(s_oe, 1)

                    def magnitudes(g):
                        act.wait_ge(s_dc, b * NG + (g + 1))
                        act.wait_ge(s_z, b * NG + (g + 1))
                        nc.scalar.activation(t[0][:, :, :], ri[:, :, 0, :], ACT.Abs).then_inc(s_abs, 1)
                        nc.scalar.activation(t[1][:, :, :], ri[:, :, 1, :], ACT.Abs).then_inc(s_abs, 1)

                    def arctangent(g):
                        act.wait_ge(s_ratio, b * NG + (g + 1))
                        nc.scalar.activation(t[4][:, :, :], t[3][:, :, :], ACT.Arctan).then_inc(s_atan, 1)
                        nc.scalar.activation(t[1][:, :, :], t[3][:, :, :], ACT.Square).then_inc(s_ach, 1)
                        act.wait_ge(s_ach, b * (2 * NG) + (2 * g + 1))
                        nc.scalar.activation(t[1][:, :, :], t[1][:, :, :], ACT.Sqrt, bias=one[:, 0:1]).then_inc(s_atan, 1)

                    def trigonometry(g):
                        act.wait_ge(s_phase, b * NG + (g + 1))
                        nc.scalar.activation(t[1][:, :, :], t[0][:, :, :], ACT.Sin).then_inc(s_trig, 1)
                        nc.scalar.activation(t[3][:, :, :], t[0][:, :, :], ACT.Abs).then_inc(s_ach, 1)
                        act.wait_ge(s_ach, b * (2 * NG) + (2 * g + 2))
                        nc.scalar.activation(t[3][:, :, :], t[3][:, :, :], ACT.Sin, bias=hpi[:, 0:1], scale=-1.0).then_inc(s_trig, 1)

                    for g in range(NG + 1):
                        if g < NG:
                            copy_rows(g * GC)
                            for i in range(GC):
                                if i + 1 < GC:
                                    copy_rows(g * GC + i + 1)
                                copy_columns(g * GC + i)
                            magnitudes(g)
                        if g:
                            copy_u(g - 1, 0)
                            copy_u(g - 1, 1)
                            copy_o(g - 1, 0)
                        if g < NG:
                            arctangent(g)
                        if g:
                            copy_u(g - 1, 2)
                            copy_o(g - 1, 1)
                            copy_u(g - 1, 3)
                            copy_o(g - 1, 2)
                        if g < NG:
                            trigonometry(g)
                        if g:
                            copy_o(g - 1, 3)
                    act.wait_ge(s_oe, b * 32 + 34)
                    act.dma_start(og[bass.ds(b, 1)].rearrange("a (r p) u n c -> p (a r) (u n c)", p=P),
                                  out[:, :, :, :].rearrange("p r w c -> p r (w c)")).then_inc(s_store, 16)
                act.wait_ge(s_store, B * 16 + 16)

            @block.vector
            def _(dve):
                dve.sem_inc(s_ri, 1)
                dve.wait_ge(s_const, 16 * (12 + B))
                nc.vector.memset(one[:, :], 1.0).then_inc(s_init, 1)
                nc.vector.memset(hpi[:, :], PI / 2).then_inc(s_init, 1)
                nc.vector.tensor_scalar(pw[:, :], pw[:, :], 2.0, None, ALU.mult).then_inc(s_init, 1)
                dve.wait_ge(s_init, 3)
                with dve.Fori(0, B) as b:
                    nc.vector.tensor_copy(rc[:, :], mr[:, bass.ds(b, 1), 1, :].rearrange("p a c -> p (a c)")).then_inc(s_rc, 1)
                    nc.vector.tensor_copy(dc[:, :], mr[0:1, bass.ds(b, 1), 0, :].rearrange("p a c -> p (a c)")).then_inc(s_rc, 1)
                    dve.wait_ge(s_rc, b * 3 + 2)
                    nc.vector.scalar_tensor_tensor(dc[:, :], dc[:, :], -float(PIX), rc[0:1, :], ALU.mult, ALU.mult).then_inc(s_rc, 1)
                    dve.wait_ge(s_rc, b * 3 + 3)
                    re, im = ri[:, :, 0, :], ri[:, :, 1, :]
                    t0, t1, t2, t3, t4 = (q[:, :, :] for q in t)
                    for g in range(NG):
                        ch = Chain(dve, s_ch, b * (NG * NS) + g * NS)
                        dve.wait_ge(s_xe, b * 64 + ((g + 1) * SL + 2))
                        zero = ri[0:1, 0:SL:2, 0, 0]
                        nc.vector.tensor_tensor(zero, zero, dc[:, g * GC:(g + 1) * GC], ALU.add).then_inc(s_dc, 1)
                        dve.wait_ge(s_abs, b * (2 * NG) + (2 * g + 2))
                        ch.step(nc.vector.tensor_tensor(t2, t0, t1, ALU.max))
                        ch.step(nc.vector.tensor_tensor(t3, t0, t1, ALU.min))
                        ch.step(nc.vector.tensor_tensor(t0, t1, t0, ALU.is_gt))
                        ch.step(nc.vector.tensor_scalar(t4, t2, TINY, None, ALU.max))
                        ch.step(nc.vector.reciprocal(t4, t4))
                        nc.vector.tensor_tensor(t3, t3, t4, ALU.mult).then_inc(s_ratio, 1)
                        dve.wait_ge(s_atan, b * (2 * NG) + (2 * g + 1))
                        ch.step(nc.vector.scalar_tensor_tensor(t0, t0, PI / 2, t4, ALU.mult, ALU.subtract))
                        ch.step(nc.vector.tensor_scalar(t4, re, 0.0, PI, ALU.is_lt, ALU.mult))
                        ch.step(nc.vector.scalar_tensor_tensor(t0, t0, -1.0, t0, ALU.mult, ALU.max))
                        ch.step(nc.vector.tensor_tensor(t0, t0, t4, ALU.subtract))
                        ch.step(nc.vector.scalar_tensor_tensor(t0, t0, -1.0, t0, ALU.mult, ALU.max))
                        ch.step(nc.vector.tensor_scalar(t4, im, 0.0, 0.5, ALU.is_ge, ALU.subtract))
                        nc.vector.tensor_tensor(t0, t0, t4, ALU.mult).then_inc(s_ri, 1)
                        dve.wait_ge(s_ri, b * NG + (g + 2))
                        for i in range(GC):
                            c, v = g * GC + i, t[0][:, 2 * i:2 * i + 2, :]
                            last = nc.vector.tensor_scalar(v, v, pw[:, c:c + 1], pb_[:, c:c + 1], ALU.mult, ALU.add)
                        ch.step(last)
                        ch.step(nc.vector.tensor_scalar(t4, t0, 0.5 / PI, ROUND, ALU.mult, ALU.add))
                        ch.step(nc.vector.tensor_scalar(t4, t4, ROUND, -2 * PI, ALU.subtract, ALU.mult))
                        ch.step(nc.vector.tensor_tensor(t0, t0, t4, ALU.add))
                        dve.wait_ge(s_atan, b * (2 * NG) + (2 * g + 2))
                        ch.step(nc.vector.tensor_tensor(t2, t2, t1, ALU.mult))
                        nc.vector.tensor_scalar(t0, t0, CLAMP, -CLAMP, ALU.min, ALU.max).then_inc(s_phase, 1)
                        for i in range(GC):
                            c, v = g * GC + i, t[2][:, 2 * i:2 * i + 2, :]
                            last = nc.vector.tensor_scalar(v, v, aw[:, c:c + 1], ab[:, c:c + 1], ALU.mult, ALU.add)
                        ch.step(last)
                        assert ch.n == NS
                        dve.wait_ge(s_trig, b * (2 * NG) + (2 * g + 1))
                        nc.vector.tensor_tensor(t1, t1, t2, ALU.mult).then_inc(s_prod, 1)
                        dve.wait_ge(s_trig, b * (2 * NG) + (2 * g + 2))
                        nc.vector.tensor_tensor(t3, t3, t2, ALU.mult).then_inc(s_prod, 1)

            @block.gpsimd
            def _(pool):
                pool.sem_inc(s_z, 1)
                with pool.Fori(0, B) as b:
                    for g in range(NG):
                        pool.wait_ge(s_prod, b * (2 * NG) + (2 * g + 2))
                        pool.sem_inc(s_pool, 1)
                        K = NF - 1
                        nc.gpsimd.tensor_scalar(zi[:, g % 2, :, 0:K], t[1][:, :, 0:K], 1e-8, None, ALU.add)
                        nc.gpsimd.tensor_scalar(zr[:, g % 2, :, K:NF], t[1][:, :, K:NF], 1e-8, -1.0, ALU.add, ALU.mult)
                        nc.gpsimd.tensor_scalar(zi[:, g % 2, :, K:NF], t[3][:, :, K:NF], 1e-8, 1e-8, ALU.add, ALU.add)
                        nc.gpsimd.tensor_scalar(zr[:, g % 2, :, 0:K], t[3][:, :, 0:K], 1e-8, 1e-8, ALU.add, ALU.add).then_inc(s_z, 1)


def project(nc, B, ol, og, x1l, x1g, proj_t, proj_b, eye, x2):
    NPC = B * 2 * WIN
    NB = NWIN // 4
    with ExitStack() as ctx:
        m = Mem(nc, ctx, "pj")
        xl, xg = m.sb("xl", [P, 4, NWIN, HALF]), m.sb("xg", [P, 4, NWIN, HALF])
        a = [m.sb(n, [P, 4, NWIN * HALF]) for n in ("al", "ag")]
        at = m.sb("at", [P, 2, 2, 512])
        o = m.sb("o", [P, 4, NWIN, C])
        pw = m.sb("pw", [P, 2, 4, C])
        pb_ = m.sb("pb", [P, C])
        idn = m.sb("idn", [P, P])
        tp = [[m.ps(f"tp{i}{s}", [P, 512]) for s in range(2)] for i in range(2)]
        pp = [m.ps(f"pp{i}", [P, 2, 4, C]) for i in range(4)]
        s_zero, s_const = m.sem("zero"), m.sem("const")
        s_in = [m.sem(f"in{j}") for j in range(4)]
        s_t, s_te, s_p, s_bias, s_add = m.sem("t"), m.sem("te"), m.sem("p"), m.sem("bias"), m.sem("add")
        s_store = [m.sem(f"store{j}") for j in range(4)]
        views = [v.rearrange("b (r p) u n c -> (b r) p u (n c)", p=P) for v in (x1l, x1g, ol, og)]
        x2v = x2.rearrange("b (r p) (n u) c -> (b r) p u n c", p=P, u=WIN)
        with nc.Block() as block:

            @block.sync
            def _(sp):
                sp.dma_start(idn[:, :], eye).then_inc(s_const, 16)
                sp.dma_start(pb_[:, :], spread(proj_b, [[1, C]])).then_inc(s_const, 16)
                sp.wait_ge(s_zero, 1)
                for w in range(4):
                    for s in range(2):
                        sp.dma_start(pw[w * HALF:(w + 1) * HALF, s, w, :], proj_t[s * HALF:(s + 1) * HALF, :]).then_inc(s_const, 16)
                with sp.Fori(0, B * 2) as t:
                    for u in range(WIN):
                        j = u % 4
                        sp.wait_ge(s_add, t * WIN + u + 1)
                        for dst, v in zip((xl[:, j].rearrange("p n c -> p (n c)"), xg[:, j].rearrange("p n c -> p (n c)"),
                                           a[0][:, j], a[1][:, j]), views):
                            sp.dma_start(dst, v[bass.ds(t, 1), :, u, :].rearrange("a p n -> (a p) n")).then_inc(s_in[j], 16)

            @block.tensor
            def _(pe):
                pe.wait_ge(s_const, 160)
                with pe.Fori(0, B * 2) as t:
                    for u in range(WIN):
                        j = u % 4
                        pe.wait_ge(s_in[j], t * 128 + (u // 4) * 64 + 64)
                        for q in range(3):
                            if q < 2:
                                pe.wait_ge(s_te, t * (2 * WIN) + (2 * u + q + 1))
                                for s in range(2):
                                    for g in range(4):
                                        gg = q * 4 + g
                                        last = nc.tensor.transpose(tp[q][s][:, g * P:(g + 1) * P],
                                                                   a[s][:, j, gg * P:(gg + 1) * P], idn[:, :])
                                last.then_inc(s_t, 1)
                            if q:
                                pe.wait_ge(s_te, t * (2 * WIN) + (2 * u + q + 2))
                                if q == 1:
                                    pe.wait_ge(s_add, t * WIN + u + 4)
                                for g in range(4):
                                    gg = (q - 1) * 4 + g
                                    for s in range(2):
                                        last = nc.tensor.matmul(pp[gg // 2][:, gg % 2, :, :].rearrange("p w d -> p (w d)"),
                                                                at[:, q - 1, s, g * P:(g + 1) * P],
                                                                pw[:, s, :, :].rearrange("p w d -> p (w d)"),
                                                                start=(s == 0), stop=(s == 1))
                        last.then_inc(s_p, 1)

            @block.scalar
            def _(act):
                act.sem_inc(s_te, 2)
                for j in range(4):
                    act.sem_inc(s_store[j], 16)
                with act.Fori(0, B * 2) as t:
                    for u in range(WIN):
                        for q in range(2):
                            act.wait_ge(s_t, t * (2 * WIN) + (2 * u + q + 1))
                            for s in range(2):
                                last = nc.scalar.activation(at[:, q, s, :], tp[q][s][:, :], ACT.Copy)
                            last.then_inc(s_te, 1)
                        act.wait_ge(s_add, t * WIN + u + 5)
                        act.dma_start(x2v[bass.ds(t, 1), :, u, :, :].rearrange("a p n c -> (a p) n c"),
                                      o[:, u % 4, :, :]).then_inc(s_store[u % 4], 16)
                for j in range(4):
                    act.wait_ge(s_store[j], B * 64 + 16)

            @block.gpsimd
            def _(pool):
                with pool.Fori(0, B * 2) as t:
                    for u in range(WIN):
                        j = u % 4
                        pool.wait_ge(s_in[j], t * 128 + (u // 4) * 64 + 64)
                        for h, v in enumerate((xl, xg)):
                            bias = pb_[:, h * HALF:(h + 1) * HALF]
                            bb = bass.AP(bias.tensor, bias.offset, [bias.ap[0], [0, NWIN], bias.ap[1]])
                            last = nc.gpsimd.tensor_tensor(v[:, j], v[:, j], bb, ALU.add)
                        last.then_inc(s_bias, 1)

            @block.vector
            def _(dve):
                dve.sem_inc(s_add, 4)
                nc.vector.memset(pw[:, :, :, :].rearrange("p s w d -> p (s w d)"), 0.0).then_inc(s_zero, 1)
                with dve.Fori(0, B * 2) as t:
                    for u in range(WIN):
                        j = u % 4
                        dve.wait_ge(s_bias, t * WIN + u + 1)
                        dve.wait_ge(s_p, t * WIN + u + 1)
                        dve.wait_ge(s_store[j], t * 32 + (u // 4) * 16 + 16)
                        for k in range(4):
                            ns = slice(16 * (k % 2) + k // 2, 16 * (k % 2) + k // 2 + 15, 2)
                            pv = pp[k][:, :, :, :].rearrange("p a w d -> p (a w) d")
                            for h, v in enumerate((xl, xg)):
                                ds = slice(h * HALF, (h + 1) * HALF)
                                last = nc.vector.tensor_tensor(o[:, j, ns, ds], pv[:, :, ds], v[:, j, ns, :], ALU.add)
                        last.then_inc(s_add, 1)


def mix_modes2(nc, B, modes, w_re, w_im, zd):
    NN = NM2 // 2
    S = w_re.shape[4]
    with ExitStack() as ctx:
        m = Mem(nc, ctx, "m2")
        a = m.sb("a", [P, 3, NN, B, NM2])
        w = m.sb("w", [P, 2, 2, NN, C * S])
        ws = m.sb("ws", [P, 2, 3, NN, C])
        o = m.sb("o", [B * NM2, NM2, 2, 2, C])
        op = [m.ps(f"op{i}", [B * NM2, 2, C]) for i in range(2)]
        s_const, s_ws, s_o, s_oe, s_store = m.sem("const"), m.sem("ws"), m.sem("o"), m.sem("oe"), m.sem("store")
        s_w = [m.sem(f"w{j}") for j in range(2)]
        with nc.Block() as block:

            @block.sync
            def _(sp):
                for par in range(2):
                    for b in range(B):
                        for q in range(3):
                            sp.dma_start(a[par * C:(par + 1) * C, q, :, b, :],
                                         modes[b, q].rearrange("c (r n k) -> r c n k", r=2, n=NN)[par]).then_inc(s_const, 16)
                with sp.Fori(0, NM2 // 2) as t:
                    for j in range(2):
                        sp.wait_ge(s_ws, t * 2 + j + 1)
                        for q, src in enumerate((w_re, w_im)):
                            sp.dma_start(w[:, j, q, :, :],
                                         src[bass.ds(t * 2 + j, 1)].rearrange("a (n r) c o s -> (r c) (a n) (o s)", r=2)).then_inc(s_w[j], 16)

            @block.vector
            def _(dve):
                dve.sem_inc(s_ws, 2)
                for n in range(NM2):
                    j = n % 2
                    dve.wait_ge(s_w[j], 32 * (n // 2 + 1))
                    if n >= 2:
                        dve.wait_ge(s_o, n - 1)
                    for q, src, neg in ((1, 0, False), (2, 1, False), (0, 1, True)):
                        last = nc.vector.tensor_reduce(ws[:, j, q, :, :].rearrange("p n o -> p (n o)"),
                                                       w[:, j, src, :, :].rearrange("p n (o s) -> p (n o) s", s=S),
                                                       axis=AX.X, op=ALU.add, negate=neg)
                    last.then_inc(s_ws, 1)

            @block.tensor
            def _(pe):
                pe.wait_ge(s_const, 16 * 6 * B)
                for n in range(NM2):
                    j = n % 2
                    pe.wait_ge(s_ws, n + 3)
                    if n >= 2:
                        pe.wait_ge(s_oe, n - 1)
                    for k in range(2 * NN):
                        i, q = k // 2, k % 2
                        last = nc.tensor.matmul(op[j][:, :, :], a[:, 1 + q, i, :, :].rearrange("p b k -> p (b k)"),
                                                ws[:, j, 1 - q:3 - q, i, :], start=(k == 0), stop=(k == 2 * NN - 1))
                    last.then_inc(s_o, 1)

            @block.scalar
            def _(act):
                for n in range(NM2):
                    j = n % 2
                    act.wait_ge(s_o, n + 1)
                    nc.scalar.activation(o[:, n, 0, :, :], op[j][:, :, :], ACT.Copy)
                    nc.scalar.activation(o[:, n, 1, 0, :], op[j][:, 1, :], ACT.Copy, scale=-1.0)
                    nc.scalar.activation(o[:, n, 1, 1, :], op[j][:, 0, :], ACT.Copy).then_inc(s_oe, 1)
                act.wait_ge(s_oe, NM2)
                for b in range(B):
                    for r in range(2):
                        act.dma_start(zd[b, r * NM2:(r + 1) * NM2].rearrange("m k q o -> k m (q o)"),
                                      o[b * NM2:(b + 1) * NM2, :, r].rearrange("k m q o -> k m (q o)")).then_inc(s_store, 16)
                act.wait_ge(s_store, 32 * B)


def point_rows(nc, B, x3, stats, eye, ft):
    NT = NPTS // P
    with ExitStack() as ctx:
        m = Mem(nc, ctx, "pr")
        x = m.sb("x", [P, 2, 2, NPTS])
        f = m.sb("f", [P, 2, NT, H])
        mr = m.sb("mr", [P, B, 2])
        sc, sh = m.sb("sc", [P, 1]), m.sb("sh", [P, B])
        idn = m.sb("idn", [P, P])
        tp = [m.ps(f"tp{i}", [P, 2, H]) for i in range(4)]
        s_const, s_sh, s_t, s_te = m.sem("const"), m.sem("sh"), m.sem("t"), m.sem("te")
        s_x = [m.sem(f"x{j}") for j in range(2)]
        s_store = [m.sem(f"store{j}") for j in range(2)]
        with nc.Block() as block:

            @block.sync
            def _(sp):
                sp.dma_start(idn[:, :], eye).then_inc(s_const, 16)
                for half in range(2):
                    for q in range(2):
                        sp.dma_start(mr[half * C:(half + 1) * C, :, q:q + 1],
                                     stats[:, q, :].rearrange("b (c a) -> c b a", a=1),
                                     allow_slow_non_contiguous=True).then_inc(s_const, 16)
                for b in range(B):
                    if b >= 2:
                        sp.wait_ge(s_t, (b - 1) * (NT // 2))
                    sp.dma_start(x[:, b % 2, :, :],
                                 x3[b, :, 0:NPTS // C, :].rearrange("(r p) w c -> p r (w c)", p=P)).then_inc(s_x[b % 2], 16)

            @block.tensor
            def _(pe):
                pe.wait_ge(s_const, 80)
                for b in range(B):
                    pe.wait_ge(s_x[b % 2], 16 * (b // 2 + 1))
                    for k in range(NT // 2):
                        n = b * (NT // 2) + k
                        if n >= 4:
                            pe.wait_ge(s_te, n - 3)
                        for i in range(2):
                            for r in range(2):
                                last = nc.tensor.transpose(tp[n % 4][:, i, r * P:(r + 1) * P],
                                                           x[:, b % 2, r, (2 * k + i) * P:(2 * k + i + 1) * P], idn[:, :])
                        last.then_inc(s_t, 1)

            @block.vector
            def _(dve):
                dve.wait_ge(s_const, 80)
                nc.vector.scalar_tensor_tensor(sh[:, :], mr[:, :, 0], -1.0, mr[:, :, 1], ALU.mult, ALU.mult).then_inc(s_sh, 1)

            @block.scalar
            def _(act):
                act.wait_ge(s_sh, 1)
                for b in range(B):
                    if b >= 2:
                        act.wait_ge(s_store[b % 2], 16 * (b // 2))
                    for k in range(NT // 2):
                        n = b * (NT // 2) + k
                        act.wait_ge(s_t, n + 1)
                        nc.scalar.activation(f[:, b % 2, 2 * k:2 * k + 2, :], tp[n % 4][:, :, :], ACT.Identity,
                                             bias=sh[:, b:b + 1], scale=mr[:, b, 1:2]).then_inc(s_te, 1)
                    act.wait_ge(s_te, (b + 1) * (NT // 2))
                    act.dma_start(ft[b].rearrange("(t p) h -> p t h", p=P), f[:, b % 2, :, :]).then_inc(s_store[b % 2], 16)
                for j in range(min(B, 2)):
                    act.wait_ge(s_store[j], 16 * ((B + 1 - j) // 2))


def select_points(nc, B, ft, mask_idx, ctx_idx, eye, cx, mn, mb, mx):
    TM, TC = NMASK // P, NCTX // P
    NT = TM + TC
    KC = 8
    NCH = NCTX // 512
    with ExitStack() as ctx:
        m = Mem(nc, ctx, "sp")
        rows = m.sb("rows", [P, 2, NT, H])
        nrm = m.sb("nrm", [P, NT, H])
        tc = m.sb("tc", [P, 2, NT * P])
        junk = m.sb("junk", [P, H])
        ss, rn = m.sb("ss", [P, NT]), m.sb("rn", [P, NT])
        cos = m.sb("cos", [P, 2, NCTX])
        best = m.sb("best", [P, TM, H])
        top, topi = m.sb("top", [P, TM, 8]), m.sb("topi", [P, TM, 8], U32)
        mxo = m.sb("mxo", [P, TM])
        idx0, idx = m.sb("idx0", [P, NT], I32), m.sb("idx", [P, NT], I32)
        idxf, bf, bi = m.sb("idxf", [P, NT]), m.sb("bf", [P, TM]), m.sb("bi", [P, TM], I32)
        idn = m.sb("idn", [P, P])
        tp = [m.ps(f"tp{i}", [P, 2, 2, P]) for i in range(2)]
        cp = [m.ps(f"cp{i}", [P, 512]) for i in range(4)]
        s_const, s_idx = m.sem("const"), m.sem("idx")
        s_g = [[m.sem(f"g{j}_{k}") for k in range(NT // KC)] for j in range(2)]
        s_cx, s_mn, s_mb = m.sem("cx"), m.sem("mn"), m.sem("mb")
        s_sq, s_root, s_rn, s_nrm = m.sem("sq"), m.sem("root"), m.sem("rn"), m.sem("nrm")
        s_t, s_te, s_c, s_ce = m.sem("t"), m.sem("te"), m.sem("c"), m.sem("ce")
        s_top, s_bi, s_ch, s_g2, s_mbs = m.sem("top"), m.sem("bi"), m.sem("ch"), m.sem("g2"), m.sem("mbs")
        ftf = ft.rearrange("b n h -> (b n) h")
        with nc.Block() as block:

            @block.sync
            def _(sp):
                sp.dma_start(idn[:, :], eye).then_inc(s_const, 16)
                sp.dma_start(idx0[:, 0:TM], mask_idx.rearrange("(t p) -> p t", p=P), allow_slow_non_contiguous=True).then_inc(s_const, 16)
                sp.dma_start(idx0[:, TM:NT], ctx_idx.rearrange("(t p) -> p t", p=P), allow_slow_non_contiguous=True).then_inc(s_const, 16)
                for b in range(B):
                    for k in range(TM // KC, NT // KC):
                        sp.wait_ge(s_g[b % 2][k], 16 * KC * (b // 2 + 1))
                    sp.dma_start(cx[b].rearrange("(t p) h -> p t h", p=P), rows[:, b % 2, TM:NT, :]).then_inc(s_cx, 16)
                    sp.wait_ge(s_nrm, b + 1)
                    sp.dma_start(mn[b].rearrange("(t p) h -> p t h", p=P), nrm[:, 0:TM, :]).then_inc(s_mn, 16)
                    sp.wait_ge(s_mbs, b + 1)
                    sp.dma_start(mb[b].rearrange("(t p) h -> p t h", p=P), best[:, :, :]).then_inc(s_mb, 16)
                    sp.dma_start(mx[b].rearrange("(t p) -> p t", p=P), mxo[:, :],
                                 allow_slow_non_contiguous=True).then_inc(s_mb, 16)
                sp.wait_ge(s_cx, 16 * B)
                sp.wait_ge(s_mn, 16 * B)
                sp.wait_ge(s_mb, 32 * B)

            @block.gpsimd
            def _(pool):
                def gather_rows(b):
                    if b >= 2:
                        pool.wait_ge(s_cx, 16 * (b - 1))
                        pool.wait_ge(s_nrm, b - 1)
                    pool.wait_ge(s_idx, b + 1)
                    for i in range(NT):
                        pool.indirect_dma_start(rows[:, b % 2, i, :], None, ftf,
                                                bass.IndirectOffsetOnAxis(ap=idx[:, i:i + 1], axis=0)).then_inc(s_g[b % 2][i // KC], 16)

                gather_rows(0)
                for b in range(B):
                    if b + 1 < B:
                        gather_rows(b + 1)
                    pool.wait_ge(s_bi, b + 1)
                    pool.wait_ge(s_cx, 16 * (b + 1))
                    if b:
                        pool.wait_ge(s_mb, 32 * b)
                    for i in range(TM):
                        pool.indirect_dma_start(best[:, i, :], None, cx[b],
                                                bass.IndirectOffsetOnAxis(ap=bi[:, i:i + 1], axis=0)).then_inc(s_g2, 16)

            @block.scalar
            def _(act):
                for b in range(B):
                    for i in range(NT):
                        if i % KC == 0:
                            act.wait_ge(s_g[b % 2][i // KC], 16 * KC * (b // 2 + 1))
                        last = nc.scalar.activation(junk[:, :], rows[:, b % 2, i, :], ACT.Square, accum_out=ss[:, i:i + 1])
                        last.then_inc(s_sq, 1)
                        act.wait_ge(s_sq, b * NT + i + 1)
                    nc.scalar.activation(rn[:, :], ss[:, :], ACT.Sqrt).then_inc(s_root, 1)
                    act.wait_ge(s_rn, b + 1)
                    if b:
                        act.wait_ge(s_mn, 16 * b)
                    for i in range(NT):
                        last = nc.scalar.activation(nrm[:, i, :], rows[:, b % 2, i, :], ACT.Copy, scale=rn[:, i:i + 1])
                    last.then_inc(s_nrm, 1)
                    for i in range(TM):
                        for k in range(NCH):
                            n = (b * TM + i) * NCH + k
                            act.wait_ge(s_c, n + 1)
                            if k == 0 and b * TM + i >= 2:
                                act.wait_ge(s_top, b * TM + i - 1)
                            nc.scalar.activation(cos[:, i % 2, k * 512:(k + 1) * 512], cp[n % 4][:, :], ACT.Copy).then_inc(s_ce, 1)
                    act.wait_ge(s_g2, 16 * TM * (b + 1))
                    act.wait_ge(s_bi, b + 1)
                    for i in range(TM):
                        last = nc.scalar.activation(best[:, i, :], best[:, i, :], ACT.Copy, scale=mxo[:, i:i + 1])
                    last.then_inc(s_mbs, 1)

            @block.tensor
            def _(pe):
                pe.wait_ge(s_const, 48)
                for b in range(B):
                    pe.wait_ge(s_nrm, b + 1)
                    for i in range(NT // 2):
                        n = b * (NT // 2) + i
                        if n >= 2:
                            pe.wait_ge(s_te, n - 1)
                        for q in range(2):
                            for r in range(2):
                                last = nc.tensor.transpose(tp[n % 2][:, q, r, :], nrm[:, 2 * i + q, r * P:(r + 1) * P], idn[:, :])
                        last.then_inc(s_t, 1)
                    pe.wait_ge(s_te, (b + 1) * (NT // 2))
                    for i in range(TM):
                        for k in range(NCH):
                            n = (b * TM + i) * NCH + k
                            if n >= 4:
                                pe.wait_ge(s_ce, n - 3)
                            for r in range(2):
                                c0 = TM * P + k * 512
                                last = nc.tensor.matmul(cp[n % 4][:, :], tc[:, r, i * P:(i + 1) * P], tc[:, r, c0:c0 + 512],
                                                        start=(r == 0), stop=(r == 1))
                            last.then_inc(s_c, 1)

            @block.vector
            def _(dve):
                ch = Chain(dve, s_ch)
                dve.wait_ge(s_const, 48)
                ch.step(nc.vector.tensor_copy(idxf[:, :], idx0[:, :]))
                nc.vector.tensor_copy(idx[:, :], idxf[:, :]).then_inc(s_idx, 1)
                for b in range(B):
                    dve.wait_ge(s_root, b + 1)
                    ch.step(nc.vector.tensor_scalar(rn[:, :], rn[:, :], CSA_EPS, None, ALU.add))
                    nc.vector.reciprocal(rn[:, :], rn[:, :]).then_inc(s_rn, 1)
                    if b + 1 < B:
                        ch.step(nc.vector.tensor_scalar(idxf[:, :], idxf[:, :], float(NPTS), None, ALU.add))
                        nc.vector.tensor_copy(idx[:, :], idxf[:, :]).then_inc(s_idx, 1)
                    for i in range(NT // 2):
                        n = b * (NT // 2) + i
                        dve.wait_ge(s_t, n + 1)
                        nc.vector.tensor_copy(tc[:, :, 2 * i * P:(2 * i + 2) * P].rearrange("p r (q n) -> p q r n", q=2),
                                              tp[n % 2][:, :, :, :]).then_inc(s_te, 1)
                    for i in range(TM):
                        n = b * TM + i
                        dve.wait_ge(s_ce, (n + 1) * NCH)
                        ch.step(nc.vector.max(top[:, i, :], cos[:, i % 2, :]))
                        nc.vector.max_index(topi[:, i, :], top[:, i, :], cos[:, i % 2, :]).then_inc(s_top, 1)
                    dve.wait_ge(s_top, (b + 1) * TM)
                    if b:
                        dve.wait_ge(s_mb, 32 * b)
                        dve.wait_ge(s_g2, 16 * TM * b)
                    ch.step(nc.vector.tensor_copy(bf[:, :], topi[:, :, 0]))
                    nc.vector.tensor_copy(mxo[:, :], top[:, :, 0])
                    nc.vector.tensor_copy(bi[:, :], bf[:, :]).then_inc(s_bi, 1)


def coherent_scan(nc, B, x3, stats, mn, mb, mx, gen, out):
    K = 16
    NL = NMASK // K
    W0 = NPTS // C
    WC = 32
    NPC = (W - W0) // WC
    CH = WC * C
    with ExitStack() as ctx:
        m = Mem(nc, ctx, "cs")
        mnt, mbt = m.sb("mnt", [B, 2, K, H]), m.sb("mbt", [B, 2, K, H])
        mxt, mxe = m.sb("mxt", [B, 2, K]), m.sb("mxe", [B, 2, K])
        rs = m.sb("rs", [B, 2])
        go = m.sb("go", [B, 2, K, H])
        num = m.sb("num", [B, 2, H])
        junk, junk2 = m.sb("junk", [B, H]), m.sb("junk2", [B, H])
        sm = m.sb("sm", [B, 2, 8])
        tiny = m.sb("tiny", [B, 1])
        xt = m.sb("xt", [P, 4, CH])
        mr = m.sb("mr", [P, B, 2, C])
        s1, s0 = m.sb("s1", [P, WC, C]), m.sb("s0", [P, WC, C])
        s_const, s_init, s_mxe = m.sem("const"), m.sem("init"), m.sem("mxe")
        s_in = [m.sem(f"in{j}") for j in range(2)]
        s_num, s_ss, s_root, s_ch, s_rs = m.sem("num"), m.sem("ss"), m.sem("root"), m.sem("ch"), m.sem("rs")
        s_cur = m.sem("cur")
        s_store = [m.sem(f"store{j}") for j in range(2)]
        s_x = [m.sem(f"x{j}") for j in range(4)]
        s_sc, s_mul, s_out = m.sem("sc"), m.sem("mul"), m.sem("out")
        s_xs = [m.sem(f"xs{j}") for j in range(4)]
        NCHAIN = 6
        with nc.Block() as block:

            @block.sync
            def _(sp):
                sp.dma_start(mr[:, :, :, :].rearrange("p b q c -> p (b q c)"), spread(stats, [[1, B * 2 * C]])).then_inc(s_const, 16)
                with sp.Fori(0, B * 2) as t:
                    for i in range(NPC):
                        j = i % 4
                        cols = slice(W0 + i * WC, W0 + (i + 1) * WC)
                        sp.wait_ge(s_xs[j], t * 16 * len(range(j, NPC, 4)) + 16 * (i // 4) + 16)
                        sp.dma_start(xt[:, j, :], x3.rearrange("b (r p) w c -> (b r) p w c", p=P)[bass.ds(t, 1), :, cols, :]
                                     .rearrange("a p w c -> (a p) (w c)")).then_inc(s_x[j], 16)
                        pi, pj = (i - 1) % NPC, (i - 1) % NPC % 4
                        if i:
                            sp.wait_ge(s_out, t * NPC + i)
                            sp.dma_start(out.rearrange("b (r p) w c -> (b r) p w c", p=P)[bass.ds(t, 1), :, W0 + pi * WC:W0 + (pi + 1) * WC, :]
                                         .rearrange("a p w c -> (a p) (w c)"), xt[:, pj, :]).then_inc(s_xs[pj], 16)
                    sp.wait_ge(s_out, t * NPC + NPC)
                    sp.dma_start(out.rearrange("b (r p) w c -> (b r) p w c", p=P)[bass.ds(t, 1), :, W - WC:W, :]
                                 .rearrange("a p w c -> (a p) (w c)"), xt[:, (NPC - 1) % 4, :]).then_inc(s_xs[(NPC - 1) % 4], 16)
                for j in range(4):
                    sp.wait_ge(s_xs[j], B * 2 * 16 * len(range(j, NPC, 4)) + 16)

            @block.gpsimd
            def _(pool):
                for j in range(4):
                    pool.sem_inc(s_xs[j], 16)
                pool.wait_ge(s_const, 16)
                for b in range(B):
                    r, mean = mr[:, b, 1, :], mr[:, b, 0, :]
                    rb = bass.AP(r.tensor, r.offset, [r.ap[0], [0, WC], r.ap[1]])
                    mb_ = bass.AP(mean.tensor, mean.offset, [mean.ap[0], [0, WC], mean.ap[1]])
                    if b:
                        pool.wait_ge(s_out, b * 2 * NPC)
                    nc.gpsimd.tensor_scalar(s1[:, :, :], rb, 1.0, None, ALU.add)
                    nc.gpsimd.tensor_tensor(s0[:, :, :], rb, mb_, ALU.mult).then_inc(s_sc, 1)
                    pool.wait_ge(s_sc, b + 1)
                    for r_ in range(2):
                        for i in range(NPC):
                            n = (b * 2 + r_) * NPC + i
                            j = i % 4
                            pool.wait_ge(s_x[j], 16 * ((b * 2 + r_) * len(range(j, NPC, 4)) + i // 4 + 1))
                            v = xt[:, j, :]
                            nc.gpsimd.tensor_tensor(v, v, s1[:, :, :].rearrange("p w c -> p (w c)"), ALU.mult).then_inc(s_mul, 1)
                            pool.wait_ge(s_mul, n + 1)
                            nc.gpsimd.tensor_tensor(v, v, s0[:, :, :].rearrange("p w c -> p (w c)"), ALU.subtract).then_inc(s_out, 1)

            @block.scalar
            def _(act):
                def load(n, j):
                    for t_, src in ((mnt, mn), (mbt, mb)):
                        v = src.rearrange("b (n k) h -> b n (k h)", k=K)[:, bass.ds(n, 1), :].rearrange("b a n -> b (a n)")
                        act.dma_start(t_[:, j, :, :].rearrange("b k h -> b (k h)"), v).then_inc(s_in[j], 16)
                    act.dma_start(mxt[:, j, :], mx.rearrange("b (n k) -> b n k", k=K)[:, bass.ds(n, 1), :]
                                  .rearrange("b a k -> b (a k)")).then_inc(s_in[j], 16)

                for j in range(2):
                    load(j, j)
                    act.sem_inc(s_store[j], 16)
                act.sem_inc(s_cur, 2)
                act.wait_ge(s_init, 3)

                def batch(n, j, more):
                    def current(k):
                        act.wait_ge(s_rs, n * K + (k + 1))
                        i = (k + 1) % 2
                        nc.scalar.activation(go[:, j, k, :], num[:, i, :], ACT.Copy, scale=rs[:, i:i + 1]).then_inc(s_cur, 1)

                    act.wait_ge(s_store[j], (n - j) * 8 + 16)
                    for k in range(K):
                        act.wait_ge(s_num, n * K + (k + 1))
                        i = k % 2
                        nc.scalar.activation(junk2[:, :], num[:, i, :], ACT.Square, accum_out=sm[:, i, 0:1]).then_inc(s_ss, 1)
                        act.wait_ge(s_ss, n * K + (k + 1))
                        nc.scalar.activation(sm[:, i, 1:2], sm[:, i, 0:1], ACT.Sqrt, bias=tiny[:, 0:1]).then_inc(s_root, 1)
                        if k:
                            current(k - 1)
                    current(K - 1)
                    act.wait_ge(s_cur, n * K + (K + 2))
                    dst = gen.rearrange("b (n k) h -> b n (k h)", k=K)[:, bass.ds(n, 1), :].rearrange("b a n -> b (a n)")
                    act.dma_start(dst, go[:, j, :, :].rearrange("b k h -> b (k h)")).then_inc(s_store[j], 16)
                    if more:
                        load(n + 2, j)

                with act.Fori(0, NL // 2 - 1) as t:
                    for j in range(2):
                        batch(t * 2 + j, j, True)
                for j in range(2):
                    batch(NL - 2 + j, j, False)
                for j in range(2):
                    act.wait_ge(s_store[j], (NL // 2) * 16 + 16)

            @block.vector
            def _(dve):
                nc.vector.memset(tiny[:, :], 1e-30).then_inc(s_init, 1)
                nc.vector.memset(num[:, 0, :], 0.0).then_inc(s_init, 1)
                nc.vector.memset(rs[:, 0:1], 1.0).then_inc(s_init, 1)
                dve.wait_ge(s_init, 3)
                dve.sem_inc(s_num, 1)
                with dve.Fori(0, NL // 2) as t:
                    for j in range(2):
                        n = t * 2 + j
                        dve.wait_ge(s_in[j], t * 48 + 48)
                        nc.vector.tensor_scalar(mxe[:, j, :], mxt[:, j, :], CSA_EPS, None, ALU.add).then_inc(s_mxe, 1)
                        dve.wait_ge(s_mxe, n + 1)
                        for k in range(K):
                            i, o = k % 2, (k + 1) % 2
                            a, r = sm[:, i, :], rs[:, i:i + 1]
                            ch = Chain(dve, s_ch, n * (K * NCHAIN) + k * NCHAIN)
                            nc.vector.tensor_tensor_reduce(out=junk[:, :], in0=mnt[:, j, k, :], in1=num[:, i, :], scale=1.0,
                                                           scalar=0.0, op0=ALU.mult, op1=ALU.add, accum_out=a[:, 2:3]).then_inc(s_ch, 1)
                            ch.n += 1
                            dve.wait_ge(s_root, n * K + (k + 1))
                            ch.step(nc.vector.tensor_scalar(a[:, 3:4], a[:, 1:2], r, CSA_EPS, ALU.mult, ALU.add))
                            ch.step(nc.vector.reciprocal(a[:, 4:5], a[:, 3:4]))
                            ch.step(nc.vector.tensor_scalar(a[:, 5:6], a[:, 2:3], a[:, 4:5], r, ALU.mult, ALU.mult))
                            nc.vector.tensor_scalar(a[:, 7:8], a[:, 5:6], 0.0, mxe[:, j, k:k + 1], ALU.max, ALU.add).then_inc(s_ch, 1)
                            ch.n += 1
                            ch.step(nc.vector.tensor_scalar(a[:, 6:7], a[:, 5:6], 0.0, r, ALU.max, ALU.mult))
                            dve.wait_ge(s_cur, n * K + (k + 1))
                            nc.vector.scalar_tensor_tensor(num[:, o, :], num[:, i, :], a[:, 6:7], mbt[:, j, k, :],
                                                           ALU.mult, ALU.add).then_inc(s_num, 1)
                            nc.vector.reciprocal(rs[:, o:o + 1], a[:, 7:8]).then_inc(s_rs, 1)
                            assert ch.n == NCHAIN
                            dve.wait_ge(s_num, n * K + (k + 2))
                            dve.wait_ge(s_rs, n * K + (k + 1))


def finish_points(nc, B, x3, ft, gen, mask_idx, eye, out):
    TM, NT = NMASK // P, NPTS // P
    with ExitStack() as ctx:
        m = Mem(nc, ctx, "fp")
        g = m.sb("g", [P, 2, TM, H])
        f = m.sb("f", [P, 2, NT, H])
        x = m.sb("x", [P, 2, 2, NPTS // 2])
        o = m.sb("o", [P, 2, 2, NPTS // 2])
        idx0, idx, idxf = m.sb("idx0", [P, TM], I32), m.sb("idx", [P, TM], I32), m.sb("idxf", [P, TM])
        idn = m.sb("idn", [P, P])
        tp = [m.ps(f"tp{i}", [P, 2, 2, P]) for i in range(4)]
        s_const, s_idx, s_ch = m.sem("const"), m.sem("idx"), m.sem("ch")
        s_g, s_f, s_x = ([m.sem(f"{n}{j}") for j in range(2)] for n in ("g", "f", "x"))
        s_sc, s_t, s_o = m.sem("sc"), m.sem("t"), m.sem("o")
        s_store = [m.sem(f"store{j}") for j in range(2)]
        ftf = ft.rearrange("b n h -> (b n) h")
        HT = NT // 2
        with nc.Block() as block:

            @block.sync
            def _(sp):
                sp.dma_start(idn[:, :], eye).then_inc(s_const, 16)
                sp.dma_start(idx0[:, :], mask_idx.rearrange("(t p) -> p t", p=P), allow_slow_non_contiguous=True).then_inc(s_const, 16)
                for b in range(B):
                    if b >= 2:
                        sp.wait_ge(s_sc, 16 * TM * (b - 1))
                    sp.dma_start(g[:, b % 2, :, :], gen[b].rearrange("(t p) h -> p t h", p=P)).then_inc(s_g[b % 2], 16)
                    sp.wait_ge(s_sc, 16 * TM * (b + 1))
                    if b >= 2:
                        sp.wait_ge(s_t, (b - 1) * HT)
                    sp.dma_start(f[:, b % 2, :, :], ft[b].rearrange("(t p) h -> p t h", p=P)).then_inc(s_f[b % 2], 16)
                    for q in range(2):
                        if b:
                            sp.wait_ge(s_o, ((b - 1) * 2 + q + 1) * (HT // 2))
                        c0 = q * (NPTS // C // 2)
                        sp.dma_start(x[:, q, :, :], x3[b, :, c0:c0 + NPTS // C // 2, :].rearrange("(r p) w c -> p r (w c)", p=P)).then_inc(s_x[q], 16)

            @block.gpsimd
            def _(pool):
                for b in range(B):
                    pool.wait_ge(s_g[b % 2], 16 * (b // 2 + 1))
                    pool.wait_ge(s_idx, b + 1)
                    for i in range(TM):
                        pool.indirect_dma_start(ftf, bass.IndirectOffsetOnAxis(ap=idx[:, i:i + 1], axis=0),
                                                g[:, b % 2, i, :], None).then_inc(s_sc, 16)

            @block.tensor
            def _(pe):
                pe.wait_ge(s_const, 32)
                for b in range(B):
                    pe.wait_ge(s_f[b % 2], 16 * (b // 2 + 1))
                    for k in range(HT):
                        n = b * HT + k
                        if n >= 4:
                            pe.wait_ge(s_o, n - 3)
                        for r in range(2):
                            for i in range(2):
                                last = nc.tensor.transpose(tp[n % 4][:, r, i, :], f[:, b % 2, 2 * k + i, r * P:(r + 1) * P], idn[:, :])
                        last.then_inc(s_t, 1)

            @block.vector
            def _(dve):
                ch = Chain(dve, s_ch)
                dve.wait_ge(s_const, 32)
                ch.step(nc.vector.tensor_copy(idxf[:, :], idx0[:, :]))
                nc.vector.tensor_copy(idx[:, :], idxf[:, :]).then_inc(s_idx, 1)
                for b in range(B):
                    if b + 1 < B:
                        ch.step(nc.vector.tensor_scalar(idxf[:, :], idxf[:, :], float(NPTS), None, ALU.add))
                        dve.wait_ge(s_sc, 16 * TM * (b + 1))
                        nc.vector.tensor_copy(idx[:, :], idxf[:, :]).then_inc(s_idx, 1)
                    for k in range(HT):
                        n, q = b * HT + k, k // (HT // 2)
                        dve.wait_ge(s_t, n + 1)
                        if k % (HT // 2) == 0:
                            dve.wait_ge(s_x[q], 16 * (b + 1))
                            if b:
                                dve.wait_ge(s_store[q], 16 * b)
                        c0 = (k % (HT // 2)) * 2 * P
                        nc.vector.tensor_tensor(o[:, q, :, c0:c0 + 2 * P], tp[n % 4][:, :, :, :].rearrange("p r i n -> p r (i n)"),
                                                x[:, q, :, c0:c0 + 2 * P], ALU.add).then_inc(s_o, 1)

            @block.scalar
            def _(act):
                for b in range(B):
                    for q in range(2):
                        act.wait_ge(s_o, (b * 2 + q + 1) * (HT // 2))
                        c0 = q * (NPTS // C // 2)
                        act.dma_start(out[b, :, c0:c0 + NPTS // C // 2, :].rearrange("(r p) w c -> p r (w c)", p=P),
                                      o[:, q, :, :]).then_inc(s_store[q], 16)
                for q in range(2):
                    act.wait_ge(s_store[q], 16 * B)


def build(nc, ins, out):
    x = ins["x"]
    B = x.shape[0]

    def dram(name, shape):
        return nc.dram_tensor(name, shape, F32, kind="Internal").ap()

    modes0 = dram("modes0", (B, 3, C, NM0 * NM0))
    zd0 = dram("zd0", (B, 2 * NM0, 2 * NM0, 2, C))
    x1l, x1g = dram("x1l", (B, H, WIN, NWIN, HALF)), dram("x1g", (B, H, WIN, NWIN, HALF))
    ol, og = dram("ol", (B, H, WIN, NWIN, HALF)), dram("og", (B, H, WIN, NWIN, HALF))
    stats1, stats3 = dram("stats1", (B, 2, C)), dram("stats3", (B, 2, C))
    x2, x3 = dram("x2", (B, H, W, C)), dram("x3", (B, H, W, C))
    modes2 = dram("modes2", (B, 3, C, NM2 * NM2))
    zd2 = dram("zd2", (B, 2 * NM2, NM2, 2, C))
    ft = dram("ft", (B, NPTS, H))
    cx = [dram(f"cx{b}", (NCTX, H)) for b in range(B)]
    mn, mb, gen = (dram(n, (B, NMASK, H)) for n in ("mn", "mb", "gen"))
    mx = dram("mx", (B, NMASK))

    forward_modes(nc, "f0", B, x, ins["f32a"], ins["f32b"], ins["pair"], modes0, NM0, 1.0 / np.sqrt(PIX), False)
    mix_modes0(nc, B, modes0, ins["L0_conv_fw1"], ins["L0_conv_fw2"], ins["L0_conv_W"], ins["eye64"], zd0)
    inverse_modes(nc, "i0", B, zd0, ins["ky0"], ins["kx0"], x, None, x1l, x1g, stats1,
                  ins["L0_conv_b"], float(PIX * np.sqrt(W * NF)))
    local_attention(nc, B, x1l, stats1, ins["w_qkv_t"], ins["L1_conv_b_qkv"], ins["L1_conv_pos_emb"],
                    ins["masks"], ins["eye"], ol)
    global_mixer(nc, B, x1g, stats1, ins["L1_conv_amp_w"], ins["L1_conv_amp_b"], ins["L1_conv_pha_w"],
                 ins["L1_conv_pha_b"], (ins["fh"], ins["fw"], ins["ec"], ins["ew"]), og)
    project(nc, B, ol, og, x1l, x1g, ins["proj_w_t"], ins["L1_conv_proj_b"], ins["eye"], x2)
    forward_modes(nc, "f2", B, x2, ins["f16a"], ins["f16b"], ins["pair"], modes2, NM2, 1.0, True)
    mix_modes2(nc, B, modes2, ins["L2_conv_weights_real"], ins["L2_conv_weights_imag"], zd2)
    inverse_modes(nc, "i2", B, zd2, ins["ky2"], ins["kx2"], x2, x3, None, None, stats3, None, None)
    point_rows(nc, B, x3, stats3, ins["eye"], ft)
    select_points(nc, B, ft, ins["L3_conv_mask_point_idx"], ins["L3_conv_nonmask_point_idx"], ins["eye"], cx, mn, mb, mx)
    coherent_scan(nc, B, x3, stats3, mn, mb, mx, gen, out)
    finish_points(nc, B, x3, ft, gen, ins["L3_conv_mask_point_idx"], ins["eye"], out)


def constants():
    def cos_sin(a, b):
        t = 2 * np.pi / H * (np.outer(a, b) % H)
        return np.cos(t), np.sin(t)

    n = np.arange(H)
    con = {}
    for nm in (NM0, NM2):
        c, s = cos_sin(n, np.arange(nm))
        con[f"f{nm}a"] = np.concatenate([c, -s], 1)
        con[f"f{nm}b"] = np.concatenate([s, c], 1)
    c, s = cos_sin(np.arange(NM0), n)
    twice = np.where(np.arange(NM0) == 0, 1.0, 2.0)[:, None]
    con["ky0"] = np.concatenate([twice * c, twice * s])
    c, s = cos_sin(np.concatenate([np.arange(NM0), H - NM0 + np.arange(NM0)]), n)
    con["kx0"] = np.stack([c, -s], 1).reshape(4 * NM0, H) / (PIX * np.sqrt(W * NF))
    c, s = cos_sin(np.arange(NM2), n)
    con["ky2"] = np.concatenate([c, s])
    con["kx2"] = np.stack([c, -s], 1).reshape(2 * NM2, H) * (0.5 / PIX)
    windows = np.arange(NWIN)
    order = (windows * WIN + np.arange(WIN)[:, None]).ravel()
    order2 = (np.concatenate([windows[::2], windows[1::2]]) * WIN + np.arange(WIN)[:, None]).ravel()
    c, s = cos_sin(n, np.arange(NF))
    con["fh"] = np.concatenate([c, -s], 1)
    c, s = c[order], s[order]
    con["fw"] = np.stack([np.concatenate(v, 1) for v in ((c, -s), (s, c), (-s, -c))])
    pos, neg = cos_sin(np.arange(P), n), cos_sin(H - 1 - np.arange(P), n)
    con["ec"] = np.stack([np.stack([pos[0], neg[0]]), np.stack([pos[1], neg[1]]), -np.stack([pos[1], neg[1]])])
    c, s = cos_sin(np.arange(NF), order2)
    c[1:-1] *= 2
    s[1:-1] *= 2
    con["ew"] = np.stack([c[:-1], np.concatenate([-s[1:-1], c[-1:]])]) / PIX
    con["eye"], con["eye64"] = np.eye(P), np.eye(C)
    con["pair"] = np.kron(np.eye(C // 2), np.ones((2, 2)))
    p = np.arange(P)
    con["masks"] = np.concatenate([(p // HALF % 2)[:, None] == np.arange(2), (p % HALF // HC)[:, None] == np.arange(HEADS)], 1)
    return {k: np.ascontiguousarray(v, np.float32) for k, v in con.items()}


def kernel(**inputs):
    import concourse.bacc as bacc
    from concourse.bass_utils import run_bass_kernel_spmd

    arrays = {k: np.asarray(v) for k, v in inputs.items() if k != "L3_conv_mask"}
    arrays["w_qkv_t"] = np.ascontiguousarray(arrays.pop("L1_conv_w_qkv").T)
    arrays["proj_w_t"] = np.ascontiguousarray(arrays.pop("L1_conv_proj_w").T)
    arrays.update(constants())
    nc = bacc.Bacc("TRN2", target_bir_lowering=False, num_devices=1)
    ins = {k: nc.dram_tensor(f"in_{k}", a.shape, mybir.dt.from_np(a.dtype), kind="ExternalInput").ap()
           for k, a in arrays.items()}
    out = nc.dram_tensor("out", arrays["x"].shape, F32, kind="ExternalOutput").ap()
    build(nc, ins, out)
    r = run_bass_kernel_spmd(nc, [{f"in_{k}": a for k, a in arrays.items()}], core_ids=[0])
    return r.results[0]["out"]
```

```python
from contextlib import ExitStack

import numpy as np

import concourse.bass as bass
from concourse import mybir

F32 = mybir.dt.float32
I32 = mybir.dt.int32
U32 = mybir.dt.uint32
ALU = mybir.AluOpType
ACT = mybir.ActivationFunctionType
AX = mybir.AxisListType

P = 128
H = W = 256
C = 64
HALF = C // 2
PIX = H * W
GROUP_N = 2 * PIX
EPS = 1e-5
NM0, NM2 = 32, 16
WIN, HEADS, HC = 8, 4, 8
NWIN = W // WIN
NF = W // 2 + 1
WARM = 4
NPTS = 64 * 64
NMASK, NCTX = 1024, 3072
CSA_EPS = 1e-8


class Chain:

    def __init__(self, eng, sem, base=0):
        self.eng, self.sem, self.base, self.n = eng, sem, base, 0

    def step(self, ins):
        self.n += 1
        ins.then_inc(self.sem, 1)
        self.eng.wait_ge(self.sem, self.base + self.n)


class Mem:

    def __init__(self, nc, ctx, tag):
        self.nc, self.ctx, self.tag, self.sems = nc, ctx, tag, []
        ctx.callback(self.clear)

    def sb(self, name, shape, dt=F32):
        return self.ctx.enter_context(self.nc.sbuf_tensor(f"{self.tag}_{name}", shape, dt))

    def ps(self, name, shape, dt=F32):
        return self.ctx.enter_context(self.nc.psum_tensor(f"{self.tag}_{name}", shape, dt))

    def sem(self, name):
        self.sems.append(self.nc.alloc_semaphore(f"{self.tag}_{name}"))
        return self.sems[-1]

    def clear(self):
        self.nc.clear_and_free_semaphores(self.sems)
        self.nc.all_engine_barrier()


def forward_modes(nc, tag, B, x, fa, fb, pair, modes, nm, out_scale, split_rows):
    n2 = 2 * nm
    n1 = max(n2, 64)
    copies = n1 // n2
    per_bank = 512 // n1
    nbank = C // per_bank
    rows_bank = 512 // n2
    kbank = (nm + rows_bank - 1) // rows_bank
    nsq, sqw = 16, 2048
    with ExitStack() as ctx:
        m = Mem(nc, ctx, tag)
        xt = m.sb("xt", [P, 2, 2, P * C])
        y = m.sb("y", [P, 2, C, n2])
        sq = m.sb("sq", [P, 2, sqw])
        part = m.sb("part", [P, nsq, C])
        tot_c = m.sb("tot_c", [P, C])
        ao = m.sb("ao", [C, 3, nm * nm])
        fas, fbs = m.sb("fas", [P, 2, n1]), m.sb("fbs", [P, 2, n2])
        pairs = m.sb("pairs", [C, C])
        ones = m.sb("ones", [P, 1])
        vs, st = m.sb("vs", [C, 2]), m.sb("st", [C, 8])
        yp = m.ps("yp", [P, 2, 512])
        ap = m.ps("ap", [C, kbank, 512])
        sp_ = m.ps("sp", [C, 512])
        s_const, s_ones = m.sem("const"), m.sem("ones")
        s_x = [m.sem(f"x{j}") for j in range(2)]
        s_xfree = [m.sem(f"xfree{j}") for j in range(2)]
        s_y, s_yfree = m.sem("y"), m.sem("yfree")
        s_sq, s_sqfree = m.sem("sq"), m.sem("sqfree")
        s_red, s_tot, s_vs, s_grp = m.sem("red"), m.sem("tot"), m.sem("vs"), m.sem("grp")
        s_a, s_var, s_std, s_ao = m.sem("a"), m.sem("var"), m.sem("std"), m.sem("ao")
        s_store, s_aofree, s_pe = m.sem("store"), m.sem("aofree"), m.sem("pe")
        s_ch = m.sem("ch")
        with nc.Block() as block:

            @block.sync
            def _(sp):
                for i in range(copies):
                    sp.dma_start(fas[:, :, i * n2:(i + 1) * n2], fa.rearrange("(a p) n -> p a n", p=P)).then_inc(s_const, 16)
                sp.dma_start(fbs[:, :, :], fb.rearrange("(a p) n -> p a n", p=P)).then_inc(s_const, 16)
                sp.dma_start(pairs[:, :], pair).then_inc(s_const, 16)
                with sp.Fori(0, B) as b:
                    for wh in range(2):
                        sp.wait_ge(s_xfree[wh], b + 1)
                        src = x[bass.ds(b, 1), :, wh * P:(wh + 1) * P, :]
                        sp.dma_start(xt[:, wh, :, :],
                                     src.rearrange("a (q p) w c -> p (a q) (w c)", p=P)).then_inc(s_x[wh], 16)

            @block.tensor
            def _(pe):
                pe.wait_ge(s_const, 32 + 16 * copies)
                pe.wait_ge(s_ones, 1)
                with pe.Fori(0, B) as b:
                    for wh in range(2):
                        pe.wait_ge(s_x[wh], b * 16 + 16)
                        xv = xt[:, wh, :, :].rearrange("p q (w c) -> p q w c", c=C)
                        for g in range(nbank):
                            n = wh * nbank + g
                            pe.wait_ge(s_yfree, b * (2 * nbank) + n + 1)
                            if n == 0:
                                pe.sem_inc(s_pe, 1)
                                for _ in range(WARM):
                                    nc.tensor.matmul(yp[:, 0, :], xt[:, 0, 0, 0:P], xt[:, 0, 0, 0:512], start=True, stop=True)
                            for j in range(per_bank):
                                c = g * per_bank + j
                                for hh in range(2):
                                    last = nc.tensor.matmul(yp[:, n % 2, j * n1:(j + 1) * n1], xv[:, hh, :, c],
                                                            fas[:, hh, :], start=(hh == 0), stop=(hh == 1))
                            last.then_inc(s_y, 1)
                    pe.wait_ge(s_yfree, b * (2 * nbank) + 2 * nbank + 2)
                    pe.wait_ge(s_ao, b + 1)
                    for k in range(nm):
                        for n in range(4):
                            wh, p = n // 2, n % 2
                            o = (k % rows_bank) * n2
                            last = nc.tensor.matmul(ap[:, k // rows_bank, o:o + n2], y[:, wh, :, p * nm + k],
                                                    (fas, fbs)[p][:, wh, 0:n2], start=(n == 0), stop=(n == 3))
                    last.then_inc(s_a, 1)
                    pe.wait_ge(s_red, b + 1)
                    nc.tensor.matmul(sp_[:, 0:1], tot_c[:, :], ones[:, :], start=True, stop=True).then_inc(s_tot, 1)
                    pe.wait_ge(s_vs, b * 2 + 1)
                    pe.sem_inc(s_pe, 1)
                    nc.tensor.matmul(sp_[:, 4:6], pairs[:, :], vs[:, :], start=True, stop=True).then_inc(s_grp, 1)

            @block.scalar
            def _(act):
                act.sem_inc(s_yfree, 2)
                act.sem_inc(s_xfree[0], 1)
                act.sem_inc(s_xfree[1], 1)
                with act.Fori(0, B) as b:
                    for wh in range(2):
                        act.wait_ge(s_x[wh], b * 16 + 16)
                        xf = xt[:, wh, :, :].rearrange("p q (s n) -> p (q s) n", n=sqw)
                        for s in range(nsq // 2):
                            n = wh * (nsq // 2) + s
                            act.wait_ge(s_sqfree, b * nsq + n + 1)
                            last = nc.scalar.activation(sq[:, n % 2, :], xf[:, s, :], ACT.Square)
                            last.then_inc(s_sq, 1)
                            for g in range(s * nbank // (nsq // 2), (s + 1) * nbank // (nsq // 2)):
                                k = wh * nbank + g
                                act.wait_ge(s_y, b * (2 * nbank) + k + 1)
                                if k == 0:
                                    act.wait_ge(s_a, b + 1)
                                nc.scalar.activation(y[:, wh, g * per_bank:(g + 1) * per_bank, :],
                                                     yp[:, k % 2, :].rearrange("p (c n) -> p c n", n=n1)[:, :, 0:n2],
                                                     ACT.Copy).then_inc(s_yfree, 1)
                        act.wait_ge(s_sq, b * nsq + (wh + 1) * (nsq // 2))
                        act.sem_inc(s_xfree[wh], 1)
                    act.wait_ge(s_var, b + 1)
                    nc.scalar.activation(st[:, 4:5], st[:, 3:4], ACT.Sqrt).then_inc(s_std, 1)

            @block.vector
            def _(dve):
                dve.sem_inc(s_sqfree, 2)
                dve.sem_inc(s_a, 1)
                dve.sem_inc(s_ao, 1)
                nc.vector.memset(ones[:, :], 1.0).then_inc(s_ones, 1)
                with dve.Fori(0, B) as b:
                    ch = Chain(dve, s_ch, b * 8)
                    for n in range(nsq):
                        dve.wait_ge(s_sq, b * nsq + n + 1)
                        nc.vector.reduce_sum(part[:, n, :], sq[:, n % 2, :].rearrange("p (w c) -> p c w", c=C),
                                             axis=AX.X).then_inc(s_sqfree, 1)
                    dve.wait_ge(s_sqfree, b * nsq + nsq + 2)
                    nc.vector.reduce_sum(tot_c[:, :], part[:, :, :].rearrange("p n c -> p c n"),
                                         axis=AX.X).then_inc(s_red, 1)
                    dve.wait_ge(s_tot, b + 1)
                    dve.wait_ge(s_a, b + 2)
                    nc.vector.tensor_copy(vs[:, 0:1], ap[:, 0, 0:1])
                    nc.vector.tensor_copy(vs[:, 1:2], sp_[:, 0:1]).then_inc(s_vs, 1)
                    dve.wait_ge(s_grp, b + 1)
                    ch.step(nc.vector.tensor_scalar(st[:, 0:2], sp_[:, 4:6], 1.0 / GROUP_N, None, ALU.mult))
                    ch.step(nc.vector.tensor_tensor(st[:, 2:3], st[:, 0:1], st[:, 0:1], ALU.mult))
                    ch.step(nc.vector.tensor_tensor(st[:, 2:3], st[:, 1:2], st[:, 2:3], ALU.subtract))
                    nc.vector.tensor_scalar(st[:, 3:4], st[:, 2:3], 0.0, EPS, ALU.max, ALU.add).then_inc(s_var, 1)
                    dve.wait_ge(s_std, b + 1)
                    ch.step(nc.vector.reciprocal(st[:, 5:6], st[:, 4:5]))
                    ch.step(nc.vector.tensor_scalar(st[:, 6:7], st[:, 5:6], out_scale, None, ALU.mult))
                    ch.step(nc.vector.tensor_scalar(st[:, 7:8], st[:, 5:6], -out_scale, None, ALU.mult))
                    ch.step(nc.vector.tensor_scalar(st[:, 0:1], st[:, 0:1], float(-PIX), None, ALU.mult))
                    nc.vector.tensor_tensor(vs[:, 0:1], ap[:, 0, 0:1], st[:, 0:1], ALU.add).then_inc(s_ch, 1)
                    dve.wait_ge(s_ch, b * 8 + 8)
                    dve.wait_ge(s_aofree, b + 1)
                    av = ap[:, :, :].rearrange("p a n -> p (a n)")[:, 0:nm * n2].rearrange("p (k q r) -> p k q r", q=2, r=nm)
                    for q, src, s in ((0, 1, 7), (1, 0, 6), (2, 1, 6)):
                        if split_rows:
                            for d in range(2):
                                dst = ao[:, q, d * nm * nm // 2:(d + 1) * nm * nm // 2]
                                last = nc.vector.tensor_scalar(
                                    dst.rearrange("p (r k) -> p k r", k=nm), av[:, :, src, d::2],
                                    st[:, s:s + 1], None, ALU.mult)
                        else:
                            last = nc.vector.tensor_scalar(ao[:, q, :].rearrange("p (k r) -> p k r", r=nm), av[:, :, src, :],
                                                           st[:, s:s + 1], None, ALU.mult)
                    last.then_inc(s_ao, 1)
                    dve.wait_ge(s_ao, b + 2)
                    nc.vector.tensor_tensor(ao[:, 1, 0:1], vs[:, 0:1], st[:, 6:7], ALU.mult).then_inc(s_vs, 1)

            @block.gpsimd
            def _(pool):
                pool.sem_inc(s_aofree, 1)
                with pool.Fori(0, B) as b:
                    pool.wait_ge(s_vs, b * 2 + 2)
                    pool.dma_start(modes[bass.ds(b, 1)].rearrange("a q p n -> p (a q) n"), ao[:, :, :]).then_inc(s_store, 16)
                    pool.wait_ge(s_store, b * 16 + 16)
                    pool.sem_inc(s_aofree, 1)


def mix_modes0(nc, B, modes, fw1, fw2, wmat, eye, zd):
    NK = 2
    with ExitStack() as ctx:
        m = Mem(nc, ctx, "mx")
        a = m.sb("a", [P, B, 3, NM0, NM0])
        fw = m.sb("fw", [P, 2, C, NK * NM0 * 2])
        z = m.sb("z", [P, B, 3, NM0])
        zo = m.sb("zo", [P, 2, B, 2, C])
        wi, eyes = m.sb("wi", [P, C]), m.sb("eyes", [P, C])
        mp = [m.ps(f"mp{f}", [P, 512]) for f in range(2)]
        qp = [m.ps(f"qp{f}", [P, B * 2 * C]) for f in range(2)]
        s_const = m.sem("const")
        s_fw = [m.sem(f"fw{j}") for j in range(2)]
        s_fwfree = m.sem("fwfree")
        s_wi, s_m, s_z, s_q, s_zo = m.sem("wi"), m.sem("m"), m.sem("z"), m.sem("q"), m.sem("zo")
        s_store = [m.sem(f"store{j}") for j in range(2)]
        nt = NM0 // NK
        with nc.Block() as block:

            def load_fw(sp, t, j):
                for f, src in enumerate((fw1, fw2)):
                    v = src.rearrange("i o (t x) y r -> i t o (x y r)", x=NK)
                    sp.dma_start(fw[f * C:(f + 1) * C, j, :, :],
                                 v[:, bass.ds(t, 1), :, :].rearrange("i a o n -> i (a o) n")).then_inc(s_fw[j], 16)

            @block.sync
            def _(sp):
                for f in range(2):
                    half = slice(f * C, (f + 1) * C)
                    sp.dma_start(wi[half, :], wmat).then_inc(s_const, 16)
                    sp.dma_start(eyes[half, :], eye).then_inc(s_const, 16)
                    for b in range(B):
                        sp.dma_start(a[half, b, :, :, :].rearrange("p q x y -> p q (x y)"),
                                     modes[b].rearrange("q i n -> i q n")).then_inc(s_const, 16)
                with sp.Fori(0, nt // 2) as t:
                    for j in range(2):
                        sp.wait_ge(s_fwfree, t * 2 + j + 1)
                        load_fw(sp, t * 2 + j, j)

            @block.tensor
            def _(pe):
                pe.sem_inc(s_fwfree, 2)
                pe.wait_ge(s_wi, 1)
                for t in range(nt):
                    j = t % 2
                    pe.wait_ge(s_fw[j], 32 * (t // 2 + 1))
                    fv = fw[:, j, :, :].rearrange("p o (x y r) -> p o x y r", y=NM0, r=2)
                    for x in range(NK):
                        n, kx = t * NK + x, t * NK + x
                        if n:
                            pe.wait_ge(s_z, n)
                        for ky in range(NM0):
                            for r in range(2):
                                for f in range(2):
                                    half = slice(f * C, (f + 1) * C)
                                    rhs = a[half, :, 1 - r:3 - r, kx, ky].rearrange("p b q -> p q b")
                                    last = nc.tensor.matmul(mp[f][half, ky * 2 * B:(ky + 1) * 2 * B],
                                                            fv[half, :, x, ky, r], rhs, start=(r == 0), stop=(r == 1))
                        last.then_inc(s_m, 1)
                        pe.wait_ge(s_z, n + 1)
                        if n:
                            pe.wait_ge(s_zo, n)
                        for b in range(B):
                            for p in range(2):
                                for f in range(2):
                                    half = slice(f * C, (f + 1) * C)
                                    o = (b * 2 + p) * C
                                    last = nc.tensor.matmul(qp[f][half, o:o + C],
                                                            z[half, b, 1 - p:3 - p, :].rearrange("p q y -> p (q y)"),
                                                            wi[half, :], start=True, stop=True)
                        last.then_inc(s_q, 1)
                    pe.sem_inc(s_fwfree, 1)

            @block.vector
            def _(dve):
                dve.wait_ge(s_const, 16 * (4 + 2 * B))
                nc.vector.tensor_tensor(wi[:, :], wi[:, :], eyes[:, :], ALU.add).then_inc(s_wi, 1)
                for n in range(NM0):
                    dve.wait_ge(s_m, n + 1)
                    for f in range(2):
                        half = slice(f * C, (f + 1) * C)
                        src = mp[f][half, 0:NM0 * 2 * B].rearrange("p (y q b) -> p q b y", q=2, b=B)
                        for q, p, sign in ((0, 1, 1.0), (1, 0, 1.0), (2, 1, -1.0)):
                            if n:
                                dve.wait_ge(s_q, n)
                            last = nc.vector.tensor_scalar(z[half, :, q, :], src[:, p], sign, None, ALU.mult)
                    last.then_inc(s_z, 1)

            @block.scalar
            def _(act):
                for n in range(NM0):
                    if n >= 2:
                        act.wait_ge(s_store[n % 2], 32 * (n // 2))
                    act.wait_ge(s_q, n + 1)
                    for f in range(2):
                        half = slice(f * C, (f + 1) * C)
                        last = nc.scalar.activation(zo[half, n % 2, :, :, :].rearrange("p b q o -> p (b q o)"),
                                                    qp[f][half, :], ACT.Copy)
                    last.then_inc(s_zo, 1)
                    act.wait_ge(s_zo, n + 1)
                    for f in range(2):
                        half = slice(f * C, (f + 1) * C)
                        act.dma_start(zd[:, :, f * NM0 + n, :, :].rearrange("b p q o -> p b (q o)"),
                                      zo[half, n % 2, :, :, :].rearrange("p b q o -> p b (q o)")).then_inc(s_store[n % 2], 16)
                for j in range(2):
                    act.wait_ge(s_store[j], 16 * NM0)


def inverse_modes(nc, tag, B, zd, ky_mat, kx_mat, res, out_nat, out_l, out_g, stats, bias, bias_scale):
    kr, nk2 = zd.shape[1], zd.shape[2]
    mc = nk2 * 2
    kp, mp = P, P
    WC = 32
    NP = W // WC
    NW = WC // WIN
    CH = WC * C
    NB = CH // 512
    NV = C // 2
    NFQ = NP * 2 * NB
    HELD = 3 * NB
    split = out_nat is None
    stores = 4 if split else 1
    with ExitStack() as ctx:
        m = Mem(nc, ctx, tag)
        zx = m.sb("zx", [kp, nk2, 2, C])
        v = m.sb("v", [mp, W, C])
        km, kxm = m.sb("km", [kp, W]), m.sb("kxm", [mp, H])
        xr = m.sb("xr", [P, 2, 2, CH])
        xo = m.sb("xo", [P, 2, 2 * CH])
        sq = m.sb("sq", [P, 2 * CH])
        acc = m.sb("acc", [P, 2 * CH])
        part = m.sb("part", [P, C, NP])
        tot = m.sb("tot", [P, 2, C])
        ones = m.sb("ones", [P, P])
        stp = m.sb("stp", [P, 6, C // 2])
        so = m.sb("so", [P, 2, C // 2, 2])
        brow = m.sb("brow", [1, C])
        vp = [m.ps(f"vp{j}", [mc, 2, W]) for j in range(2)]
        fp = [m.ps(f"fp{j}", [P, 512]) for j in range(4)]
        tp = m.ps("tp", [P, 2 * C])
        s_const, s_ones, s_pad = m.sem("const"), m.sem("ones"), m.sem("pad")
        s_acc, s_accfree, s_pool = m.sem("acc"), m.sem("accfree"), m.sem("pool")
        s_z, s_zb = m.sem("z"), m.sem("zb")
        s_vp, s_vused = m.sem("vp"), m.sem("vused")
        s_x = [m.sem(f"x{j}") for j in range(2)]
        s_f, s_fused = m.sem("f"), m.sem("fused")
        s_sq, s_sqfree = m.sem("sq"), m.sem("sqfree")
        s_store = [m.sem(f"store{j}") for j in range(2)]
        s_tot, s_tp, s_var, s_std = m.sem("tot"), m.sem("tp"), m.sem("var"), m.sem("std")
        s_st, s_sst, s_ch, s_pe = m.sem("st"), m.sem("sst"), m.sem("ch"), m.sem("pe")

        def local(t, j):
            return t[:, j, 0:CH].rearrange("p (r u n c) -> p r u n c", r=2, u=WIN, c=HALF)

        def glob(t, j):
            return t[:, j, CH:2 * CH].rearrange("p (r u n c) -> p r u n c", r=2, u=WIN, c=HALF)

        def channel_views(flat):
            if not split:
                return [(slice(0, C), flat.rearrange("p (n c) -> p c n", c=C))]
            return [(slice(h * HALF, (h + 1) * HALF),
                     flat[:, h * CH:(h + 1) * CH].rearrange("p (n c) -> p c n", c=HALF)) for h in range(2)]

        def for_images(eng, body, finish):
            body(0, True)
            if B > 1:
                with eng.Fori(1, B) as b:
                    body(b, False)
            finish(B - 1)

        with nc.Block() as block:

            @block.sync
            def _(sp):
                sp.wait_ge(s_pad, 1)
                sp.dma_start(km[0:kr, :], ky_mat).then_inc(s_const, 16)
                sp.dma_start(kxm[0:mc, :], kx_mat).then_inc(s_const, 16)
                if bias is not None:
                    sp.dma_start(brow[:, :], bias.rearrange("(a c) -> a c", a=1)).then_inc(s_const, 16)
                with sp.Fori(0, B) as b:
                    sp.wait_ge(s_vp, b * NV + 1)
                    sp.dma_start(zx[0:kr, :, :, :].rearrange("p k q o -> p (k q o)"),
                                 zd[bass.ds(b, 1)].rearrange("a p k q o -> (a p) (k q o)")).then_inc(s_z, 16)
                    for wc in range(NP):
                        sp.wait_ge(s_fused, b * NFQ + wc * 2 * NB + HELD - 2 * NB)
                        sp.dma_start(xr[:, wc % 2, :, :],
                                     res[bass.ds(b, 1), :, wc * WC:(wc + 1) * WC, :]
                                     .rearrange("a (r p) w c -> p (a r) (w c)", p=P)).then_inc(s_x[wc % 2], 16)

            @block.tensor
            def _(pe):
                pe.sem_inc(s_vp, 1)
                pe.wait_ge(s_const, 48 if bias is not None else 32)
                pe.wait_ge(s_ones, 1)
                pe.wait_ge(s_pad, 1)

                def group_sums(b):
                    pe.wait_ge(s_tot, b + 1)
                    nc.tensor.matmul(tp[:, :], ones[:, :], tot[:, :, :].rearrange("p a c -> p (a c)"),
                                     start=True, stop=True).then_inc(s_tp, 1)

                def body(b, first):
                    if bias is not None:
                        pe.wait_ge(s_zb, b + 1)
                    else:
                        pe.wait_ge(s_z, b * 16 + 16)
                    zv = zx[:, :, :, :].rearrange("p k q o -> p (k q) o")
                    for n in range(NV):
                        pe.wait_ge(s_vused, b * NV + n + 1)
                        pe.sem_inc(s_pe, 1)
                        if n == 0:
                            if not first:
                                pe.wait_ge(s_sq, b * NP)
                                pe.sem_inc(s_pe, 1)
                            for _ in range(4 * WARM):
                                nc.tensor.matmul(vp[0][:, 0, 0:P], ones[:, 0:mc], ones[:, :], start=True, stop=True)
                        for k in range(2):
                            last = nc.tensor.matmul(vp[n % 2][:, k, :], zv[:, :, 2 * n + k], km[:, :],
                                                    start=True, stop=True)
                        last.then_inc(s_vp, 1)
                    if not first:
                        group_sums(b - 1)
                    pe.wait_ge(s_vused, b * NV + NV + 2)
                    for wc in range(NP):
                        for r in range(2):
                            for i in range(NB):
                                n = (wc * 2 + r) * NB + i
                                pe.wait_ge(s_fused, b * NFQ + n + HELD - 3)
                                pe.sem_inc(s_pe, 1)
                                w0 = wc * WC + i * WIN
                                nc.tensor.matmul(fp[n % 4][:, :], kxm[:, r * P:(r + 1) * P],
                                                 v[:, w0:w0 + WIN, :].rearrange("p w c -> p (w c)"),
                                                 start=True, stop=True).then_inc(s_f, 1)

                for_images(pe, body, group_sums)

            @block.vector
            def _(dve):
                dve.sem_inc(s_fused, HELD)
                dve.sem_inc(s_sqfree, 1)
                nc.vector.memset(ones[:, :], 1.0).then_inc(s_ones, 1)
                if bias is not None:
                    dve.wait_ge(s_const, 48)
                    nc.vector.tensor_scalar(brow[:, :], brow[:, :], bias_scale, None, ALU.mult).then_inc(s_ones, 1)
                    dve.wait_ge(s_ones, 2)

                def finish(b):
                    ch = Chain(dve, s_ch, b * 5)
                    dve.wait_ge(s_tp, b + 1)
                    mean, msq, var = stp[:, 0, :], stp[:, 1, :], stp[:, 2, :]
                    ch.step(nc.vector.reduce_sum(stp[:, 0:2, :], tp[:, :].rearrange("p (a g t) -> p a g t", a=2, t=2), axis=AX.X))
                    ch.step(nc.vector.tensor_scalar(stp[:, 0:2, :], stp[:, 0:2, :], 1.0 / GROUP_N, None, ALU.mult))
                    ch.step(nc.vector.tensor_tensor(var, mean, mean, ALU.mult))
                    ch.step(nc.vector.tensor_tensor(var, msq, var, ALU.subtract))
                    nc.vector.tensor_scalar(stp[:, 3, :], var, 0.0, EPS, ALU.max, ALU.add).then_inc(s_var, 1)
                    dve.wait_ge(s_std, b + 1)
                    ch.step(nc.vector.reciprocal(stp[:, 5, :], stp[:, 4, :]))
                    dve.wait_ge(s_sst, b * 16 + 16)
                    for t in range(2):
                        nc.vector.tensor_copy(so[:, 0, :, t], mean)
                        last = nc.vector.tensor_copy(so[:, 1, :, t], stp[:, 5, :])
                    last.then_inc(s_st, 1)

                def body(b, first):
                    if bias is not None:
                        dve.wait_ge(s_z, b * 16 + 16)
                        nc.vector.tensor_tensor(zx[0:1, 0, 0, :], zx[0:1, 0, 0, :], brow[:, :], ALU.add).then_inc(s_zb, 1)

                    if not first:
                        finish(b - 1)

                    def square_sums(wc):
                        dve.wait_ge(s_sq, b * NP + wc + 1)
                        for cs, vv in channel_views(sq[:, :]):
                            last = nc.vector.reduce_sum(part[:, cs, wc], vv, axis=AX.X)
                        last.then_inc(s_sqfree, 1)

                    for wc in range(NP):
                        j = wc % 2
                        dve.wait_ge(s_x[j], b * (8 * NP) + 16 * (wc // 2) + 16)
                        dve.wait_ge(s_store[j], (b * (NP // 2) + wc // 2 + 1) * (16 * stores))
                        dve.wait_ge(s_acc, b * NP + wc + 1)
                        for r in range(2):
                            for i in range(NB):
                                n = (wc * 2 + r) * NB + i
                                dve.wait_ge(s_f, b * NFQ + n + 1)
                                f = fp[n % 4][:, :].rearrange("p (w c) -> p w c", c=C)
                                x = xr[:, j, r, i * 512:(i + 1) * 512].rearrange("p (w c) -> p w c", c=C)
                                if split:
                                    nc.vector.scalar_tensor_tensor(local(xo, j)[:, r, :, i, :], f[:, :, 0:HALF], 0.0,
                                                                   x[:, :, 0:HALF], ALU.max, ALU.add)
                                    last = nc.vector.scalar_tensor_tensor(
                                        glob(xo, j)[:, r, :, i, :], f[:, :, HALF:C], 0.0,
                                        x[:, :, HALF:C], ALU.max, ALU.add)
                                else:
                                    o = r * CH + i * 512
                                    last = nc.vector.tensor_tensor(xo[:, j, o:o + 512], fp[n % 4][:, :],
                                                                   xr[:, j, r, i * 512:(i + 1) * 512], ALU.add)
                                last.then_inc(s_fused, 1)
                        if wc:
                            square_sums(wc - 1)
                    square_sums(NP - 1)
                    dve.wait_ge(s_acc, b * NP + NP + 2)
                    for cs, vv in channel_views(acc[:, :]):
                        last = nc.vector.reduce_sum(tot[:, 0, cs], vv, axis=AX.X)
                    last.then_inc(s_accfree, 1)
                    dve.wait_ge(s_sqfree, b * NP + NP + 1)
                    nc.vector.reduce_sum(tot[:, 1, :], part[:, :, :], axis=AX.X).then_inc(s_tot, 1)

                for_images(dve, body, finish)

            @block.gpsimd
            def _(pool):
                for t in (zx[:, :, :, :].rearrange("p k q o -> p (k q o)"), km[:, :], kxm[:, :]) + \
                        ((v[:, :, :].rearrange("p w c -> p (w c)"),) if mc < mp else ()):
                    last = nc.gpsimd.memset(t, 0.0)
                last.then_inc(s_pad, 1)
                pool.sem_inc(s_acc, 2)
                with pool.Fori(0, B) as b:
                    for wc in range(NP):
                        pool.wait_ge(s_fused, b * NFQ + (wc + 1) * 2 * NB + HELD)
                        if wc == 0:
                            pool.wait_ge(s_accfree, b + 1)
                            pool.sem_inc(s_pool, 1)
                            nc.gpsimd.tensor_copy(acc[:, :], xo[:, 0, :]).then_inc(s_acc, 1)
                        else:
                            pool.wait_ge(s_acc, b * NP + wc + 2)
                            nc.gpsimd.tensor_tensor(acc[:, :], acc[:, :], xo[:, wc % 2, :], ALU.add).then_inc(s_acc, 1)

            @block.scalar
            def _(act):
                act.sem_inc(s_accfree, 1)
                act.sem_inc(s_vused, 2)
                act.sem_inc(s_sst, 16)
                for j in range(2):
                    act.sem_inc(s_store[j], 16 * stores)

                def finish(b):
                    act.wait_ge(s_var, b + 1)
                    nc.scalar.activation(stp[:, 4, :], stp[:, 3, :], ACT.Sqrt).then_inc(s_std, 1)
                    act.wait_ge(s_st, b + 1)
                    act.dma_start(stats[bass.ds(b, 1)].rearrange("a q c -> a (q c)"),
                                  so[0:1, :, :, :].rearrange("p q g t -> p (q g t)")).then_inc(s_sst, 16)

                def body(b, first):
                    for n in range(NV):
                        act.wait_ge(s_vp, b * NV + n + 2)
                        nc.scalar.activation(v[0:mc, :, 2 * n:2 * n + 2].rearrange("p w k -> p k w"), vp[n % 2][:, :, :],
                                             ACT.Copy).then_inc(s_vused, 1)
                    if not first:
                        finish(b - 1)
                    for wc in range(NP):
                        j = wc % 2
                        act.wait_ge(s_fused, b * NFQ + (wc + 1) * 2 * NB + HELD)
                        rows = slice(wc * WC, (wc + 1) * WC)
                        if split:
                            for half, out in ((local(xo, j), out_l), (glob(xo, j), out_g)):
                                for r in range(2):
                                    act.dma_start(out[bass.ds(b, 1), r * P:(r + 1) * P, :, wc * NW:(wc + 1) * NW, :]
                                                  .rearrange("a p u n c -> (a p) u (n c)"),
                                                  half[:, r].rearrange("p u n c -> p u (n c)")).then_inc(s_store[j], 16)
                        else:
                            act.dma_start(out_nat[bass.ds(b, 1), :, rows, :].rearrange("a (r p) w c -> p (a r) (w c)", p=P),
                                          xo[:, j, :].rearrange("p (r n) -> p r n", r=2)).then_inc(s_store[j], 16)
                        act.wait_ge(s_sqfree, b * NP + wc + 1)
                        nc.scalar.activation(sq[:, :], xo[:, j, :], ACT.Square).then_inc(s_sq, 1)

                for_images(act, body, finish)
                for j in range(2):
                    act.wait_ge(s_store[j], (B * (NP // 2) + 1) * (16 * stores))
                act.wait_ge(s_sst, B * 16 + 16)


def at_least(eng, sem, value):
    if not isinstance(value, int) or value > 0:
        eng.wait_ge(sem, value)


def local_attention(nc, B, x1l, stats, wqkv_t, b_qkv, pos, masks, eye, ol):
    NBLK = B * (H // (2 * WIN))
    NG, NU = 8, 16
    N2 = WIN * WIN
    LAG_M, LAG_E, LAG_T, LAG_V, LAG_N = 1, 2, 5, 6, 8
    RS, RT = 8, 2
    VC = HC + 1
    AT = {1: 0, 2: 1, 4: 2, 5: 3, 7: 4, 8: 5, 12: 6, 13: 7}
    ACT_AT = {2: (0, 0), 3: (1, 0), 4: (2, 0), 5: (2, 1), 6: (3, 0), 7: (3, 1), 8: (4, 0), 9: (4, 1), 10: (4, 2), 11: (4, 3)}
    DVE_AT = {8: (5, 0), 9: (5, 1), 10: (5, 2), 11: (5, 3), 12: (6, 0), 13: (6, 1), 14: (7, 0), 15: (7, 1)}
    T0, Q0, K0, V0 = 0, 2, 4, 6
    QS = HC ** -0.5
    with ExitStack() as ctx:
        m = Mem(nc, ctx, "la")
        x = m.sb("x", [P, 2, NG * P])
        tn = m.sb("tn", [P, NG, P])
        qx = m.sb("qx", [P, 2, NG * 2, 2, N2])
        kx = m.sb("kx", [P, 2, NG * 2, HEADS, N2])
        v2 = m.sb("v2", [P, 2, NG, 4, HEADS, 2, VC])
        s = m.sb("s", [P, RS, HEADS, 2, N2])
        et = m.sb("et", [P, RT, HEADS, P])
        mx = m.sb("mx", [P, RS, HEADS * 2])
        o = m.sb("o", [P, 2, 2, NU, HALF])
        rc = m.sb("rc", [P, 2, 2 * HEADS, 2])
        post = m.sb("post", [P, HEADS, 2, N2])
        idn = m.sb("idn", [P, P])
        wq, wk, wv = m.sb("wq", [P, P]), m.sb("wk", [P, P]), m.sb("wv", [P, P])
        bq, bk, bv = m.sb("bq", [P, 1]), m.sb("bk", [P, 1]), m.sb("bv", [P, 4, HALF])
        msk = m.sb("msk", [P, 6])
        sq_, bq_, bk_ = m.sb("sq_", [P, 2]), m.sb("bq_", [P, 2]), m.sb("bk_", [P, HEADS])
        mr = m.sb("mr", [P, B, 2])
        nb = m.sb("nb", [P, B])
        sc = m.sb("sc", [P, B, 16])
        sh = m.sb("sh", [P, B, 16])
        pa = [m.ps(f"pa{i}", [P, 512]) for i in range(2)]
        ps = [m.ps(f"ps{i}", [P, HEADS, 2, N2]) for i in range(2)]
        pt = [m.ps(f"pt{i}", [P, HEADS, P]) for i in range(2)]
        po = [m.ps(f"po{i}", [P, 2, HEADS, 2, 2, VC]) for i in range(2)]
        s_zero, s_const, s_prep, s_ready = m.sem("zero"), m.sem("const"), m.sem("prep"), m.sem("ready")
        s_x = [m.sem(f"x{j}") for j in range(2)]
        s_piece, s_apiece, s_dpiece = m.sem("piece"), m.sem("apiece"), m.sem("dpiece")
        s_s, s_add, s_max, s_sub, s_exp = m.sem("s"), m.sem("add"), m.sem("max"), m.sem("sub"), m.sem("exp")
        s_t, s_te, s_av, s_rc, s_norm = m.sem("t"), m.sem("te"), m.sem("av"), m.sem("rc"), m.sem("norm")
        s_act = m.sem("act")
        s_store = [m.sem(f"store{j}") for j in range(2)]
        xv = x1l.rearrange("b (j r) u n c -> (b j) (r u) (n c)", r=2 * WIN)
        ov = ol.rearrange("b (j d r) w (u t) c -> (b j) d (r w) u (t c)", d=2, r=WIN, u=2)

        def for_blocks(eng, body):
            body(0, 0, True, False)
            with eng.Fori(0, NBLK // 2 - 1) as t:
                body(t * 2 + 1, 1, False, False)
                body(t * 2 + 2, 0, False, False)
            body(NBLK - 1, 1, False, True)

        with nc.Block() as block:

            @block.sync
            def _(sp):
                for w in range(4):
                    rows = slice(w * HALF, (w + 1) * HALF)
                    for dst, i in ((bq, 0), (bk, 1)):
                        sp.dma_start(dst[rows, :], b_qkv[i * HALF:(i + 1) * HALF].rearrange("(c a) -> c a", a=1)).then_inc(s_const, 16)
                    for q in range(2):
                        sp.dma_start(mr[rows, :, q:q + 1], stats[:, q, 0:HALF].rearrange("b (c a) -> c b a", a=1),
                                     allow_slow_non_contiguous=True).then_inc(s_const, 16)
                sp.dma_start(msk[:, :], masks).then_inc(s_const, 16)
                sp.dma_start(idn[:, :], eye).then_inc(s_const, 16)
                bvv = b_qkv[2 * HALF:3 * HALF]
                sp.dma_start(bv[:, :, :], bass.AP(bvv.tensor, bvv.offset, [[0, P], [0, 4], [1, HALF]])).then_inc(s_const, 16)
                for u in range(2):
                    for d in range(2):
                        sp.dma_start(post[u * N2:(u + 1) * N2, :, d, :], pos[0].rearrange("h i j -> i h j")).then_inc(s_const, 16)
                sp.wait_ge(s_zero, 1)
                for w in range(4):
                    rows = slice(w * HALF, (w + 1) * HALF)
                    for i, dst in enumerate((wq, wk, wv)):
                        sp.dma_start(dst[rows, rows], wqkv_t[:, i * HALF:(i + 1) * HALF]).then_inc(s_const, 16)
                for j in range(2):
                    sp.dma_start(x[:, j, :], xv[j]).then_inc(s_x[j], 16)
                with sp.Fori(0, NBLK // 2 - 1) as t:
                    for j in range(2):
                        sp.wait_ge(s_piece, t * 16 + (j * 8 + 2))
                        sp.dma_start(x[:, j, :], xv[bass.ds(t * 2 + (2 + j), 1)].rearrange("a p n -> (a p) n")).then_inc(s_x[j], 16)

            @block.tensor
            def _(pe):
                pe.wait_ge(s_const, 16 * (4 * 4 + 3 + 4 + 12))

                def piece(p, n, j):
                    bank = pa[p % 2]
                    half = p % 2
                    if p < Q0:
                        if p == T0:
                            pe.wait_ge(s_x[j], (n // 2) * 16 + 16 if isinstance(n, int) else (n - j) * 8 + 16)
                        at_least(pe, s_dpiece, n * 3 - 1 + half)
                        for g in range(4):
                            gg = half * 4 + g
                            last = nc.tensor.transpose(bank[:, g * P:(g + 1) * P], x[:, j, gg * P:(gg + 1) * P], idn[:, :])
                    elif p < V0:
                        pe.wait_ge(s_apiece, n * 5 + (2 if p < K0 else p - 1))
                        last = nc.tensor.matmul(bank[:, :], (wq if p < K0 else wk)[:, :],
                                                tn[:, half * 4:half * 4 + 4, :].rearrange("p g n -> p (g n)"),
                                                start=True, stop=True)
                    else:
                        if half:
                            pe.wait_ge(s_dpiece, n * 3 + 1)
                        else:
                            pe.wait_ge(s_apiece, n * 5 + 5)
                        for g in range(4):
                            last = nc.tensor.matmul(bank[:, g * P:(g + 1) * P], tn[:, half * 4 + g, :], wv[:, :],
                                                    start=True, stop=True)
                    last.then_inc(s_piece, 1)

                def scores(n, k, j):
                    g = k // 2
                    if k == 0:
                        pe.wait_ge(s_apiece, n * 5 + 5)
                        pe.wait_ge(s_dpiece, n * 3 + 1)
                    at_least(pe, s_add, n * NU + k)
                    for d in range(2):
                        for e in range(2):
                            rows = slice(e * 64, e * 64 + 64)
                            last = nc.tensor.matmul(ps[e][:, :, d, :],
                                                    qx[rows, j, g * 2 + d, :, :].rearrange("p u i -> p (u i)"),
                                                    kx[rows, j, g * 2 + d, :, :], start=True, stop=True)
                            if d:
                                last.then_inc(s_s, 1)

                def transposes(n, k):
                    at_least(pe, s_te, n * NU + k - 1)
                    pe.wait_ge(s_exp, n * NU + k + 1)
                    for h in range(HEADS):
                        last = nc.tensor.transpose(pt[k % 2][:, h, :], s[:, k % RS, h, :, :].rearrange("p d j -> p (d j)"), idn[:, :])
                    last.then_inc(s_t, 1)

                def values(n, k, j):
                    g, e = k // 2, k % 2
                    if k == 0:
                        pe.wait_ge(s_dpiece, n * 3 + 3)
                    pe.wait_ge(s_te, n * NU + k + 1)
                    if k % 2 == 0:
                        at_least(pe, s_norm, n * (NU // 2) + k // 2 - 1)
                    for h in range(HEADS):
                        last = nc.tensor.matmul(po[(k // 2) % 2][:, e, h, :, :, :].rearrange("p u d c -> p (u d c)"),
                                                et[:, k % RT, h, :],
                                                v2[:, j, g, 2 * e:2 * e + 2, h, :, :].rearrange("p w d c -> p w (d c)"),
                                                start=True, stop=True)
                    last.then_inc(s_av, 1)

                for p in range(8):
                    piece(p, 0, 0)

                def body(n, j, first, last):
                    for k in range(NU):
                        if k % 2 == 0:
                            scores(n, k, j)
                        if k in AT and not last:
                            piece(AT[k], n + 1, 1 - j)
                        for lag, op in ((LAG_T, lambda n, k, j: transposes(n, k)), (LAG_V, values)):
                            if k >= lag:
                                op(n, k - lag, j)
                            elif not first:
                                op(n - 1, k - lag + NU, 1 - j)
                    if last:
                        for k in range(NU, NU + LAG_V):
                            if k < NU + LAG_T:
                                transposes(n, k - LAG_T)
                            values(n, k - LAG_V, j)

                for_blocks(pe, body)

            @block.vector
            def _(dve):
                for t in (wq, wk, wv):
                    last = nc.vector.memset(t[:, :], 0.0)
                last.then_inc(s_zero, 1)
                nc.vector.memset(v2[:, :, :, :, :, :, :].rearrange("p a g w h d c -> p (a g w h d c)"), 0.0).then_inc(s_prep, 1)
                dve.wait_ge(s_prep, 1)
                for d in range(2):
                    ones = v2[d * 64:(d + 1) * 64, :, :, :, :, d, HC:VC]
                    nc.vector.memset(ones.rearrange("p a g w h c -> p (a g w h) c"), 1.0).then_inc(s_prep, 1)
                dve.wait_ge(s_const, 16 * (4 * 4 + 3 + 4 + 12))
                nc.vector.tensor_scalar(sq_[:, :], msk[:, 0:2], QS, None, ALU.mult).then_inc(s_prep, 1)
                nc.vector.tensor_scalar(bk_[:, :], msk[:, 2:6], bk[:, 0:1], None, ALU.mult).then_inc(s_prep, 1)
                dve.wait_ge(s_prep, 5)
                nc.vector.tensor_scalar(bq_[:, :], sq_[:, :], bq[:, 0:1], None, ALU.mult).then_inc(s_prep, 1)
                nc.vector.scalar_tensor_tensor(nb[:, :], mr[:, :, 0], -1.0, mr[:, :, 1], ALU.mult, ALU.mult).then_inc(s_prep, 1)
                dve.wait_ge(s_prep, 7)
                for i in range(16):
                    nc.vector.tensor_copy(sc[:, :, i], mr[:, :, 1])
                    last = nc.vector.tensor_copy(sh[:, :, i], nb[:, :])
                last.then_inc(s_ready, 1)

                def add(n, k):
                    dve.wait_ge(s_s, n * NU + k + 1)
                    at_least(dve, s_t, n * NU + k - RS + 1)
                    nc.vector.tensor_tensor(s[:, k % RS], ps[k % 2][:, :, :, :], post[:, :, :, :], ALU.add).then_inc(s_add, 1)

                def maximum(n, k):
                    dve.wait_ge(s_add, n * NU + k + 1)
                    nc.vector.reduce_max(mx[:, k % RS, :], s[:, k % RS].rearrange("p h d j -> p (h d) j"), axis=AX.X).then_inc(s_max, 1)

                def divide(n, k, j):
                    i = (k // 2) % 2
                    dve.wait_ge(s_av, n * NU + k + 1)
                    if k == 1:
                        dve.wait_ge(s_store[j], (n - j) * 16 + 16)
                    for u in range(2):
                        rows = slice(u * 64, u * 64 + 64)
                        po_ = po[i][rows, :, :, u, :, :].rearrange("p e h d c -> p (e h) d c")
                        last = nc.vector.reciprocal(rc[rows, i, :, :], po_[:, :, :, HC])
                    last.then_inc(s_rc, 1)
                    dve.wait_ge(s_rc, n * (NU // 2) + k // 2 + 1)
                    for u in range(2):
                        rows = slice(u * 64, u * 64 + 64)
                        po_ = po[i][rows, :, :, u, :, :].rearrange("p e h d c -> p (e h) d c")
                        out = o[rows, j, :, k - 1:k + 1, :].rearrange("p d e (h c) -> p (e h) d c", h=HEADS)
                        r = rc[rows, i, :, :]
                        rb = bass.AP(r.tensor, r.offset, list(r.ap) + [[0, HC]])
                        last = nc.vector.tensor_tensor(out, po_[:, :, :, 0:HC], rb, ALU.mult)
                    last.then_inc(s_norm, 1)

                def piece(p, part, n, j):
                    if part == 0:
                        dve.wait_ge(s_piece, n * 8 + p + 1)
                    half, h, d = p % 2, part, part
                    if p < V0:
                        last = nc.vector.tensor_scalar(kx[:, j, half * 8:half * 8 + 8, h, :],
                                                       pa[p % 2][:, :].rearrange("p (a i) -> p a i", i=N2),
                                                       msk[:, 2 + h:3 + h], bk_[:, h:h + 1], ALU.mult, ALU.add)
                    else:
                        rows = slice(d * 64, d * 64 + 64)
                        for g in range(4):
                            last = nc.vector.tensor_tensor(
                                v2[rows, j, half * 4 + g, :, :, d, 0:HC],
                                pa[p % 2][rows, g * P:(g + 1) * P].rearrange("p (w h c) -> p w h c", w=4, h=HEADS),
                                bv[rows, :, :].rearrange("p w (h c) -> p w h c", h=HEADS), ALU.add)
                    if part == (HEADS if p < V0 else 2) - 1:
                        last.then_inc(s_dpiece, 1)

                for p, part in DVE_AT.values():
                    piece(p, part, 0, 0)

                def body(n, j, first, last):
                    for k in range(NU):
                        add(n, k)
                        if k >= LAG_M:
                            maximum(n, k - LAG_M)
                        elif not first:
                            maximum(n - 1, k - LAG_M + NU)
                        if k in DVE_AT and not last:
                            piece(*DVE_AT[k], n + 1, 1 - j)
                        q = k - LAG_N
                        if q % 2 and q >= 0:
                            divide(n, q, j)
                        elif q % 2 and not first:
                            divide(n - 1, q + NU, 1 - j)
                    if last:
                        for k in range(NU - LAG_M, NU):
                            maximum(n, k)
                        for q in range(NU - LAG_N, NU):
                            if q % 2:
                                divide(n, q, j)

                for_blocks(dve, body)

            @block.gpsimd
            def _(pool):
                def body(n, j, first, last):
                    for k in range(NU):
                        pool.wait_ge(s_max, n * NU + k + 1)
                        mk = mx[:, k % RS, :]
                        mb = bass.AP(mk.tensor, mk.offset, list(mk.ap) + [[0, N2]])
                        sv = s[:, k % RS].rearrange("p h d j -> p (h d) j")
                        nc.gpsimd.tensor_tensor(sv, sv, mb, ALU.subtract).then_inc(s_sub, 1)

                for_blocks(pool, body)

            @block.scalar
            def _(act):
                for j in range(2):
                    act.sem_inc(s_store[j], 16)
                act.wait_ge(s_ready, 1)

                def piece(p, part, n, j):
                    if part == 0:
                        act.wait_ge(s_piece, n * 8 + p + 1)
                    half, u, h = p % 2, part, part
                    if p < Q0:
                        act.sem_inc(s_act, 1)
                        scale = sc[:, :, :].rearrange("p b i -> p (b i)")[:, bass.ds(n, 1)]
                        shift = sh[:, :, :].rearrange("p b i -> p (b i)")[:, bass.ds(n, 1)]
                        last = nc.scalar.activation(tn[:, half * 4:half * 4 + 4, :].rearrange("p g n -> p (g n)"),
                                                    pa[p % 2][:, :], ACT.Identity, bias=shift, scale=scale)
                    elif p < K0:
                        last = nc.scalar.activation(qx[:, j, half * 8:half * 8 + 8, u, :],
                                                    pa[p % 2][:, :].rearrange("p (a i) -> p a i", i=N2),
                                                    ACT.Identity, bias=bq_[:, u:u + 1], scale=sq_[:, u:u + 1])
                    else:
                        last = nc.scalar.activation(kx[:, j, half * 8:half * 8 + 8, h, :],
                                                    pa[p % 2][:, :].rearrange("p (a i) -> p a i", i=N2),
                                                    ACT.Identity, bias=bk_[:, h:h + 1], scale=msk[:, 2 + h:3 + h])
                    if part == (1 if p < Q0 else 2 if p < K0 else HEADS) - 1:
                        last.then_inc(s_apiece, 1)

                def exponentials(n, k):
                    act.wait_ge(s_sub, n * NU + k + 1)
                    sk = s[:, k % RS].rearrange("p h d j -> p (h d j)")
                    nc.scalar.activation(sk, sk, ACT.Exp).then_inc(s_exp, 1)

                def copy_out(n, k, j):
                    act.wait_ge(s_t, n * NU + k + 1)
                    at_least(act, s_av, n * NU + k - 1)
                    nc.scalar.activation(et[:, k % RT].rearrange("p h n -> p (h n)"),
                                         pt[k % 2][:, :, :].rearrange("p h n -> p (h n)"), ACT.Copy).then_inc(s_te, 1)

                def store(n, j):
                    act.wait_ge(s_norm, n * (NU // 2) + NU // 2)
                    for u in range(2):
                        dst = ov[n, :, :, u, :] if isinstance(n, int) else ov[bass.ds(n, 1), :, :, u, :].rearrange("a d i n -> (a d) i n")
                        act.dma_start(dst.rearrange("d i n -> i d n"),
                                      o[u * 64:u * 64 + 64, j, :, :, :].rearrange("p d e c -> p d (e c)")).then_inc(s_store[j], 16)

                for p, part in ACT_AT.values():
                    piece(p, part, 0, 0)

                def body(n, j, first, last):
                    for k in range(NU):
                        if k >= LAG_E:
                            exponentials(n, k - LAG_E)
                        elif not first:
                            exponentials(n - 1, k - LAG_E + NU)
                        if k >= LAG_T:
                            copy_out(n, k - LAG_T, j)
                        elif not first:
                            copy_out(n - 1, k - LAG_T + NU, 1 - j)
                        if k in ACT_AT and not last:
                            piece(*ACT_AT[k], n + 1, 1 - j)
                        if k == LAG_N + 2 and not first:
                            store(n - 1, 1 - j)
                    if last:
                        for k in range(NU, NU + LAG_T):
                            if k < NU + LAG_E:
                                exponentials(n, k - LAG_E)
                            copy_out(n, k - LAG_T, j)
                        store(n, j)

                for_blocks(act, body)
                for j in range(2):
                    act.wait_ge(s_store[j], NBLK * 16 + 16)


def spread(ap, dims):
    return bass.AP(ap.tensor, ap.offset, [[0, P]] + dims)


def global_mixer(nc, B, x1g, stats, amp_w, amp_b, pha_w, pha_b, mats, og):
    fh, fw_, ec, ew = mats
    NG, GC = 8, 4
    SL = 2 * GC
    LAG = 2
    PI = float(np.pi)
    ROUND = 1.5 * 2.0 ** 23
    CLAMP = 3.1415925
    TINY = 1e-30
    NS = 16
    with ExitStack() as ctx:
        m = Mem(nc, ctx, "gm")
        x = m.sb("x", [P, 2, W, HALF])
        out = m.sb("out", [P, 2, W, HALF])
        y = m.sb("y", [P, 2, 2, 2 * NF])
        ri = m.sb("ri", [P, SL, 2, NF])
        t = [m.sb(f"t{i}", [P, SL, NF]) for i in range(5)]
        zr, zi = (m.sb(n, [P, 2, SL, NF]) for n in ("zr", "zi"))
        u = m.sb("u", [P, 2, 2, H])
        fhs = m.sb("fhs", [P, 2, 2 * NF])
        fws = m.sb("fws", [P, 3, 2, 2 * NF])
        ecs = m.sb("ecs", [P, 3, 2, H])
        ews = m.sb("ews", [P, 2, W])
        aw, ab, pw, pb_ = (m.sb(n, [P, HALF]) for n in ("aw", "ab", "pw", "pb"))
        mr = m.sb("mr", [P, B + 1, 2, HALF])
        rc, dc = m.sb("rc", [P, HALF]), m.sb("dc", [1, HALF])
        one, hpi = m.sb("one", [P, 1]), m.sb("hpi", [P, 1])
        yp = [m.ps(f"yp{i}", [P, 2 * NF]) for i in range(2)]
        xp = [m.ps(f"xp{i}", [P, 2 * NF]) for i in range(2)]
        up = [m.ps(f"up{i}", [P, 2, H]) for i in range(2)]
        op = [m.ps(f"op{i}", [P, 2, W]) for i in range(2)]
        s_const, s_init, s_x = m.sem("const"), m.sem("init"), m.sem("x")
        s_y, s_ye, s_xp, s_xe = m.sem("y"), m.sem("ye"), m.sem("xp"), m.sem("xe")
        s_u, s_ue, s_o, s_oe = m.sem("u"), m.sem("ue"), m.sem("o"), m.sem("oe")
        s_rc, s_ch, s_ach = m.sem("rc"), m.sem("ch"), m.sem("ach")
        s_dc, s_abs, s_ratio, s_atan, s_phase, s_trig, s_ri, s_prod, s_z = (
            m.sem(n) for n in ("dc", "abs", "ratio", "atan", "phase", "trig", "ri", "prod", "z"))
        s_store, s_pool = m.sem("store"), m.sem("pool")

        def for_images(eng, body):
            body(0, True)
            if B > 1:
                with eng.Fori(1, B) as b:
                    body(b, False)

        with nc.Block() as block:

            @block.sync
            def _(sp):
                sp.dma_start(fhs[:, :, :], fh.rearrange("(a p) n -> p a n", p=P)).then_inc(s_const, 16)
                for i in range(3):
                    sp.dma_start(fws[:, i, :, :], fw_[i].rearrange("(a p) n -> p a n", p=P)).then_inc(s_const, 16)
                    sp.dma_start(ecs[:, i, :, :], ec[i].rearrange("a p n -> p a n")).then_inc(s_const, 16)
                sp.dma_start(ews[:, :, :], ew.rearrange("a p n -> p a n")).then_inc(s_const, 16)
                for dst, src in ((aw, amp_w), (ab, amp_b), (pw, pha_w), (pb_, pha_b)):
                    sp.dma_start(dst[:, :], spread(src, [[1, HALF]])).then_inc(s_const, 16)
                for b in range(B):
                    sp.dma_start(mr[:, b, :, :], spread(stats[b, :, HALF:C], [[C, 2], [1, HALF]])).then_inc(s_const, 16)
                with sp.Fori(0, B) as b:
                    sp.wait_ge(s_y, b * 64 + 1)
                    sp.dma_start(x[:, :, :, :].rearrange("p r w c -> p r (w c)"),
                                 x1g[bass.ds(b, 1)].rearrange("a (r p) u n c -> p (a r) (u n c)", p=P)).then_inc(s_x, 16)

            @block.tensor
            def _(pe):
                pe.sem_inc(s_y, 1)
                pe.wait_ge(s_const, 16 * (12 + B))
                def rows(b, c):
                    for wh in range(2):
                        pe.wait_ge(s_ye, b * 64 + (2 * c + wh + 1))
                        for r in range(2):
                            last = nc.tensor.matmul(yp[wh][:, :], x[:, r, wh * P:(wh + 1) * P, c], fhs[:, r, :],
                                                    start=(r == 0), stop=(r == 1))
                        last.then_inc(s_y, 1)

                def columns(b, c):
                    pe.wait_ge(s_ye, b * 64 + (2 * c + 4))
                    for s in range(2):
                        pe.wait_ge(s_xe, b * 64 + (2 * c + s + 1))
                        for k in range(4):
                            wh, q = k // 2, k % 2
                            last = nc.tensor.matmul(xp[s][:, :], y[:, c % 2, wh, q * NF + s:q * NF + s + P],
                                                    fws[:, q * (1 + s), wh, :], start=(k == 0), stop=(k == 3))
                        last.then_inc(s_xp, 1)

                def inverse_rows(b, g, i):
                    n = g * GC + i
                    if i == 0:
                        pe.wait_ge(s_z, b * NG + (g + 2))
                    pe.wait_ge(s_ue, b * 32 + (n + 1))
                    for blk in range(2):
                        for k in range(4):
                            s, q = k // 2, k % 2
                            mat = ((0, 2), (1, 0))[blk][q]
                            last = nc.tensor.matmul(up[n % 2][:, blk, :],
                                                    (zr, zi)[q][:, g % 2, 2 * i + s, blk:blk + P], ecs[:, mat, s, :],
                                                    start=(k == 0), stop=(k == 3))
                    last.then_inc(s_u, 1)

                def inverse_columns(b, g, i):
                    n = g * GC + i
                    pe.wait_ge(s_ue, b * 32 + (n + 3))
                    pe.wait_ge(s_oe, b * 32 + (n + 1))
                    for r in range(2):
                        for blk in range(2):
                            last = nc.tensor.matmul(op[n % 2][:, r, :], u[:, n % 2, blk, r * P:(r + 1) * P],
                                                    ews[:, blk, :], start=(blk == 0), stop=(blk == 1))
                    last.then_inc(s_o, 1)

                def inverse(b, g):
                    inverse_rows(b, g, 0)
                    for i in range(GC):
                        if i + 1 < GC:
                            inverse_rows(b, g, i + 1)
                        inverse_columns(b, g, i)

                def body(b, first):
                    pe.wait_ge(s_x, b * 16 + 16)
                    for g in range(NG):
                        rows(b, g * GC)
                        for i in range(GC):
                            if i + 1 < GC:
                                rows(b, g * GC + i + 1)
                            columns(b, g * GC + i)
                        if g >= LAG:
                            inverse(b, g - LAG)
                        elif not first:
                            inverse(b - 1, g - LAG + NG)

                for_images(pe, body)
                for g in range(NG - LAG, NG):
                    inverse(B - 1, g)

            @block.scalar
            def _(act):
                act.sem_inc(s_ye, 2)
                act.sem_inc(s_xe, 2)
                act.sem_inc(s_ue, 2)
                act.sem_inc(s_oe, 2)
                act.sem_inc(s_store, 16)
                act.wait_ge(s_init, 4)
                def copy_rows(b, c):
                    for wh in range(2):
                        act.wait_ge(s_y, b * 64 + (2 * c + wh + 2))
                        nc.scalar.activation(y[:, c % 2, wh, :], yp[wh][:, :], ACT.Copy).then_inc(s_ye, 1)

                def copy_columns(b, c):
                    if c % GC == 0:
                        act.wait_ge(s_ri, b * NG + (c // GC + 1))
                    for s in range(2):
                        act.wait_ge(s_xp, b * 64 + (2 * c + s + 1))
                        nc.scalar.activation(ri[:, 2 * (c % GC) + s, :, :].rearrange("p q k -> p (q k)"), xp[s][:, :],
                                             ACT.Copy, scale=rc[:, c:c + 1]).then_inc(s_xe, 1)

                def copy_u(b, g, i):
                    n = g * GC + i
                    act.wait_ge(s_u, b * 32 + (n + 1))
                    nc.scalar.activation(u[:, n % 2, :, :].rearrange("p k h -> p (k h)"),
                                         up[n % 2][:, :, :].rearrange("p k h -> p (k h)"), ACT.Copy).then_inc(s_ue, 1)

                def copy_o(b, g, i):
                    n = g * GC + i
                    act.wait_ge(s_o, b * 32 + (n + 1))
                    if n == 0:
                        act.wait_ge(s_store, b * 16 + 16)
                    nc.scalar.activation(out[:, :, :, n], op[n % 2][:, :, :], ACT.Abs).then_inc(s_oe, 1)
                    if n == HALF - 1:
                        act.wait_ge(s_oe, b * 32 + 34)
                        dst = og[b:b + 1] if isinstance(b, int) else og[bass.ds(b, 1)]
                        act.dma_start(dst.rearrange("a (r p) u n c -> p (a r) (u n c)", p=P),
                                      out[:, :, :, :].rearrange("p r w c -> p r (w c)")).then_inc(s_store, 16)

                def magnitudes(b, g):
                    act.wait_ge(s_dc, b * NG + (g + 1))
                    act.wait_ge(s_z, b * NG + (g + 1))
                    nc.scalar.activation(t[0][:, :, :], ri[:, :, 0, :], ACT.Abs).then_inc(s_abs, 1)
                    nc.scalar.activation(t[1][:, :, :], ri[:, :, 1, :], ACT.Abs).then_inc(s_abs, 1)

                def arctangent(b, g):
                    act.wait_ge(s_ratio, b * NG + (g + 1))
                    nc.scalar.activation(t[4][:, :, :], t[3][:, :, :], ACT.Arctan).then_inc(s_atan, 1)
                    nc.scalar.activation(t[1][:, :, :], t[3][:, :, :], ACT.Square).then_inc(s_ach, 1)
                    act.wait_ge(s_ach, b * (2 * NG) + (2 * g + 1))
                    nc.scalar.activation(t[1][:, :, :], t[1][:, :, :], ACT.Sqrt, bias=one[:, 0:1]).then_inc(s_atan, 1)

                def trigonometry(b, g):
                    act.wait_ge(s_phase, b * NG + (g + 1))
                    nc.scalar.activation(t[1][:, :, :], t[0][:, :, :], ACT.Sin).then_inc(s_trig, 1)
                    nc.scalar.activation(t[3][:, :, :], t[0][:, :, :], ACT.Abs).then_inc(s_ach, 1)
                    act.wait_ge(s_ach, b * (2 * NG) + (2 * g + 2))
                    nc.scalar.activation(t[3][:, :, :], t[3][:, :, :], ACT.Sin, bias=hpi[:, 0:1], scale=-1.0).then_inc(s_trig, 1)

                def inverse_copies(b, g, between):
                    copy_u(b, g, 0)
                    copy_u(b, g, 1)
                    copy_o(b, g, 0)
                    copy_u(b, g, 2)
                    copy_o(b, g, 1)
                    copy_u(b, g, 3)
                    between()
                    copy_o(b, g, 2)
                    copy_o(b, g, 3)

                def body(b, first):
                    act.wait_ge(s_rc, b * 3 + 3)
                    for g in range(NG):
                        copy_rows(b, g * GC)
                        for i in range(GC):
                            if i + 1 < GC:
                                copy_rows(b, g * GC + i + 1)
                            copy_columns(b, g * GC + i)
                            if i == 1 and g:
                                trigonometry(b, g - 1)
                            elif i == 1 and not first:
                                trigonometry(b - 1, NG - 1)
                        magnitudes(b, g)
                        if g >= LAG:
                            inverse_copies(b, g - LAG, lambda: arctangent(b, g))
                        elif not first:
                            inverse_copies(b - 1, g - LAG + NG, lambda: arctangent(b, g))
                        else:
                            arctangent(b, g)

                for_images(act, body)
                inverse_copies(B - 1, NG - 2, lambda: trigonometry(B - 1, NG - 1))
                inverse_copies(B - 1, NG - 1, lambda: None)
                act.wait_ge(s_store, B * 16 + 16)

            @block.vector
            def _(dve):
                dve.sem_inc(s_ri, 1)
                dve.wait_ge(s_const, 16 * (12 + B))
                nc.vector.memset(one[:, :], 1.0).then_inc(s_init, 1)
                nc.vector.memset(mr[:, B, :, :], 0.0).then_inc(s_init, 1)
                nc.vector.memset(hpi[:, :], PI / 2).then_inc(s_init, 1)
                nc.vector.tensor_scalar(pw[:, :], pw[:, :], 2.0, None, ALU.mult).then_inc(s_init, 1)
                dve.wait_ge(s_init, 4)

                def scales(b):
                    nc.vector.tensor_copy(rc[:, :], mr[:, bass.ds(b, 1), 1, :].rearrange("p a c -> p (a c)")).then_inc(s_rc, 1)
                    nc.vector.tensor_copy(dc[:, :], mr[0:1, bass.ds(b, 1), 0, :].rearrange("p a c -> p (a c)")).then_inc(s_rc, 1)
                    dve.wait_ge(s_rc, b * 3 + 2)
                    nc.vector.scalar_tensor_tensor(dc[:, :], dc[:, :], -float(PIX), rc[0:1, :], ALU.mult, ALU.mult).then_inc(s_rc, 1)

                scales(0)
                with dve.Fori(0, B) as b:
                    dve.wait_ge(s_rc, b * 3 + 3)
                    re, im = ri[:, :, 0, :], ri[:, :, 1, :]
                    t0, t1, t2, t3, t4 = (q[:, :, :] for q in t)
                    for g in range(NG):
                        ch = Chain(dve, s_ch, b * (NG * NS) + g * NS)
                        dve.wait_ge(s_xe, b * 64 + ((g + 1) * SL + 2))
                        zero = ri[0:1, 0:SL:2, 0, 0]
                        nc.vector.tensor_tensor(zero, zero, dc[:, g * GC:(g + 1) * GC], ALU.add).then_inc(s_dc, 1)
                        if g == NG - 1:
                            dve.wait_ge(s_dc, b * NG + NG)
                            scales(b + 1)
                        dve.wait_ge(s_abs, b * (2 * NG) + (2 * g + 2))
                        ch.step(nc.vector.scalar_tensor_tensor(t2, t0, TINY, t1, ALU.max, ALU.max))
                        ch.step(nc.vector.reciprocal(t4, t2))
                        ch.step(nc.vector.tensor_tensor(t3, t0, t1, ALU.min))
                        ch.step(nc.vector.tensor_tensor(t0, t1, t0, ALU.is_gt))
                        nc.vector.tensor_tensor(t3, t3, t4, ALU.mult).then_inc(s_ratio, 1)
                        dve.wait_ge(s_atan, b * (2 * NG) + (2 * g + 1))
                        ch.step(nc.vector.scalar_tensor_tensor(t0, t0, PI / 2, t4, ALU.mult, ALU.subtract))
                        ch.step(nc.vector.tensor_scalar(t4, re, 0.0, PI, ALU.is_lt, ALU.mult))
                        ch.step(nc.vector.scalar_tensor_tensor(t0, t0, -1.0, t0, ALU.mult, ALU.max))
                        ch.step(nc.vector.tensor_tensor(t0, t0, t4, ALU.subtract))
                        ch.step(nc.vector.scalar_tensor_tensor(t0, t0, -1.0, t0, ALU.mult, ALU.max))
                        ch.step(nc.vector.tensor_scalar(t4, im, 0.0, 0.5, ALU.is_ge, ALU.subtract))
                        nc.vector.tensor_tensor(t0, t0, t4, ALU.mult).then_inc(s_ri, 1)
                        dve.wait_ge(s_ri, b * NG + (g + 2))
                        for i in range(GC):
                            c, v = g * GC + i, t[0][:, 2 * i:2 * i + 2, :]
                            last = nc.vector.tensor_scalar(v, v, pw[:, c:c + 1], pb_[:, c:c + 1], ALU.mult, ALU.add)
                        ch.step(last)
                        ch.step(nc.vector.tensor_scalar(t4, t0, 0.5 / PI, ROUND, ALU.mult, ALU.add))
                        ch.step(nc.vector.tensor_scalar(t4, t4, ROUND, -2 * PI, ALU.subtract, ALU.mult))
                        ch.step(nc.vector.tensor_tensor(t0, t0, t4, ALU.add))
                        dve.wait_ge(s_atan, b * (2 * NG) + (2 * g + 2))
                        ch.step(nc.vector.tensor_tensor(t2, t2, t1, ALU.mult))
                        nc.vector.tensor_scalar(t0, t0, CLAMP, -CLAMP, ALU.min, ALU.max).then_inc(s_phase, 1)
                        for i in range(GC):
                            c, v = g * GC + i, t[2][:, 2 * i:2 * i + 2, :]
                            last = nc.vector.tensor_scalar(v, v, aw[:, c:c + 1], ab[:, c:c + 1], ALU.mult, ALU.add)
                        ch.step(last)
                        assert ch.n == NS
                        dve.wait_ge(s_trig, b * (2 * NG) + (2 * g + 1))
                        nc.vector.tensor_tensor(t1, t1, t2, ALU.mult).then_inc(s_prod, 1)
                        dve.wait_ge(s_trig, b * (2 * NG) + (2 * g + 2))
                        nc.vector.tensor_tensor(t3, t3, t2, ALU.mult).then_inc(s_prod, 1)

            @block.gpsimd
            def _(pool):
                pool.sem_inc(s_z, 1)

                def body(b, first):
                    for g in range(NG):
                        if g >= LAG or not first:
                            pool.wait_ge(s_u, b * 32 + (g - LAG + 1) * GC)
                        pool.wait_ge(s_prod, b * (2 * NG) + (2 * g + 1))
                        pool.sem_inc(s_pool, 1)
                        K = NF - 1
                        nc.gpsimd.tensor_scalar(zi[:, g % 2, :, 0:K], t[1][:, :, 0:K], 1e-8, None, ALU.add)
                        nc.gpsimd.tensor_scalar(zr[:, g % 2, :, K:NF], t[1][:, :, K:NF], 1e-8, -1.0, ALU.add, ALU.mult)
                        pool.wait_ge(s_prod, b * (2 * NG) + (2 * g + 2))
                        pool.sem_inc(s_pool, 1)
                        nc.gpsimd.tensor_scalar(zi[:, g % 2, :, K:NF], t[3][:, :, K:NF], 1e-8, 1e-8, ALU.add, ALU.add)
                        nc.gpsimd.tensor_scalar(zr[:, g % 2, :, 0:K], t[3][:, :, 0:K], 1e-8, 1e-8, ALU.add, ALU.add).then_inc(s_z, 1)

                for_images(pool, body)


def project(nc, B, ol, og, x1l, x1g, proj_t, proj_b, eye, x2):
    NT = B * 2
    NB = NWIN // 8
    with ExitStack() as ctx:
        m = Mem(nc, ctx, "pj")
        xl, xg = m.sb("xl", [P, 4, NWIN, HALF]), m.sb("xg", [P, 4, NWIN, HALF])
        a = [m.sb(n, [P, 4, NWIN * HALF]) for n in ("al", "ag")]
        at = m.sb("at", [P, 2, 2, 512])
        o = m.sb("o", [P, 2, NWIN, 2, C])
        pw = m.sb("pw", [P, 2, 4, C])
        pb_ = m.sb("pb", [P, C])
        idn = m.sb("idn", [P, P])
        tp = [[m.ps(f"tp{i}{s}", [P, 512]) for s in range(2)] for i in range(2)]
        pp = [m.ps(f"pp{i}", [P, 2, 4, C]) for i in range(4)]
        s_zero, s_const = m.sem("zero"), m.sem("const")
        s_in = [m.sem(f"in{j}") for j in range(4)]
        s_t, s_te, s_p, s_bias, s_add = m.sem("t"), m.sem("te"), m.sem("p"), m.sem("bias"), m.sem("add")
        s_store = [m.sem(f"store{j}") for j in range(2)]
        views = [v.rearrange("b (r p) u n c -> (b r) p u (n c)", p=P) for v in (x1l, x1g, ol, og)]
        x2v = x2.rearrange("b (r p) (n v k) c -> (b r) p v n (k c)", p=P, n=NWIN, k=2)
        with nc.Block() as block:

            @block.sync
            def _(sp):
                sp.dma_start(idn[:, :], eye).then_inc(s_const, 16)
                sp.dma_start(pb_[:, :], spread(proj_b, [[1, C]])).then_inc(s_const, 16)
                sp.wait_ge(s_zero, 1)
                for w in range(4):
                    for s in range(2):
                        sp.dma_start(pw[w * HALF:(w + 1) * HALF, s, w, :], proj_t[s * HALF:(s + 1) * HALF, :]).then_inc(s_const, 16)
                for j in range(2):
                    sp.sem_inc(s_store[j], 16)

                def store(t, v):
                    dst = x2v[t:t + 1] if isinstance(t, int) else x2v[bass.ds(t, 1)]
                    sp.dma_start(dst[:, :, v, :, :].rearrange("a p n c -> (a p) n c"),
                                 o[:, v % 2].rearrange("p n k c -> p n (k c)")).then_inc(s_store[v % 2], 16)

                def body(t, first):
                    for u in range(WIN):
                        j = u % 4
                        sp.wait_ge(s_add, t * (2 * WIN) + (2 * u + 2))
                        if u % 2 and u > 4:
                            store(t, u // 2 - 2)
                        elif u % 2 and not first:
                            store(t - 1, u // 2 + 2)
                        for dst, v in zip((xl[:, j].rearrange("p n c -> p (n c)"), xg[:, j].rearrange("p n c -> p (n c)"),
                                           a[0][:, j], a[1][:, j]), views):
                            src = v[t:t + 1] if isinstance(t, int) else v[bass.ds(t, 1)]
                            sp.dma_start(dst, src[:, :, u, :].rearrange("a p n -> (a p) n")).then_inc(s_in[j], 16)

                body(0, True)
                with sp.Fori(1, NT) as t:
                    body(t, False)
                for v in range(2, 4):
                    sp.wait_ge(s_add, NT * 2 * WIN + 4 * v - 4)
                    store(NT - 1, v)
                for j in range(2):
                    sp.wait_ge(s_store[j], NT * 32 + 16)

            @block.tensor
            def _(pe):
                def transposes(t, u, q):
                    if q == 0:
                        pe.wait_ge(s_in[u % 4], t * 128 + ((u // 4) * 64 + 64))
                    pe.wait_ge(s_te, t * (2 * WIN) + (2 * u + q + 1))
                    for s in range(2):
                        for g in range(NB):
                            gg = q * NB + g
                            last = nc.tensor.transpose(tp[q][s][:, g * P:(g + 1) * P],
                                                       a[s][:, u % 4, gg * P:(gg + 1) * P], idn[:, :])
                    last.then_inc(s_t, 1)

                def products(t, u, q):
                    pe.wait_ge(s_te, t * (2 * WIN) + (2 * u + q + 3))
                    pe.wait_ge(s_add, t * (2 * WIN) + (2 * u + q + 7))
                    for g in range(NB):
                        gg = q * NB + g
                        for s in range(2):
                            last = nc.tensor.matmul(pp[gg // 2][:, gg % 2, :, :].rearrange("p w d -> p (w d)"),
                                                    at[:, q, s, g * P:(g + 1) * P],
                                                    pw[:, s, :, :].rearrange("p w d -> p (w d)"),
                                                    start=(s == 0), stop=(s == 1))
                    last.then_inc(s_p, 1)

                def body(t, last_round):
                    for u in range(WIN):
                        transposes(t, u, 1)
                        products(t, u, 0)
                        if u + 1 < WIN:
                            transposes(t, u + 1, 0)
                        elif not last_round:
                            transposes(t + 1, 0, 0)
                        products(t, u, 1)

                pe.wait_ge(s_const, 160)
                transposes(0, 0, 0)
                with pe.Fori(0, NT - 1) as t:
                    body(t, False)
                body(NT - 1, True)

            @block.scalar
            def _(act):
                act.sem_inc(s_te, 2)
                with act.Fori(0, NT) as t:
                    for k in range(2 * WIN):
                        act.wait_ge(s_t, t * (2 * WIN) + (k + 1))
                        for s in range(2):
                            last = nc.scalar.activation(at[:, k % 2, s, :], tp[k % 2][s][:, :], ACT.Copy)
                        last.then_inc(s_te, 1)

            @block.gpsimd
            def _(pool):
                with pool.Fori(0, NT) as t:
                    for u in range(WIN):
                        j = u % 4
                        pool.wait_ge(s_in[j], t * 128 + (u // 4) * 64 + 64)
                        for h, v in enumerate((xl, xg)):
                            bias = pb_[:, h * HALF:(h + 1) * HALF]
                            bb = bass.AP(bias.tensor, bias.offset, [bias.ap[0], [0, NWIN], bias.ap[1]])
                            last = nc.gpsimd.tensor_tensor(v[:, j], v[:, j], bb, ALU.add)
                        last.then_inc(s_bias, 1)

            @block.vector
            def _(dve):
                dve.sem_inc(s_add, 8)
                nc.vector.memset(pw[:, :, :, :].rearrange("p s w d -> p (s w d)"), 0.0).then_inc(s_zero, 1)
                with dve.Fori(0, NT) as t:
                    for u in range(WIN):
                        j, i = u % 4, u // 2 % 2
                        dve.wait_ge(s_bias, t * WIN + u + 1)
                        if u % 2 == 0:
                            dve.wait_ge(s_store[i], t * 32 + ((u // 4) * 16 + 16))
                        for q in range(2):
                            dve.wait_ge(s_p, t * (2 * WIN) + (2 * u + q + 1))
                            for k in range(2):
                                ns = slice(16 * k + q, 16 * k + q + 15, 2)
                                pv = pp[2 * q + k][:, :, :, :].rearrange("p a w d -> p (a w) d")
                                for h, v in enumerate((xl, xg)):
                                    ds = slice(h * HALF, (h + 1) * HALF)
                                    last = nc.vector.tensor_tensor(o[:, i, ns, u % 2, ds], pv[:, :, ds], v[:, j, ns, :], ALU.add)
                            last.then_inc(s_add, 1)


def mix_modes2(nc, B, modes, w_re, w_im, zd):
    NN = NM2 // 2
    S = w_re.shape[4]
    with ExitStack() as ctx:
        m = Mem(nc, ctx, "m2")
        a = m.sb("a", [P, 3, NN, B, NM2])
        w = m.sb("w", [P, 2, 2, NN, C * S])
        ws = m.sb("ws", [P, 2, 3, NN, C])
        o = m.sb("o", [B * NM2, NM2, 2, 2, C])
        op = [m.ps(f"op{i}", [B * NM2, 2, C]) for i in range(2)]
        s_const, s_ws, s_o, s_oe, s_store = m.sem("const"), m.sem("ws"), m.sem("o"), m.sem("oe"), m.sem("store")
        s_w = [m.sem(f"w{j}") for j in range(2)]
        with nc.Block() as block:

            @block.sync
            def _(sp):
                for par in range(2):
                    for b in range(B):
                        for q in range(3):
                            sp.dma_start(a[par * C:(par + 1) * C, q, :, b, :],
                                         modes[b, q].rearrange("c (r n k) -> r c n k", r=2, n=NN)[par]).then_inc(s_const, 16)
                with sp.Fori(0, NM2 // 2) as t:
                    for j in range(2):
                        sp.wait_ge(s_ws, t * 2 + j + 1)
                        for q, src in enumerate((w_re, w_im)):
                            sp.dma_start(w[:, j, q, :, :],
                                         src[bass.ds(t * 2 + j, 1)].rearrange("a (n r) c o s -> (r c) (a n) (o s)", r=2)).then_inc(s_w[j], 16)

            @block.vector
            def _(dve):
                dve.sem_inc(s_ws, 2)
                for n in range(NM2):
                    j = n % 2
                    dve.wait_ge(s_w[j], 32 * (n // 2 + 1))
                    if n >= 2:
                        dve.wait_ge(s_o, n - 1)
                    for q, src, neg in ((1, 0, False), (2, 1, False), (0, 1, True)):
                        last = nc.vector.tensor_reduce(ws[:, j, q, :, :].rearrange("p n o -> p (n o)"),
                                                       w[:, j, src, :, :].rearrange("p n (o s) -> p (n o) s", s=S),
                                                       axis=AX.X, op=ALU.add, negate=neg)
                    last.then_inc(s_ws, 1)

            @block.tensor
            def _(pe):
                pe.wait_ge(s_const, 16 * 6 * B)
                for n in range(NM2):
                    j = n % 2
                    pe.wait_ge(s_ws, n + 3)
                    if n >= 2:
                        pe.wait_ge(s_oe, n - 1)
                    for k in range(2 * NN):
                        i, q = k // 2, k % 2
                        last = nc.tensor.matmul(op[j][:, :, :], a[:, 1 + q, i, :, :].rearrange("p b k -> p (b k)"),
                                                ws[:, j, 1 - q:3 - q, i, :], start=(k == 0), stop=(k == 2 * NN - 1))
                    last.then_inc(s_o, 1)

            @block.scalar
            def _(act):
                for n in range(NM2):
                    j = n % 2
                    act.wait_ge(s_o, n + 1)
                    nc.scalar.activation(o[:, n, 0, :, :], op[j][:, :, :], ACT.Copy)
                    nc.scalar.activation(o[:, n, 1, 0, :], op[j][:, 1, :], ACT.Copy, scale=-1.0)
                    nc.scalar.activation(o[:, n, 1, 1, :], op[j][:, 0, :], ACT.Copy).then_inc(s_oe, 1)
                act.wait_ge(s_oe, NM2)
                for b in range(B):
                    for r in range(2):
                        act.dma_start(zd[b, r * NM2:(r + 1) * NM2].rearrange("m k q o -> k m (q o)"),
                                      o[b * NM2:(b + 1) * NM2, :, r].rearrange("k m q o -> k m (q o)")).then_inc(s_store, 16)
                act.wait_ge(s_store, 32 * B)


def point_rows(nc, B, x3, stats, eye, ft):
    NT = NPTS // P
    with ExitStack() as ctx:
        m = Mem(nc, ctx, "pr")
        x = m.sb("x", [P, 2, 2, NPTS])
        f = m.sb("f", [P, 2, NT, H])
        mr = m.sb("mr", [P, B, 2])
        sh = m.sb("sh", [P, B])
        idn = m.sb("idn", [P, P])
        tp = [m.ps(f"tp{i}", [P, 2, H]) for i in range(4)]
        s_const, s_sh, s_t, s_te = m.sem("const"), m.sem("sh"), m.sem("t"), m.sem("te")
        s_x = [m.sem(f"x{j}") for j in range(2)]
        s_store = [m.sem(f"store{j}") for j in range(2)]
        with nc.Block() as block:

            @block.sync
            def _(sp):
                sp.dma_start(idn[:, :], eye).then_inc(s_const, 16)
                for half in range(2):
                    for q in range(2):
                        sp.dma_start(mr[half * C:(half + 1) * C, :, q:q + 1],
                                     stats[:, q, :].rearrange("b (c a) -> c b a", a=1),
                                     allow_slow_non_contiguous=True).then_inc(s_const, 16)
                for b in range(B):
                    if b >= 2:
                        sp.wait_ge(s_t, (b - 1) * (NT // 2))
                    sp.dma_start(x[:, b % 2, :, :],
                                 x3[b, :, 0:NPTS // C, :].rearrange("(r p) w c -> p r (w c)", p=P)).then_inc(s_x[b % 2], 16)

            @block.tensor
            def _(pe):
                pe.wait_ge(s_const, 80)
                for b in range(B):
                    pe.wait_ge(s_x[b % 2], 16 * (b // 2 + 1))
                    for k in range(NT // 2):
                        n = b * (NT // 2) + k
                        if n >= 4:
                            pe.wait_ge(s_te, n - 3)
                        for i in range(2):
                            for r in range(2):
                                last = nc.tensor.transpose(tp[n % 4][:, i, r * P:(r + 1) * P],
                                                           x[:, b % 2, r, (2 * k + i) * P:(2 * k + i + 1) * P], idn[:, :])
                        last.then_inc(s_t, 1)

            @block.vector
            def _(dve):
                dve.wait_ge(s_const, 80)
                nc.vector.scalar_tensor_tensor(sh[:, :], mr[:, :, 0], -1.0, mr[:, :, 1], ALU.mult, ALU.mult).then_inc(s_sh, 1)

            @block.scalar
            def _(act):
                act.wait_ge(s_sh, 1)
                for b in range(B):
                    if b >= 2:
                        act.wait_ge(s_store[b % 2], 16 * (b // 2))
                    for k in range(NT // 2):
                        n = b * (NT // 2) + k
                        act.wait_ge(s_t, n + 1)
                        nc.scalar.activation(f[:, b % 2, 2 * k:2 * k + 2, :], tp[n % 4][:, :, :], ACT.Identity,
                                             bias=sh[:, b:b + 1], scale=mr[:, b, 1:2]).then_inc(s_te, 1)
                    act.wait_ge(s_te, (b + 1) * (NT // 2))
                    act.dma_start(ft[b].rearrange("(t p) h -> p t h", p=P), f[:, b % 2, :, :]).then_inc(s_store[b % 2], 16)
                for j in range(min(B, 2)):
                    act.wait_ge(s_store[j], 16 * ((B + 1 - j) // 2))


def select_points(nc, B, ft, mask_idx, ctx_idx, eye, cx, mn, mb, mx):
    TM, TC = NMASK // P, NCTX // P
    NT = TM + TC
    KC = 8
    NCH = NCTX // 512
    SQ = TM - 6
    with ExitStack() as ctx:
        m = Mem(nc, ctx, "sp")
        rows = m.sb("rows", [P, 2, NT, H])
        nrm = m.sb("nrm", [P, 2, NT, H])
        tc = m.sb("tc", [P, 2, NT * P])
        junk = m.sb("junk", [P, H])
        ss, rn = m.sb("ss", [P, NT]), m.sb("rn", [P, NT])
        cos = m.sb("cos", [P, 2, NCTX])
        best = m.sb("best", [P, TM, H])
        top, topi = m.sb("top", [P, TM, 8]), m.sb("topi", [P, TM, 8], U32)
        mxo = m.sb("mxo", [P, TM])
        idx0, idx = m.sb("idx0", [P, NT], I32), m.sb("idx", [P, NT], I32)
        idxf, bf, bi = m.sb("idxf", [P, NT]), m.sb("bf", [P, TM]), m.sb("bi", [P, TM], I32)
        idn = m.sb("idn", [P, P])
        tp = [m.ps(f"tp{i}", [P, 2, 2, P]) for i in range(2)]
        cp = [m.ps(f"cp{i}", [P, 512]) for i in range(4)]
        s_const, s_idx = m.sem("const"), m.sem("idx")
        s_g = [[m.sem(f"g{j}_{k}") for k in range(NT // KC)] for j in range(2)]
        s_cx, s_mb = m.sem("cx"), m.sem("mb")
        s_mn = [m.sem(f"mn{j}") for j in range(2)]
        s_sq, s_root, s_rn, s_nrm = m.sem("sq"), m.sem("root"), m.sem("rn"), m.sem("nrm")
        s_t, s_te, s_c, s_ce = m.sem("t"), m.sem("te"), m.sem("c"), m.sem("ce")
        s_top, s_bi, s_ch, s_g2, s_mbs = m.sem("top"), m.sem("bi"), m.sem("ch"), m.sem("g2"), m.sem("mbs")
        ftf = ft.rearrange("b n h -> (b n) h")
        with nc.Block() as block:

            @block.sync
            def _(sp):
                sp.dma_start(idn[:, :], eye).then_inc(s_const, 16)
                sp.dma_start(idx0[:, 0:TM], mask_idx.rearrange("(t p) -> p t", p=P), allow_slow_non_contiguous=True).then_inc(s_const, 16)
                sp.dma_start(idx0[:, TM:NT], ctx_idx.rearrange("(t p) -> p t", p=P), allow_slow_non_contiguous=True).then_inc(s_const, 16)
                for b in range(B):
                    for k in range(TM // KC, NT // KC):
                        sp.wait_ge(s_g[b % 2][k], 16 * KC * (b // 2 + 1))
                    sp.dma_start(cx[b].rearrange("(t p) h -> p t h", p=P), rows[:, b % 2, TM:NT, :]).then_inc(s_cx, 16)
                    sp.wait_ge(s_nrm, b + 1)
                    sp.dma_start(mn[b].rearrange("(t p) h -> p t h", p=P), nrm[:, b % 2, 0:TM, :]).then_inc(s_mn[b % 2], 16)
                    sp.wait_ge(s_mbs, b + 1)
                    sp.dma_start(mb[b].rearrange("(t p) h -> p t h", p=P), best[:, :, :]).then_inc(s_mb, 16)
                    sp.dma_start(mx[b].rearrange("(t p) -> p t", p=P), mxo[:, :],
                                 allow_slow_non_contiguous=True).then_inc(s_mb, 16)
                sp.wait_ge(s_cx, 16 * B)
                for j in range(min(B, 2)):
                    sp.wait_ge(s_mn[j], 16 * len(range(j, B, 2)))
                sp.wait_ge(s_mb, 32 * B)

            @block.gpsimd
            def _(pool):
                def gather_rows(b):
                    if b >= 2:
                        pool.wait_ge(s_cx, 16 * (b - 1))
                        pool.wait_ge(s_nrm, b - 1)
                    pool.wait_ge(s_idx, b + 1)
                    for i in range(NT):
                        pool.indirect_dma_start(rows[:, b % 2, i, :], None, ftf,
                                                bass.IndirectOffsetOnAxis(ap=idx[:, i:i + 1], axis=0)).then_inc(s_g[b % 2][i // KC], 16)

                gather_rows(0)
                for b in range(B):
                    if b + 1 < B:
                        gather_rows(b + 1)
                    pool.wait_ge(s_bi, b + 1)
                    pool.wait_ge(s_cx, 16 * (b + 1))
                    if b:
                        pool.wait_ge(s_mb, 32 * b)
                    for i in range(TM):
                        pool.indirect_dma_start(best[:, i, :], None, cx[b],
                                                bass.IndirectOffsetOnAxis(ap=bi[:, i:i + 1], axis=0)).then_inc(s_g2, 16)

            @block.scalar
            def _(act):
                def squares(b, tiles):
                    for i in tiles:
                        if i % KC == 0:
                            act.wait_ge(s_g[b % 2][i // KC], 16 * KC * (b // 2 + 1))
                        nc.scalar.activation(junk[:, :], rows[:, b % 2, i, :], ACT.Square,
                                             accum_out=ss[:, i:i + 1]).then_inc(s_sq, 1)
                        act.wait_ge(s_sq, b * NT + i + 1)
                    if i == NT - 1:
                        nc.scalar.activation(rn[:, :], ss[:, :], ACT.Sqrt).then_inc(s_root, 1)

                def normalise(b, tiles):
                    for i in tiles:
                        if i == 0:
                            act.wait_ge(s_rn, b + 1)
                            if b >= 2:
                                act.wait_ge(s_mn[b % 2], 16 * (b // 2))
                        last = nc.scalar.activation(nrm[:, b % 2, i, :], rows[:, b % 2, i, :], ACT.Copy, scale=rn[:, i:i + 1])
                    if i == NT - 1:
                        last.then_inc(s_nrm, 1)

                def scale_best(b):
                    act.wait_ge(s_g2, 16 * TM * (b + 1))
                    act.wait_ge(s_bi, b + 1)
                    for i in range(TM):
                        last = nc.scalar.activation(best[:, i, :], best[:, i, :], ACT.Copy, scale=mxo[:, i:i + 1])
                    last.then_inc(s_mbs, 1)

                thirds = (range(0, 11), range(11, 22), range(22, NT))
                squares(0, range(NT))
                normalise(0, range(NT))
                for b in range(B):
                    for i in range(TM):
                        for k in range(NCH):
                            n = (b * TM + i) * NCH + k
                            act.wait_ge(s_c, n + 1)
                            if k == 0 and b * TM + i >= 2:
                                act.wait_ge(s_top, b * TM + i - 1)
                            nc.scalar.activation(cos[:, i % 2, k * 512:(k + 1) * 512], cp[n % 4][:, :], ACT.Copy).then_inc(s_ce, 1)
                        if i == 1 and b:
                            scale_best(b - 1)
                        if b + 1 < B and SQ <= i < SQ + 3:
                            squares(b + 1, thirds[i - SQ])
                        elif b + 1 < B and i >= SQ + 3:
                            normalise(b + 1, thirds[i - SQ - 3])
                scale_best(B - 1)

            @block.tensor
            def _(pe):
                pe.wait_ge(s_const, 48)
                for b in range(B):
                    pe.wait_ge(s_nrm, b + 1)
                    for i in range(NT // 2):
                        n = b * (NT // 2) + i
                        if n >= 2:
                            pe.wait_ge(s_te, n - 1)
                        for q in range(2):
                            for r in range(2):
                                last = nc.tensor.transpose(tp[n % 2][:, q, r, :], nrm[:, b % 2, 2 * i + q, r * P:(r + 1) * P], idn[:, :])
                        last.then_inc(s_t, 1)
                    pe.wait_ge(s_te, (b + 1) * (NT // 2))
                    for i in range(TM):
                        for k in range(NCH):
                            n = (b * TM + i) * NCH + k
                            if n >= 4:
                                pe.wait_ge(s_ce, n - 3)
                            for r in range(2):
                                c0 = TM * P + k * 512
                                last = nc.tensor.matmul(cp[n % 4][:, :], tc[:, r, i * P:(i + 1) * P], tc[:, r, c0:c0 + 512],
                                                        start=(r == 0), stop=(r == 1))
                            last.then_inc(s_c, 1)

            @block.vector
            def _(dve):
                ch = Chain(dve, s_ch)
                dve.wait_ge(s_const, 48)
                ch.step(nc.vector.tensor_copy(idxf[:, :], idx0[:, :]))
                nc.vector.tensor_copy(idx[:, :], idxf[:, :]).then_inc(s_idx, 1)

                def norms(b):
                    dve.wait_ge(s_root, b + 1)
                    ch.step(nc.vector.tensor_scalar(rn[:, :], rn[:, :], CSA_EPS, None, ALU.add))
                    nc.vector.reciprocal(rn[:, :], rn[:, :]).then_inc(s_rn, 1)
                    if b + 1 < B:
                        ch.step(nc.vector.tensor_scalar(idxf[:, :], idxf[:, :], float(NPTS), None, ALU.add))
                        nc.vector.tensor_copy(idx[:, :], idxf[:, :]).then_inc(s_idx, 1)

                norms(0)
                for b in range(B):
                    for i in range(NT // 2):
                        n = b * (NT // 2) + i
                        dve.wait_ge(s_t, n + 1)
                        nc.vector.tensor_copy(tc[:, :, 2 * i * P:(2 * i + 2) * P].rearrange("p r (q n) -> p q r n", q=2),
                                              tp[n % 2][:, :, :, :]).then_inc(s_te, 1)
                    for i in range(TM):
                        n = b * TM + i
                        dve.wait_ge(s_ce, (n + 1) * NCH)
                        ch.step(nc.vector.max(top[:, i, :], cos[:, i % 2, :]))
                        nc.vector.max_index(topi[:, i, :], top[:, i, :], cos[:, i % 2, :]).then_inc(s_top, 1)
                        if i == SQ + 2 and b + 1 < B:
                            norms(b + 1)
                    dve.wait_ge(s_top, (b + 1) * TM)
                    if b:
                        dve.wait_ge(s_mb, 32 * b)
                        dve.wait_ge(s_g2, 16 * TM * b)
                    ch.step(nc.vector.tensor_copy(bf[:, :], topi[:, :, 0]))
                    nc.vector.tensor_copy(mxo[:, :], top[:, :, 0])
                    nc.vector.tensor_copy(bi[:, :], bf[:, :]).then_inc(s_bi, 1)


def coherent_scan(nc, B, x3, stats, mn, mb, mx, gen, out):
    K = 16
    NL = NMASK // K
    W0 = NPTS // C
    WC = 32
    NPC = (W - W0) // WC
    CH = WC * C
    with ExitStack() as ctx:
        m = Mem(nc, ctx, "cs")
        mnt, mbt = m.sb("mnt", [B, 2, K, H]), m.sb("mbt", [B, 2, K, H])
        mxt, mxe = m.sb("mxt", [B, 2, K]), m.sb("mxe", [B, 2, K])
        rs = m.sb("rs", [B, 2])
        go = m.sb("go", [B, 2, K, H])
        num = m.sb("num", [B, 2, H])
        junk, junk2 = m.sb("junk", [B, H]), m.sb("junk2", [B, H])
        sm = m.sb("sm", [B, 2, 10])
        tiny = m.sb("tiny", [B, 1])
        xt = m.sb("xt", [P, 4, CH])
        mr = m.sb("mr", [P, B, 2, C])
        s1, s0 = m.sb("s1", [P, WC, C]), m.sb("s0", [P, WC, C])
        s_const, s_init, s_mxe = m.sem("const"), m.sem("init"), m.sem("mxe")
        s_in = [m.sem(f"in{j}") for j in range(2)]
        s_num, s_ss, s_root, s_ch, s_rs = m.sem("num"), m.sem("ss"), m.sem("root"), m.sem("ch"), m.sem("rs")
        s_cur = m.sem("cur")
        s_store = [m.sem(f"store{j}") for j in range(2)]
        s_x = [m.sem(f"x{j}") for j in range(4)]
        s_sc, s_mul, s_out = m.sem("sc"), m.sem("mul"), m.sem("out")
        s_xs = [m.sem(f"xs{j}") for j in range(4)]
        NCHAIN = 8
        with nc.Block() as block:

            @block.sync
            def _(sp):
                sp.dma_start(mr[:, :, :, :].rearrange("p b q c -> p (b q c)"), spread(stats, [[1, B * 2 * C]])).then_inc(s_const, 16)
                with sp.Fori(0, B * 2) as t:
                    for i in range(NPC):
                        j = i % 4
                        cols = slice(W0 + i * WC, W0 + (i + 1) * WC)
                        sp.wait_ge(s_xs[j], t * 16 * len(range(j, NPC, 4)) + 16 * (i // 4) + 16)
                        sp.dma_start(xt[:, j, :], x3.rearrange("b (r p) w c -> (b r) p w c", p=P)[bass.ds(t, 1), :, cols, :]
                                     .rearrange("a p w c -> (a p) (w c)")).then_inc(s_x[j], 16)
                        pi, pj = (i - 1) % NPC, (i - 1) % NPC % 4
                        if i:
                            sp.wait_ge(s_out, t * NPC + i)
                            sp.dma_start(out.rearrange("b (r p) w c -> (b r) p w c", p=P)[bass.ds(t, 1), :, W0 + pi * WC:W0 + (pi + 1) * WC, :]
                                         .rearrange("a p w c -> (a p) (w c)"), xt[:, pj, :]).then_inc(s_xs[pj], 16)
                    sp.wait_ge(s_out, t * NPC + NPC)
                    sp.dma_start(out.rearrange("b (r p) w c -> (b r) p w c", p=P)[bass.ds(t, 1), :, W - WC:W, :]
                                 .rearrange("a p w c -> (a p) (w c)"), xt[:, (NPC - 1) % 4, :]).then_inc(s_xs[(NPC - 1) % 4], 16)
                for j in range(4):
                    sp.wait_ge(s_xs[j], B * 2 * 16 * len(range(j, NPC, 4)) + 16)

            @block.gpsimd
            def _(pool):
                for j in range(4):
                    pool.sem_inc(s_xs[j], 16)
                pool.wait_ge(s_const, 16)
                for b in range(B):
                    r, mean = mr[:, b, 1, :], mr[:, b, 0, :]
                    rb = bass.AP(r.tensor, r.offset, [r.ap[0], [0, WC], r.ap[1]])
                    mb_ = bass.AP(mean.tensor, mean.offset, [mean.ap[0], [0, WC], mean.ap[1]])
                    if b:
                        pool.wait_ge(s_out, b * 2 * NPC)
                    nc.gpsimd.tensor_scalar(s1[:, :, :], rb, 1.0, None, ALU.add)
                    nc.gpsimd.tensor_tensor(s0[:, :, :], rb, mb_, ALU.mult).then_inc(s_sc, 1)
                    pool.wait_ge(s_sc, b + 1)
                    for r_ in range(2):
                        for i in range(NPC):
                            n = (b * 2 + r_) * NPC + i
                            j = i % 4
                            pool.wait_ge(s_x[j], 16 * ((b * 2 + r_) * len(range(j, NPC, 4)) + i // 4 + 1))
                            v = xt[:, j, :]
                            nc.gpsimd.tensor_tensor(v, v, s1[:, :, :].rearrange("p w c -> p (w c)"), ALU.mult).then_inc(s_mul, 1)
                            pool.wait_ge(s_mul, n + 1)
                            nc.gpsimd.tensor_tensor(v, v, s0[:, :, :].rearrange("p w c -> p (w c)"), ALU.subtract).then_inc(s_out, 1)

            @block.scalar
            def _(act):
                def load(n, j):
                    for t_, src in ((mnt, mn), (mbt, mb)):
                        v = src.rearrange("b (n k) h -> b n (k h)", k=K)[:, bass.ds(n, 1), :].rearrange("b a n -> b (a n)")
                        act.dma_start(t_[:, j, :, :].rearrange("b k h -> b (k h)"), v).then_inc(s_in[j], 16)
                    act.dma_start(mxt[:, j, :], mx.rearrange("b (n k) -> b n k", k=K)[:, bass.ds(n, 1), :]
                                  .rearrange("b a k -> b (a k)")).then_inc(s_in[j], 16)

                for j in range(2):
                    load(j, j)
                    act.sem_inc(s_store[j], 16)
                act.sem_inc(s_cur, 2)
                act.wait_ge(s_init, 3)

                def batch(n, j, more):
                    def current(k):
                        act.wait_ge(s_rs, n * K + (k + 1))
                        i = (k + 1) % 2
                        nc.scalar.activation(go[:, j, k, :], num[:, i, :], ACT.Copy, scale=rs[:, i:i + 1]).then_inc(s_cur, 1)

                    act.wait_ge(s_store[j], (n - j) * 8 + 16)
                    for k in range(K):
                        act.wait_ge(s_num, n * K + (k + 1))
                        i = k % 2
                        nc.scalar.activation(junk2[:, :], num[:, i, :], ACT.Square, accum_out=sm[:, i, 0:1]).then_inc(s_ss, 1)
                        act.wait_ge(s_ss, n * K + (k + 1))
                        nc.scalar.activation(sm[:, i, 1:2], sm[:, i, 0:1], ACT.Sqrt, bias=tiny[:, 0:1]).then_inc(s_root, 1)
                        if k:
                            current(k - 1)
                    current(K - 1)
                    act.wait_ge(s_cur, n * K + (K + 2))
                    dst = gen.rearrange("b (n k) h -> b n (k h)", k=K)[:, bass.ds(n, 1), :].rearrange("b a n -> b (a n)")
                    act.dma_start(dst, go[:, j, :, :].rearrange("b k h -> b (k h)")).then_inc(s_store[j], 16)
                    if more:
                        load(n + 2, j)

                with act.Fori(0, NL // 2 - 1) as t:
                    for j in range(2):
                        batch(t * 2 + j, j, True)
                for j in range(2):
                    batch(NL - 2 + j, j, False)
                for j in range(2):
                    act.wait_ge(s_store[j], (NL // 2) * 16 + 16)

            @block.vector
            def _(dve):
                nc.vector.memset(tiny[:, :], 1e-30).then_inc(s_init, 1)
                nc.vector.memset(num[:, 0, :], 0.0).then_inc(s_init, 1)
                nc.vector.memset(rs[:, 0:1], 1.0).then_inc(s_init, 1)
                dve.wait_ge(s_init, 3)
                dve.sem_inc(s_num, 1)
                with dve.Fori(0, NL // 2) as t:
                    for j in range(2):
                        n = t * 2 + j
                        dve.wait_ge(s_in[j], t * 48 + 48)
                        nc.vector.tensor_scalar(mxe[:, j, :], mxt[:, j, :], CSA_EPS, None, ALU.add).then_inc(s_mxe, 1)
                        dve.wait_ge(s_mxe, n + 1)
                        for k in range(K):
                            i, o = k % 2, (k + 1) % 2
                            a, r = sm[:, i, :], rs[:, i:i + 1]
                            step = n * K + k
                            c = step * NCHAIN
                            dot, root, length, inverse = a[:, 2:3], a[:, 1:2], a[:, 3:4], a[:, 4:5]
                            e1, e2, d, den, ar = a[:, 5:6], a[:, 8:9], a[:, 6:7], a[:, 7:8], a[:, 9:10]
                            nc.vector.tensor_tensor_reduce(out=junk[:, :], in0=mnt[:, j, k, :], in1=num[:, i, :], scale=1.0,
                                                           scalar=0.0, op0=ALU.mult, op1=ALU.add, accum_out=dot).then_inc(s_ch, 1)
                            if k:
                                dve.wait_ge(s_rs, step)
                            nc.vector.tensor_scalar(ar, r, -1.0, r, ALU.mult, ALU.max).then_inc(s_ch, 1)
                            dve.wait_ge(s_ch, c + 1)
                            nc.vector.tensor_scalar(e1, dot, r, 0.0, ALU.mult, ALU.max).then_inc(s_ch, 1)
                            dve.wait_ge(s_ch, c + 2)
                            dve.wait_ge(s_root, step + 1)
                            nc.vector.tensor_scalar(length, root, ar, CSA_EPS, ALU.mult, ALU.add).then_inc(s_ch, 1)
                            dve.wait_ge(s_ch, c + 3)
                            nc.vector.tensor_scalar(e2, e1, r, None, ALU.mult).then_inc(s_ch, 1)
                            dve.wait_ge(s_ch, c + 4)
                            nc.vector.reciprocal(inverse, length).then_inc(s_ch, 1)
                            dve.wait_ge(s_ch, c + 6)
                            nc.vector.tensor_scalar(d, e2, inverse, None, ALU.mult).then_inc(s_ch, 1)
                            nc.vector.tensor_scalar(den, e1, inverse, mxe[:, j, k:k + 1], ALU.mult, ALU.add).then_inc(s_ch, 1)
                            dve.wait_ge(s_ch, c + 7)
                            dve.wait_ge(s_cur, step + 1)
                            nc.vector.scalar_tensor_tensor(num[:, o, :], num[:, i, :], d, mbt[:, j, k, :],
                                                           ALU.mult, ALU.add).then_inc(s_num, 1)
                            dve.wait_ge(s_ch, c + 8)
                            nc.vector.reciprocal(rs[:, o:o + 1], den).then_inc(s_rs, 1)
                            dve.wait_ge(s_num, step + 2)


def finish_points(nc, B, x3, ft, gen, mask_idx, eye, out):
    TM, NT = NMASK // P, NPTS // P
    with ExitStack() as ctx:
        m = Mem(nc, ctx, "fp")
        g = m.sb("g", [P, 2, TM, H])
        f = m.sb("f", [P, 2, NT, H])
        x = m.sb("x", [P, 2, 2, NPTS // 2])
        o = m.sb("o", [P, 2, 2, NPTS // 2])
        idx0, idx, idxf = m.sb("idx0", [P, TM], I32), m.sb("idx", [P, TM], I32), m.sb("idxf", [P, TM])
        idn = m.sb("idn", [P, P])
        tp = [m.ps(f"tp{i}", [P, 2, 2, P]) for i in range(4)]
        s_const, s_idx, s_ch = m.sem("const"), m.sem("idx"), m.sem("ch")
        s_g, s_f, s_x = ([m.sem(f"{n}{j}") for j in range(2)] for n in ("g", "f", "x"))
        s_sc, s_t, s_o = m.sem("sc"), m.sem("t"), m.sem("o")
        s_store = [m.sem(f"store{j}") for j in range(2)]
        ftf = ft.rearrange("b n h -> (b n) h")
        HT = NT // 2
        with nc.Block() as block:

            @block.sync
            def _(sp):
                sp.dma_start(idn[:, :], eye).then_inc(s_const, 16)
                sp.dma_start(idx0[:, :], mask_idx.rearrange("(t p) -> p t", p=P), allow_slow_non_contiguous=True).then_inc(s_const, 16)
                for b in range(B):
                    if b >= 2:
                        sp.wait_ge(s_sc, 16 * TM * (b - 1))
                    sp.dma_start(g[:, b % 2, :, :], gen[b].rearrange("(t p) h -> p t h", p=P)).then_inc(s_g[b % 2], 16)
                    sp.wait_ge(s_sc, 16 * TM * (b + 1))
                    if b >= 2:
                        sp.wait_ge(s_t, (b - 1) * HT)
                    sp.dma_start(f[:, b % 2, :, :], ft[b].rearrange("(t p) h -> p t h", p=P)).then_inc(s_f[b % 2], 16)
                    for q in range(2):
                        if b:
                            sp.wait_ge(s_o, ((b - 1) * 2 + q + 1) * (HT // 2))
                        c0 = q * (NPTS // C // 2)
                        sp.dma_start(x[:, q, :, :], x3[b, :, c0:c0 + NPTS // C // 2, :].rearrange("(r p) w c -> p r (w c)", p=P)).then_inc(s_x[q], 16)

            @block.gpsimd
            def _(pool):
                for b in range(B):
                    pool.wait_ge(s_g[b % 2], 16 * (b // 2 + 1))
                    pool.wait_ge(s_idx, b + 1)
                    for i in range(TM):
                        pool.indirect_dma_start(ftf, bass.IndirectOffsetOnAxis(ap=idx[:, i:i + 1], axis=0),
                                                g[:, b % 2, i, :], None).then_inc(s_sc, 16)

            @block.tensor
            def _(pe):
                pe.wait_ge(s_const, 32)
                for b in range(B):
                    pe.wait_ge(s_f[b % 2], 16 * (b // 2 + 1))
                    for k in range(HT):
                        n = b * HT + k
                        if n >= 4:
                            pe.wait_ge(s_o, n - 3)
                        for r in range(2):
                            for i in range(2):
                                last = nc.tensor.transpose(tp[n % 4][:, r, i, :], f[:, b % 2, 2 * k + i, r * P:(r + 1) * P], idn[:, :])
                        last.then_inc(s_t, 1)

            @block.vector
            def _(dve):
                ch = Chain(dve, s_ch)
                dve.wait_ge(s_const, 32)
                ch.step(nc.vector.tensor_copy(idxf[:, :], idx0[:, :]))
                nc.vector.tensor_copy(idx[:, :], idxf[:, :]).then_inc(s_idx, 1)
                for b in range(B):
                    if b + 1 < B:
                        ch.step(nc.vector.tensor_scalar(idxf[:, :], idxf[:, :], float(NPTS), None, ALU.add))
                        dve.wait_ge(s_sc, 16 * TM * (b + 1))
                        nc.vector.tensor_copy(idx[:, :], idxf[:, :]).then_inc(s_idx, 1)
                    for k in range(HT):
                        n, q = b * HT + k, k // (HT // 2)
                        dve.wait_ge(s_t, n + 1)
                        if k % (HT // 2) == 0:
                            dve.wait_ge(s_x[q], 16 * (b + 1))
                            if b:
                                dve.wait_ge(s_store[q], 16 * b)
                        c0 = (k % (HT // 2)) * 2 * P
                        nc.vector.tensor_tensor(o[:, q, :, c0:c0 + 2 * P], tp[n % 4][:, :, :, :].rearrange("p r i n -> p r (i n)"),
                                                x[:, q, :, c0:c0 + 2 * P], ALU.add).then_inc(s_o, 1)

            @block.scalar
            def _(act):
                for b in range(B):
                    for q in range(2):
                        act.wait_ge(s_o, (b * 2 + q + 1) * (HT // 2))
                        c0 = q * (NPTS // C // 2)
                        act.dma_start(out[b, :, c0:c0 + NPTS // C // 2, :].rearrange("(r p) w c -> p r (w c)", p=P),
                                      o[:, q, :, :]).then_inc(s_store[q], 16)
                for q in range(2):
                    act.wait_ge(s_store[q], 16 * B)


def build(nc, ins, out):
    x = ins["x"]
    B = x.shape[0]

    def dram(name, shape):
        return nc.dram_tensor(name, shape, F32, kind="Internal").ap()

    modes0 = dram("modes0", (B, 3, C, NM0 * NM0))
    zd0 = dram("zd0", (B, 2 * NM0, 2 * NM0, 2, C))
    x1l, x1g = dram("x1l", (B, H, WIN, NWIN, HALF)), dram("x1g", (B, H, WIN, NWIN, HALF))
    ol, og = dram("ol", (B, H, WIN, NWIN, HALF)), dram("og", (B, H, WIN, NWIN, HALF))
    stats1, stats3 = dram("stats1", (B, 2, C)), dram("stats3", (B, 2, C))
    x2, x3 = dram("x2", (B, H, W, C)), dram("x3", (B, H, W, C))
    modes2 = dram("modes2", (B, 3, C, NM2 * NM2))
    zd2 = dram("zd2", (B, 2 * NM2, NM2, 2, C))
    ft = dram("ft", (B, NPTS, H))
    cx = [dram(f"cx{b}", (NCTX, H)) for b in range(B)]
    mn, mb, gen = (dram(n, (B, NMASK, H)) for n in ("mn", "mb", "gen"))
    mx = dram("mx", (B, NMASK))

    forward_modes(nc, "f0", B, x, ins["f32a"], ins["f32b"], ins["pair"], modes0, NM0, 1.0 / np.sqrt(PIX), False)
    mix_modes0(nc, B, modes0, ins["L0_conv_fw1"], ins["L0_conv_fw2"], ins["L0_conv_W"], ins["eye64"], zd0)
    inverse_modes(nc, "i0", B, zd0, ins["ky0"], ins["kx0"], x, None, x1l, x1g, stats1,
                  ins["L0_conv_b"], float(PIX * np.sqrt(W * NF)))
    local_attention(nc, B, x1l, stats1, ins["w_qkv_t"], ins["L1_conv_b_qkv"], ins["L1_conv_pos_emb"],
                    ins["masks"], ins["eye"], ol)
    global_mixer(nc, B, x1g, stats1, ins["L1_conv_amp_w"], ins["L1_conv_amp_b"], ins["L1_conv_pha_w"],
                 ins["L1_conv_pha_b"], (ins["fh"], ins["fw"], ins["ec"], ins["ew"]), og)
    project(nc, B, ol, og, x1l, x1g, ins["proj_w_t"], ins["L1_conv_proj_b"], ins["eye"], x2)
    forward_modes(nc, "f2", B, x2, ins["f16a"], ins["f16b"], ins["pair"], modes2, NM2, 1.0, True)
    mix_modes2(nc, B, modes2, ins["L2_conv_weights_real"], ins["L2_conv_weights_imag"], zd2)
    inverse_modes(nc, "i2", B, zd2, ins["ky2"], ins["kx2"], x2, x3, None, None, stats3, None, None)
    point_rows(nc, B, x3, stats3, ins["eye"], ft)
    select_points(nc, B, ft, ins["L3_conv_mask_point_idx"], ins["L3_conv_nonmask_point_idx"], ins["eye"], cx, mn, mb, mx)
    coherent_scan(nc, B, x3, stats3, mn, mb, mx, gen, out)
    finish_points(nc, B, x3, ft, gen, ins["L3_conv_mask_point_idx"], ins["eye"], out)


def constants():
    def cos_sin(a, b):
        t = 2 * np.pi / H * (np.outer(a, b) % H)
        return np.cos(t), np.sin(t)

    n = np.arange(H)
    con = {}
    for nm in (NM0, NM2):
        c, s = cos_sin(n, np.arange(nm))
        con[f"f{nm}a"] = np.concatenate([c, -s], 1)
        con[f"f{nm}b"] = np.concatenate([s, c], 1)
    c, s = cos_sin(np.arange(NM0), n)
    twice = np.where(np.arange(NM0) == 0, 1.0, 2.0)[:, None]
    con["ky0"] = np.concatenate([twice * c, twice * s])
    c, s = cos_sin(np.concatenate([np.arange(NM0), H - NM0 + np.arange(NM0)]), n)
    con["kx0"] = np.stack([c, -s], 1).reshape(4 * NM0, H) / (PIX * np.sqrt(W * NF))
    c, s = cos_sin(np.arange(NM2), n)
    con["ky2"] = np.concatenate([c, s])
    con["kx2"] = np.stack([c, -s], 1).reshape(2 * NM2, H) * (0.5 / PIX)
    windows = np.arange(NWIN)
    order = (windows * WIN + np.arange(WIN)[:, None]).ravel()
    order2 = (np.concatenate([windows[::2], windows[1::2]]) * WIN + np.arange(WIN)[:, None]).ravel()
    c, s = cos_sin(n, np.arange(NF))
    con["fh"] = np.concatenate([c, -s], 1)
    c, s = c[order], s[order]
    con["fw"] = np.stack([np.concatenate(v, 1) for v in ((c, -s), (s, c), (-s, -c))])
    pos, neg = cos_sin(np.arange(P), n), cos_sin(H - 1 - np.arange(P), n)
    con["ec"] = np.stack([np.stack([pos[0], neg[0]]), np.stack([pos[1], neg[1]]), -np.stack([pos[1], neg[1]])])
    c, s = cos_sin(np.arange(NF), order2)
    c[1:-1] *= 2
    s[1:-1] *= 2
    con["ew"] = np.stack([c[:-1], np.concatenate([-s[1:-1], c[-1:]])]) / PIX
    con["eye"], con["eye64"] = np.eye(P), np.eye(C)
    con["pair"] = np.kron(np.eye(C // 2), np.ones((2, 2)))
    p = np.arange(P)
    con["masks"] = np.concatenate([(p // HALF % 2)[:, None] == np.arange(2), (p % HALF // HC)[:, None] == np.arange(HEADS)], 1)
    return {k: np.ascontiguousarray(v, np.float32) for k, v in con.items()}


def kernel(**inputs):
    import concourse.bacc as bacc
    from concourse.bass_utils import run_bass_kernel_spmd

    arrays = {k: np.asarray(v) for k, v in inputs.items() if k != "L3_conv_mask"}
    arrays["w_qkv_t"] = np.ascontiguousarray(arrays.pop("L1_conv_w_qkv").T)
    arrays["proj_w_t"] = np.ascontiguousarray(arrays.pop("L1_conv_proj_w").T)
    arrays.update(constants())
    nc = bacc.Bacc("TRN2", target_bir_lowering=False, num_devices=1)
    ins = {k: nc.dram_tensor(f"in_{k}", a.shape, mybir.dt.from_np(a.dtype), kind="ExternalInput").ap()
           for k, a in arrays.items()}
    out = nc.dram_tensor("out", arrays["x"].shape, F32, kind="ExternalOutput").ap()
    build(nc, ins, out)
    r = run_bass_kernel_spmd(nc, [{f"in_{k}": a for k, a in arrays.items()}], core_ids=[0])
    return r.results[0]["out"]
```
